# Optimizing a Trainium2 kernel written in Bass

```python
import numpy as np
import jax
import jax.numpy as jnp

def _softmax(x, axis=-1):
    return jax.nn.softmax(x, axis=axis)
def _gelu(x):
    return jax.nn.gelu(x, approximate=True)
def _silu(x):
    return jax.nn.silu(x)
def _sigmoid(x):
    return jax.nn.sigmoid(x)
def _layernorm(x, axis=-1, eps=1e-5):
    m = jnp.mean(x, axis=axis, keepdims=True)
    v = jnp.var(x, axis=axis, keepdims=True)
    return (x - m) / jnp.sqrt(v + eps)
def _scatter_add(tgt, idx, src, axis=0):
    return tgt.at[idx].add(src)
def _segment_sum(src, seg, n):
    return jax.ops.segment_sum(src, seg, n)

kernel_name = 'mk_conv_attn_hybrid_d2_conv_nchw128_8ac8be'

def setup_inputs(seed: int = 0):
    np.random.seed(seed)
    _w = jnp.asarray
    def _rec_inputs():
        import jax
        import jax.numpy as jnp
        _gk = jax.random.key(seed)
        x = 0.0004705 + 0.9998 * jax.random.normal(jax.random.fold_in(_gk, 1), (4, 128, 64, 64), jnp.float32)
        return x
    x = _rec_inputs()
    def _L0_conv_setup():
        import jax, jax.numpy as jnp
        import numpy as np
        KSIZE = 3
        STRIDE = 1
        DIL = 2
        SCALE = 10.0
        EPS = 0.0001

        def same_pad(x, k, s, d):
            H, W = (x.shape[2], x.shape[3])
            eff = (k - 1) * d + 1
            out_h = -(-H // s)
            out_w = -(-W // s)
            ph = max((out_h - 1) * s + eff - H, 0)
            pw = max((out_w - 1) * s + eff - W, 0)
            return jnp.pad(x, ((0, 0), (0, 0), (ph // 2, ph - ph // 2), (pw // 2, pw - pw // 2)))

        def extract_patches(x, k, s, d):
            B, C, H, W = x.shape
            xp = same_pad(x, k, s, d)
            out_h = -(-H // s)
            out_w = -(-W // s)
            r = (jnp.arange(out_h) * s)[:, None] + jnp.arange(k)[None, :] * d
            c = (jnp.arange(out_w) * s)[:, None] + jnp.arange(k)[None, :] * d
            p = xp[:, :, r[:, None, :, None], c[None, :, None, :]]
            return p.transpose(0, 2, 3, 1, 4, 5).reshape(B, out_h * out_w, C, k, k)

        def forward(X, mask):
            B, C, H, W = X.shape
            kd = 2 * DIL
            deconv_W = extract_patches(X, kd, STRIDE * DIL, 1)
            Xd = X[:, :, ::DIL, ::DIL]
            h, w = (Xd.shape[2], Xd.shape[3])
            L = h * w
            conv_W = extract_patches(Xd, KSIZE, STRIDE, 1)
            md = mask[:, :, ::4 * DIL, ::4 * DIL]
            m0 = extract_patches(md, KSIZE, STRIDE, 1)[0]
            mm = (jnp.mean(m0, axis=(1, 2, 3)) == 0).astype(X.dtype)[None, :, None, None]
            norms = jnp.sqrt(jnp.sum(conv_W * conv_W, axis=(2, 3, 4), keepdims=True))
            Wn = conv_W / jnp.maximum(norms, EPS)
            Xp = extract_patches(Xd, KSIZE, 1, 1)
            scores = jnp.einsum('bpcuv,blcuv->blp', Xp, Wn).reshape(B, L, h, w)
            yi = scores * mm
            yi = jax.nn.softmax(yi * SCALE, axis=1) * mm
            T = jnp.einsum('blij,blcuv->bcijuv', yi, deconv_W)
            ch = (h - 1) * DIL + kd
            cw = (w - 1) * DIL + kd
            canvas = jnp.zeros((B, C, ch, cw), X.dtype)
            r = (DIL * jnp.arange(h))[:, None] + jnp.arange(kd)[None, :]
            c = (DIL * jnp.arange(w))[:, None] + jnp.arange(kd)[None, :]
            canvas = canvas.at[:, :, r[:, None, :, None], c[None, :, None, :]].add(T)
            return canvas[:, :, 1:1 + H, 1:1 + W] / 4.0
        key = jax.random.key(seed)
        X = jax.random.normal(key, (4, 128, 64, 64), jnp.float32)
        mask = jnp.zeros((4, 1, 256, 256), jnp.float32)
        mask = mask.at[:, :, 96:160, 96:160].set(1.0)
        return {'X': X, 'mask': mask}
    _L0_conv_all = _L0_conv_setup()
    _L0_conv_in = {k: v for k, v in _L0_conv_all.items() if k in ('mask', )}
    del _L0_conv_all

    def _L1_attn_setup():
        import jax, jax.numpy as jnp
        import numpy as np
        E = 128
        H = 4
        D = E // H
        key = jax.random.key(seed)
        ks = jax.random.split(key, 5)
        b, n = (4, 4096)
        x = jax.random.normal(ks[0], (b, n, E), dtype=jnp.float32)
        W_qkv = jax.random.normal(ks[1], (E, 3 * E), dtype=jnp.float32) * (1.0 / np.sqrt(E))
        b_qkv = jax.random.normal(ks[2], (3 * E,), dtype=jnp.float32) * 0.01
        W_proj = jax.random.normal(ks[3], (E, E), dtype=jnp.float32) * (1.0 / np.sqrt(E))
        b_proj = jax.random.normal(ks[4], (E,), dtype=jnp.float32) * 0.01
        return {'x': x, 'W_qkv': W_qkv, 'b_qkv': b_qkv, 'W_proj': W_proj, 'b_proj': b_proj}
    _L1_attn_all = _L1_attn_setup()
    _L1_attn_in = {k: v for k, v in _L1_attn_all.items() if k in ('W_qkv', 'b_qkv', 'W_proj', 'b_proj', )}
    del _L1_attn_all

    def _L1_ffn_setup():
        import jax, jax.numpy as jnp
        import numpy as np
        B, S, D, E, H, O, K = (512, 2048, 128, 64, 512, 128, 8)
        key = jax.random.key(seed)
        k0, k1, k2, k3 = jax.random.split(key, 4)
        x = jax.random.normal(k0, (B, S, D), dtype=jnp.float32)
        gate_w = jax.random.normal(k1, (E, D), dtype=jnp.float32) * (1.0 / np.sqrt(D))
        gate_b = jnp.zeros((E,), dtype=jnp.float32)
        weight1 = jax.random.uniform(k2, (E, D + 1, H), dtype=jnp.float32, minval=-1.0, maxval=1.0) * (1.0 / np.sqrt(D + 1))
        weight2 = jax.random.uniform(k3, (E, H + 1, O), dtype=jnp.float32, minval=-1.0, maxval=1.0) * (1.0 / np.sqrt(H + 1))
        return {'x': x, 'gate_w': gate_w, 'gate_b': gate_b, 'weight1': weight1, 'weight2': weight2}
    _L1_ffn_all = _L1_ffn_setup()
    _L1_ffn_in = {k: v for k, v in _L1_ffn_all.items() if k in ('gate_w', 'gate_b', 'weight1', 'weight2', )}
    del _L1_ffn_all

    return {
        "x": x,
        "L0_conv_mask": _L0_conv_in["mask"],
        "L1_attn_W_qkv": _L1_attn_in["W_qkv"],
        "L1_attn_b_qkv": _L1_attn_in["b_qkv"],
        "L1_attn_W_proj": _L1_attn_in["W_proj"],
        "L1_attn_b_proj": _L1_attn_in["b_proj"],
        "L1_ffn_gate_w": _L1_ffn_in["gate_w"],
        "L1_ffn_gate_b": _L1_ffn_in["gate_b"],
        "L1_ffn_weight1": _L1_ffn_in["weight1"],
        "L1_ffn_weight2": _L1_ffn_in["weight2"],
    }

def reference(x, L0_conv_mask, L1_attn_W_qkv, L1_attn_b_qkv, L1_attn_W_proj, L1_attn_b_proj, L1_ffn_gate_w, L1_ffn_gate_b, L1_ffn_weight1, L1_ffn_weight2):
    import jax
    import jax.numpy as jnp
    def _L0_conv_ref(X, mask):
        import jax, jax.numpy as jnp
        import numpy as np
        KSIZE = 3
        STRIDE = 1
        DIL = 2
        SCALE = 10.0
        EPS = 0.0001

        def same_pad(x, k, s, d):
            H, W = (x.shape[2], x.shape[3])
            eff = (k - 1) * d + 1
            out_h = -(-H // s)
            out_w = -(-W // s)
            ph = max((out_h - 1) * s + eff - H, 0)
            pw = max((out_w - 1) * s + eff - W, 0)
            return jnp.pad(x, ((0, 0), (0, 0), (ph // 2, ph - ph // 2), (pw // 2, pw - pw // 2)))

        def extract_patches(x, k, s, d):
            B, C, H, W = x.shape
            xp = same_pad(x, k, s, d)
            out_h = -(-H // s)
            out_w = -(-W // s)
            r = (jnp.arange(out_h) * s)[:, None] + jnp.arange(k)[None, :] * d
            c = (jnp.arange(out_w) * s)[:, None] + jnp.arange(k)[None, :] * d
            p = xp[:, :, r[:, None, :, None], c[None, :, None, :]]
            return p.transpose(0, 2, 3, 1, 4, 5).reshape(B, out_h * out_w, C, k, k)

        def forward(X, mask):
            B, C, H, W = X.shape
            kd = 2 * DIL
            deconv_W = extract_patches(X, kd, STRIDE * DIL, 1)
            Xd = X[:, :, ::DIL, ::DIL]
            h, w = (Xd.shape[2], Xd.shape[3])
            L = h * w
            conv_W = extract_patches(Xd, KSIZE, STRIDE, 1)
            md = mask[:, :, ::4 * DIL, ::4 * DIL]
            m0 = extract_patches(md, KSIZE, STRIDE, 1)[0]
            mm = (jnp.mean(m0, axis=(1, 2, 3)) == 0).astype(X.dtype)[None, :, None, None]
            norms = jnp.sqrt(jnp.sum(conv_W * conv_W, axis=(2, 3, 4), keepdims=True))
            Wn = conv_W / jnp.maximum(norms, EPS)
            Xp = extract_patches(Xd, KSIZE, 1, 1)
            scores = jnp.einsum('bpcuv,blcuv->blp', Xp, Wn).reshape(B, L, h, w)
            yi = scores * mm
            yi = jax.nn.softmax(yi * SCALE, axis=1) * mm
            T = jnp.einsum('blij,blcuv->bcijuv', yi, deconv_W)
            ch = (h - 1) * DIL + kd
            cw = (w - 1) * DIL + kd
            canvas = jnp.zeros((B, C, ch, cw), X.dtype)
            r = (DIL * jnp.arange(h))[:, None] + jnp.arange(kd)[None, :]
            c = (DIL * jnp.arange(w))[:, None] + jnp.arange(kd)[None, :]
            canvas = canvas.at[:, :, r[:, None, :, None], c[None, :, None, :]].add(T)
            return canvas[:, :, 1:1 + H, 1:1 + W] / 4.0
        return forward(X, mask)

    def _L1_attn_ref(x, W_qkv, b_qkv, W_proj, b_proj):
        import jax, jax.numpy as jnp
        import numpy as np
        E = 128
        H = 4
        D = E // H
        b, n, e = x.shape
        qkv = (x @ W_qkv + b_qkv).reshape(b, n, H, D, 3)
        qkv = jnp.transpose(qkv, (4, 0, 2, 1, 3))
        q, k, v = (qkv[0], qkv[1], qkv[2])
        scale = 1.0 / np.float32(np.sqrt(e))
        scores = jnp.einsum('bhnd,bhmd->bhnm', q, k) * scale
        att = jax.nn.softmax(scores, axis=-1)
        out = jnp.einsum('bhnm,bhmd->bhnd', att, v)
        out = jnp.transpose(out, (0, 2, 1, 3)).reshape(b, n, e)
        return out @ W_proj + b_proj

    def _L1_ffn_ref(x, gate_w, gate_b, weight1, weight2):
        import jax, jax.numpy as jnp
        import numpy as np
        B, S, D, E, H, O, K = (512, 2048, 128, 64, 512, 128, 8)
        Bn, Sn, Dn = x.shape
        logits = jnp.einsum('bsd,ed->bse', x, gate_w) + gate_b
        probs = jax.nn.softmax(logits, axis=1)
        vals, idx = jax.lax.top_k(probs.transpose(0, 2, 1), K)
        topv = vals.transpose(0, 2, 1)
        topi = idx.transpose(0, 2, 1)
        flat_idx = topi.reshape(Bn, K * E)
        gathered = jnp.take_along_axis(x, flat_idx[:, :, None], axis=1)
        gathered = gathered.reshape(Bn, K, E, Dn)
        pooled = jnp.einsum('bked,bke->bed', gathered, topv)
        ones = jnp.ones((E, Bn, 1), dtype=x.dtype)
        h = jnp.concatenate([pooled.transpose(1, 0, 2), ones], axis=-1)
        h = jax.nn.gelu(jnp.einsum('ebd,edh->ebh', h, weight1), approximate=False)
        h = jnp.concatenate([h, ones], axis=-1)
        out = jnp.einsum('ebh,eho->ebo', h, weight2)
        out = out.transpose(1, 0, 2)
        weighted = jnp.einsum('beo,bke->bkeo', out, topv).reshape(Bn, K * E, O)
        outputs = jnp.zeros((Bn, Sn, O), dtype=x.dtype)
        outputs = outputs.at[jnp.arange(Bn)[:, None], flat_idx].add(weighted)
        return outputs

    def _gn(v, G=32, eps=1e-5):
        B_, C_, H_, W_ = v.shape
        g = v.reshape(B_, G, C_ // G, H_, W_)
        m = jnp.mean(g, axis=(2, 3, 4), keepdims=True)
        s = jnp.var(g, axis=(2, 3, 4), keepdims=True)
        return ((g - m) / jnp.sqrt(s + eps)).reshape(v.shape)

    def _ln_c(v, eps=1e-6):
        m = jnp.mean(v, axis=1, keepdims=True)
        s = jnp.var(v, axis=1, keepdims=True)
        return (v - m) / jnp.sqrt(s + eps)

    def _ln_t(v, eps=1e-5):
        m = jnp.mean(v, axis=-1, keepdims=True)
        s = jnp.var(v, axis=-1, keepdims=True)
        return (v - m) / jnp.sqrt(s + eps)

    def _to_tokens(v):
        B_, C_, H_, W_ = v.shape
        return v.reshape(B_, C_, H_ * W_).transpose(0, 2, 1)
    def _from_tokens(t, like):
        B_, C_, H_, W_ = like.shape
        return t.transpose(0, 2, 1).reshape(B_, C_, H_, W_)

    x = x + _L0_conv_ref(_gn(x), L0_conv_mask)
    t = _to_tokens(x)
    t = t + _L1_attn_ref(_ln_t(t), L1_attn_W_qkv, L1_attn_b_qkv, L1_attn_W_proj, L1_attn_b_proj)
    t = t + _L1_ffn_ref(_ln_t(t), L1_ffn_gate_w, L1_ffn_gate_b, L1_ffn_weight1, L1_ffn_weight2)
    x = _from_tokens(t, x)
    return x


_drawn_inputs = setup_inputs


def setup_inputs(seed=0):
    import zlib

    import numpy as np

    out = dict(_drawn_inputs(seed))
    spreads = {'L1_ffn_gate_b': (0.0, 0.1)}
    factors = {'L1_attn_b_qkv': 8.0,
     'L1_attn_b_proj': 8.0,
     'L1_ffn_gate_w': 8.0,
     'L1_ffn_weight1': 8.0,
     'L1_ffn_weight2': 8.0}
    for name, (base, spread) in spreads.items():
        noise = np.random.default_rng([zlib.crc32(name.encode()), seed]).standard_normal(out[name].shape)
        drawn = base * np.exp(spread * noise) if base else spread * noise
        out[name] = jnp.asarray(drawn.astype(out[name].dtype))
    for name, factor in factors.items():
        out[name] = (out[name] * factor).astype(out[name].dtype)
    return out
```

```python
import concourse.bass as bass
from concourse import mybir
from contextlib import ExitStack

f32 = mybir.dt.float32
f32r = mybir.dt.float32r
ALU = mybir.AluOpType
ACT = mybir.ActivationFunctionType
AX = mybir.AxisListType

P = 128
NIMG = 4
IMG = 64
TOK = IMG * IMG
NT = TOK // P
BANK = 512
NC = TOK // BANK
H = 4
D = 32
G = 4
LOW = 32
LOC = LOW * LOW
PAD = LOW + 2
LT = LOC // P
ROWS = P // LOW
E = 64
HID = 512
HC = HID // P
GN_EPS, LN_EPS, PATCH_EPS = 1e-5, 1e-5, 1e-4
SCALE0 = 10.0
SCALE1 = float(P) ** -0.5
MOVES = 3 * H
PBUFS = 3
PAIR = 2 * BANK
POOL_TILES = (0, 1, 5, 8, 11, 14, 17, 20, 23, 26)
DVE_TILES = tuple(t for t in range(NT) if t not in POOL_TILES)
LOGIT_BOUND = 64.0
EG = 4
NEG = E // EG
WBUFS = 4


def slot_of(u):
    return 1 if u == 2 * NT - 1 else u % 3


def split_rows(ap):
    return ap.rearrange("p (q t) c -> p q t c", t=LT)


def tile_order(ap):
    return ap.rearrange("p (t q c) -> p q t c", q=ROWS, c=LOW)


def build(nc, x, mask, w_qkv, b_qkv, w_proj, b_proj, gate_w, gate_b, w1, w2, out):
    ctx = ExitStack()
    sems = {}

    def sem(name):
        if name not in sems:
            sems[name] = ctx.enter_context(nc.semaphore(name))
        return sems[name]

    def clear_all():
        nums = [s.num for s in sems.values()]
        nc.all_engine_barrier(sems_to_clear=range(min(nums), max(nums) + 1))

    with ctx:
        def sb(name, shape, dt=f32):
            return ctx.enter_context(nc.sbuf_tensor(name, shape, dt))

        for n in ("load", "consts", "chain_pool", "chain_dve", "chain_act", "tr", "ready_a", "ready_b", "ready_c",
                  "ready_d", "ready_e", "ready_f", "ready_g", "ready_h", "store", "mm_a", "mm_b", "mm_c", "mm_d",
                  "free_a", "free_b", "free_c", "free_d", "exp_done", "scores_done", "pv_done", "sum_dve", "sum_pool",
                  "move", "move_even", "move_odd", "misc_pe", "misc_free", "ln_tr", "ln_raw", "ln_var", "ln_log", "ln_exp", "ln_norm",
                  "ln_back", "ln_out"):
            sem(n)

        t_d = nc.dram_tensor("t_scratch", [NIMG, P, TOK], f32, kind="Internal").ap()
        sel_d = nc.dram_tensor("sel_scratch", [NIMG, E, TOK], f32, kind="Internal").ap()

        ps = ctx.enter_context(nc.psum_tensor("ps", [P, 8, BANK], f32))
        ident = sb("ident", [P, P])
        ones = sb("ones", [P, P])
        gmat = sb("gmat", [P, P])
        wq = sb("wq", [P, P])
        wk = sb("wk", [P, P])
        wv = sb("wv", [P, P])
        wp = sb("wp", [P, P])
        wgT = sb("wgT", [P, E])
        bq = sb("bq", [P, 1])
        bk = sb("bk", [P, 1])
        bp = sb("bp", [P, 1])
        bg = sb("bg", [E, 1])
        bv = sb("bv", [P, P])
        mm = sb("mm", [P, LOC])
        left = sb("left", [P, 1])
        right = sb("right", [P, 1])
        poolT = sb("poolT", [P, E, NIMG])
        bounded = sb("bounded", [1, 1], mybir.dt.int32)
        X = sb("X", [P, TOK])

        def newton_rsqrt(dve, chain, y, w, t):
            chain(nc.vector.tensor_tensor(t, y, y, ALU.mult))
            chain(nc.vector.tensor_tensor(t, t, w, ALU.mult))
            chain(nc.vector.tensor_scalar(t, t, -0.5, 1.5, ALU.mult, ALU.add))
            chain(nc.vector.tensor_tensor(y, y, t, ALU.mult))

        def chain_of(eng, s):
            n = [0]

            def chain(ins):
                n[0] += 1
                ins.then_inc(s, 1)
                eng.wait_ge(s, n[0])
            return chain

        with ExitStack() as tmp:
            wqkv = tmp.enter_context(nc.sbuf_tensor("wqkv", [P, 3 * P], f32))
            bqkv = tmp.enter_context(nc.sbuf_tensor("bqkv", [P, 3 * P], f32))
            gw = tmp.enter_context(nc.sbuf_tensor("gw", [E, P], f32))
            mrow = tmp.enter_context(nc.sbuf_tensor("mrow", [1, LOW, 256], f32))
            mpad = tmp.enter_context(nc.sbuf_tensor("mpad", [P, PAD, PAD], f32))
            mbox = tmp.enter_context(nc.sbuf_tensor("mbox", [P, PAD, LOW], f32))
            with nc.Block() as block:
                @block.sync
                def _(sp):
                    sp.dma_start(wqkv[:], w_qkv).then_inc(sem("load"), 16)
                    sp.dma_start(bqkv[:], b_qkv.rearrange("(a n) -> a n", a=1).broadcast_to([P, 3 * P])).then_inc(sem("load"), 16)
                    sp.dma_start(gw[:], gate_w).then_inc(sem("load"), 16)
                    sp.dma_start(wp[:], w_proj).then_inc(sem("load"), 16)
                    b3 = b_qkv.rearrange("(p k) -> p k", k=3)
                    with nc.allow_non_contiguous_dma("128 bias values, once"):
                        sp.dma_start(bq[:], b3[:, 0:1]).then_inc(sem("load"), 16)
                        sp.dma_start(bk[:], b3[:, 1:2]).then_inc(sem("load"), 16)
                        sp.dma_start(bp[:], b_proj.rearrange("(p k) -> p k", k=1)).then_inc(sem("load"), 16)
                        sp.dma_start(bg[:], gate_b.rearrange("(p k) -> p k", k=1)).then_inc(sem("load"), 16)
                    sp.dma_start(mrow[:], mask[0:1, 0, :, :].rearrange("a (r s) c -> a r s c", s=8)[:, :, 0, :]).then_inc(sem("load"), 16)

                @block.gpsimd
                def _(pool):
                    chain = chain_of(pool, sem("chain_pool"))
                    chain(nc.gpsimd.memset(ident[:], 0.0))
                    chain(nc.gpsimd.affine_select(out=ident[:], in_=ident[:], compare_op=ALU.not_equal, fill=1.0,
                                                  base=0, pattern=[[-1, P]], channel_multiplier=1))
                    nc.gpsimd.memset(ones[:], 1.0).then_inc(sem("consts"), 1)
                    chain(nc.gpsimd.memset(gmat[:], 1.0 / G))
                    g3 = gmat[:].rearrange("p (g r) -> p g r", r=G)
                    chain(nc.gpsimd.affine_select(out=g3, in_=g3, compare_op=ALU.is_ge, fill=0.0, base=0,
                                                  pattern=[[-G, P // G], [0, G]], channel_multiplier=1))
                    chain(nc.gpsimd.affine_select(out=g3, in_=g3, compare_op=ALU.is_ge, fill=0.0, base=G - 1,
                                                  pattern=[[G, P // G], [0, G]], channel_multiplier=-1))
                    chain(nc.gpsimd.memset(left[:], 1.0))
                    for q in range(ROWS):
                        chain(nc.gpsimd.memset(left[q * LOW:q * LOW + 1, :], 0.0))
                    nc.gpsimd.memset(mpad[:], 0.0).then_inc(sem("consts"), 1)

                @block.tensor
                def _(pe):
                    pe.wait_ge(sem("load"), 9 * 16)
                    pe.wait_ge(sem("consts"), 2)
                    pe.wait_ge(sem("chain_pool"), 6 + ROWS)
                    nc.tensor.transpose(ps[:, 0, 0:E], gw[:], ident[0:E, 0:E]).then_inc(sem("tr"), 1)
                    picked = mrow[:].rearrange("a r (c s) -> a r c s", s=8)[:, :, :, 0]
                    for n in range(2):
                        nc.tensor.matmul(ps[:, 1 + n, :], ones[0:1, :], picked[:, 16 * n:16 * n + 16, :],
                                         start=True, stop=True).then_inc(sem("tr"), 1)

                @block.vector
                def _(dve):
                    chain = chain_of(dve, sem("chain_dve"))
                    dve.wait_ge(sem("load"), 9 * 16)
                    w3 = wqkv[:].rearrange("p (n k) -> p n k", k=3)
                    for k, w in enumerate((wq, wk, wv)):
                        nc.vector.tensor_copy(w[:], w3[:, :, k]).then_inc(sem("ready_a"), 1)
                    nc.vector.tensor_copy(bv[:], bqkv[:].rearrange("p (n k) -> p n k", k=3)[:, :, 2]).then_inc(sem("ready_a"), 1)
                    dve.wait_ge(sem("chain_pool"), 6 + ROWS)
                    nc.vector.stream_shuffle(right[:], left[:], [(j + 1) % LOW for j in range(LOW)]).then_inc(sem("ready_a"), 1)
                    dve.wait_ge(sem("tr"), 3)
                    dve.wait_ge(sem("consts"), 2)
                    nc.vector.tensor_copy(wgT[:], ps[:, 0, 0:E]).then_inc(sem("ready_a"), 1)
                    chain(nc.vector.tensor_copy(mpad[:, 1:1 + LOW, 1:1 + LOW], ps[:, 1:3, :].rearrange("p n (r c) -> p (n r) c", c=LOW)))
                    chain(nc.vector.tensor_tensor(mbox[:], mpad[:, :, 0:LOW], mpad[:, :, 1:1 + LOW], ALU.add))
                    chain(nc.vector.tensor_tensor(mbox[:], mbox[:], mpad[:, :, 2:2 + LOW], ALU.add))
                    by_tile = tile_order(mm[:])
                    chain(nc.vector.tensor_tensor(by_tile, split_rows(mbox[:, 0:LOW, :]), split_rows(mbox[:, 1:1 + LOW, :]), ALU.add))
                    chain(nc.vector.tensor_tensor(by_tile, by_tile, split_rows(mbox[:, 2:2 + LOW, :]), ALU.add))
                    chain(nc.vector.tensor_scalar(mm[:], mm[:], 0.0, None, ALU.is_equal))
        clear_all()
        bound_logits(nc, sem, chain_of, ps, ones, wq, wk, bq, bk, bounded)
        clear_all()

        def ln_tensor(pe):
            for g in range(NC):
                if g >= 4:
                    pe.wait_ge(sem("ln_raw"), g - 3)
                for r in range(4):
                    j = 4 * g + r
                    last = nc.tensor.transpose(ps[:, g % 4, r * P:(r + 1) * P], X[:, j * P:(j + 1) * P], ident[:])
                last.then_inc(sem("ln_tr"), 1)
            return

        def ln_tensor_back(pe, tok):
            for g in range(NC):
                pe.wait_ge(sem("ln_norm"), g + 1)
                if g >= 4:
                    pe.wait_ge(sem("ln_out"), g - 3)
                for r in range(4):
                    last = nc.tensor.transpose(ps[:, 4 + g % 4, r * P:(r + 1) * P], tok[:, 4 * g + r, :], ident[:])
                last.then_inc(sem("ln_back"), 1)

        def ln_scalar(act, tok, wv_, yv_, xnT):
            for g in range(NC):
                act.wait_ge(sem("ln_tr"), g + 1)
                nc.scalar.activation(tok[:, 4 * g:4 * g + 4, :], ps[:, g % 4, :].rearrange("p (r n) -> p r n", n=P),
                                     ACT.Copy).then_inc(sem("ln_raw"), 1)
            act.wait_ge(sem("ln_var"), 1)
            nc.scalar.activation(yv_, wv_, ACT.Ln).then_inc(sem("ln_log"), 1)
            act.wait_ge(sem("ln_log"), 1)
            nc.scalar.activation(yv_, yv_, ACT.Exp, scale=-0.5).then_inc(sem("ln_exp"), 1)
            for g in range(NC):
                act.wait_ge(sem("ln_back"), g + 1)
                nc.scalar.activation(xnT[:, g * BANK:(g + 1) * BANK], ps[:, 4 + g % 4, :], ACT.Copy).then_inc(sem("ln_out"), 1)

        def ln_vector(dve, chain, tok, st, mv, w, y, t):
            for g in range(NC):
                dve.wait_ge(sem("ln_raw"), g + 1)
                for r in range(4):
                    last = nc.vector.bn_stats(st[:, 4 * g + r, :], tok[:, 4 * g + r, :])
            chain(last)
            for j in range(NT):
                last = nc.vector.bn_aggr(mv[:, j, :], st[:, j, :])
            chain(last)
            chain(nc.vector.tensor_scalar(w[:], mv[:, :, 1], LN_EPS, None, ALU.add))
            nc.vector.tensor_copy(t[:], w[:]).then_inc(sem("ln_var"), 1)
            dve.wait_ge(sem("ln_exp"), 1)
            newton_rsqrt(dve, chain, y[:], w[:], t[:])
            for g in range(NC):
                for r in range(4):
                    j = 4 * g + r
                    last = nc.vector.tensor_scalar(tok[:, j, :], tok[:, j, :], mv[:, j, 0:1], y[:, j:j + 1],
                                                   ALU.subtract, ALU.mult)
                last.then_inc(sem("ln_norm"), 1)

        with nc.Fori(0, NIMG) as b:
            contextual_attention(nc, sem, chain_of, newton_rsqrt, b, x, X, ps, ident, ones, gmat, mm, left, right)
            clear_all()
            with ExitStack() as big:
                def sbb(name, shape, dt=f32):
                    return big.enter_context(nc.sbuf_tensor(name, shape, dt))
                xnT = sbb("xnT", [P, TOK + BANK])
                KS = sbb("KS", [3 * D, H, TOK], f32r)
                V = sbb("V", [P, NT, P])
                with ExitStack() as tmp:
                    def sbt(name, shape, dt=f32):
                        return tmp.enter_context(nc.sbuf_tensor(name, shape, dt))
                    tok = sbt("tok", [P, NT, P])
                    st = sbt("st", [P, NT, 6])
                    mv = sbt("mv", [P, NT, 2])
                    w = sbt("w", [P, NT])
                    y = sbt("y", [P, NT])
                    t = sbt("t", [P, NT])
                    khi = sbt("khi", [P, 2, BANK], f32r)
                    klo = sbt("klo", [P, 2, BANK], f32r)
                    move = (sem("move_even"), sem("move_odd"))
                    with nc.Block() as block:
                        @block.gpsimd
                        def _(pool):
                            nc.gpsimd.memset(xnT[:, TOK:TOK + BANK], 0.0).then_inc(sem("consts"), 1)

                        @block.tensor
                        def _(pe):
                            ln_tensor(pe)
                            ln_tensor_back(pe, tok)
                            for g in range(NC):
                                pe.wait_ge(sem("ln_out"), g + 1)
                                if g >= 2:
                                    pe.wait_ge(sem("free_a"), g - 1)
                                    pe.wait_ge(sem("free_b"), g - 1)
                                nc.tensor.matmul(ps[:, g % 2, :], wk[:], xnT[:, g * BANK:(g + 1) * BANK],
                                                 start=True, stop=True).then_inc(sem("mm_a"), 1)
                                for r in range(4):
                                    j = 4 * g + r
                                    last = nc.tensor.matmul(ps[:, 2 + g % 2, r * P:(r + 1) * P], xnT[:, j * P:(j + 1) * P],
                                                            wv[:], start=True, stop=True)
                                last.then_inc(sem("mm_b"), 1)

                        @block.scalar
                        def _(act):
                            ln_scalar(act, tok, w[:], y[:], xnT)
                            for g in range(NC):
                                act.wait_ge(sem("mm_a"), g + 1)
                                if g >= 2:
                                    act.wait_ge(move[g % 2], 16 * MOVES * (g // 2))
                                nc.scalar.activation(khi[:, g % 2, :], ps[:, g % 2, :], ACT.Identity, bias=bk[:]).then_inc(sem("ready_a"), 1)

                        @block.vector
                        def _(dve):
                            chain = chain_of(dve, sem("chain_dve"))
                            ln_vector(dve, chain, tok, st, mv, w, y, t)
                            for g in range(NC):
                                dve.wait_ge(sem("ready_a"), g + 1)
                                if g >= 2:
                                    dve.wait_ge(move[g % 2], 16 * MOVES * (g // 2))
                                nc.vector.scalar_tensor_tensor(klo[:, g % 2, :], ps[:, g % 2, :], bk[:], khi[:, g % 2, :].bitcast(f32),
                                                               ALU.add, ALU.subtract).then_inc(sem("free_a"), 1)
                                dve.wait_ge(sem("mm_b"), g + 1)
                                nc.vector.tensor_tensor(V[:, 4 * g:4 * g + 4, :], ps[:, 2 + g % 2, :].rearrange("p (r n) -> p r n", n=P),
                                                        bv[:].rearrange("p (o n) -> p o n", o=1).broadcast_to([P, 4, P]),
                                                        ALU.add).then_inc(sem("free_b"), 1)

                        @block.sync
                        def _(sp):
                            for g in range(NC):
                                sp.wait_ge(sem("free_a"), g + 1)
                                move_parts(sp, move[g % 2], KS[:, :, g * BANK:(g + 1) * BANK], khi[:, g % 2, :], klo[:, g % 2, :], (0, 0, 1))
                            for m in move:
                                sp.wait_ge(m, 16 * MOVES * (NC // 2))
                clear_all()
                flag = nc.values_load(bounded[0:1, 0:1], min_val=0, max_val=P)
                with nc.If(flag >= P):
                    self_attention(nc, sem, X, ps, ones, wq, bq, wp, bp, xnT, KS, V)
                    clear_all()
                with nc.Else():
                    self_attention_with_maximum(nc, sem, clear_all, X, ps, ident, wq, bq, wk, bk, wp, bp, xnT, V)
                    clear_all()

            with ExitStack() as tmp:
                def sbt(name, shape, dt=f32):
                    return tmp.enter_context(nc.sbuf_tensor(name, shape, dt))
                tok = sbt("tok2", [P, NT, P])
                xnT = sbt("xnT2", [P, TOK])
                st = sbt("st2", [P, NT, 6])
                mv = sbt("mv2", [P, NT, 2])
                w = sbt("w2s", [P, NT])
                y = sbt("y2", [P, NT])
                t = sbt("t2", [P, NT])
                logit = sbt("logit", [E, TOK])
                prob = sbt("prob", [E, TOK])
                rest = sbt("rest", [E, TOK])
                top = sbt("top", [E, 8])
                nmax = sbt("nmax", [E, 1])
                zsum = sbt("zsum", [E, 1])
                rz = sbt("rzg", [E, 1])
                selT = sbt("selT", [P, NT, E])
                with nc.Block() as block:
                    @block.sync
                    def _(sp):
                        sp.dma_start(t_d[bass.ds(b, 1)].rearrange("a p n -> (a p) n"), X[:]).then_inc(sem("store"), 16)
                        sp.wait_ge(sem("ready_d"), 1)
                        sp.dma_start(sel_d[bass.ds(b, 1)].rearrange("a p n -> (a p) n"), rest[:]).then_inc(sem("store"), 16)
                        sp.wait_ge(sem("store"), 32)

                    @block.tensor
                    def _(pe):
                        ln_tensor(pe)
                        ln_tensor_back(pe, tok)
                        for g in range(NC):
                            pe.wait_ge(sem("ln_out"), NC if g >= 4 else g + 1)
                            nc.tensor.matmul(ps[0:E, g, :], wgT[:], xnT[:, g * BANK:(g + 1) * BANK],
                                             start=True, stop=True).then_inc(sem("mm_a"), 1)
                        pe.wait_ge(sem("ready_d"), 1)
                        for j in range(NT):
                            last = nc.tensor.transpose(ps[:, j // 8, (j % 8) * E:(j % 8 + 1) * E], rest[:, j * P:(j + 1) * P], ident[0:E, 0:E])
                            if j % 8 == 7:
                                last.then_inc(sem("mm_b"), 1)
                        for j in range(NT):
                            if j % 8 == 0:
                                pe.wait_ge(sem("ready_e"), j // 8 + 1)
                            last = nc.tensor.matmul(ps[:, 4, 0:E], tok[:, j, :], selT[:, j, :], start=(j == 0), stop=(j == NT - 1))
                        last.then_inc(sem("mm_c"), 1)

                    @block.scalar
                    def _(act):
                        ln_scalar(act, tok, w[:], y[:], xnT)
                        for g in range(NC):
                            act.wait_ge(sem("mm_a"), g + 1)
                            nc.scalar.activation(logit[:, g * BANK:(g + 1) * BANK], ps[0:E, g, :], ACT.Identity, bias=bg[:]).then_inc(sem("ready_a"), 1)
                        act.wait_ge(sem("ready_b"), 1)
                        nc.scalar.activation(prob[:], logit[:], ACT.Exp, bias=nmax[:], accum_out=zsum[:]).then_inc(sem("ready_c"), 1)
                        for k in range(4):
                            act.wait_ge(sem("mm_b"), k + 1)
                            nc.scalar.activation(selT[:, 8 * k:8 * k + 8, :], ps[:, k, :].rearrange("p (r n) -> p r n", n=E), ACT.Copy).then_inc(sem("ready_e"), 1)

                    @block.vector
                    def _(dve):
                        chain = chain_of(dve, sem("chain_dve"))
                        ln_vector(dve, chain, tok, st, mv, w, y, t)
                        dve.wait_ge(sem("ready_a"), NC)
                        chain(nc.vector.reduce_max(nmax[:], logit[:], AX.X))
                        nc.vector.tensor_scalar(nmax[:], nmax[:], -1.0, None, ALU.mult).then_inc(sem("ready_b"), 1)
                        dve.wait_ge(sem("ready_c"), 1)
                        chain(nc.vector.reciprocal(rz[:], zsum[:]))
                        chain(nc.vector.tensor_scalar(prob[:], prob[:], rz[:], None, ALU.mult))
                        chain(nc.vector.max(out=top[:], in_=prob[:]))
                        chain(nc.vector.match_replace(out=rest[:], in_to_replace=top[:], in_values=prob[:], imm_value=0.0))
                        nc.vector.tensor_tensor(rest[:], prob[:], rest[:], ALU.subtract).then_inc(sem("ready_d"), 1)
                        dve.wait_ge(sem("mm_c"), 1)
                        nc.vector.tensor_copy(poolT[:, :, bass.ds(b, 1)], ps[:, 4, 0:E].rearrange("p (e o) -> p e o", o=1)).then_inc(sem("ready_f"), 1)
            clear_all()

        experts(nc, sem, chain_of, ps, ident, poolT, t_d, sel_d, w1, w2, out)


def move_parts(sp, moved, stack, high, low, parts):
    for k, part in enumerate(parts):
        for h in range(H):
            src = (high, low)[part][h * D:(h + 1) * D, :].bitcast(f32)
            ins = sp.dma_start(stack[k * D:(k + 1) * D, h, :].bitcast(f32), src)
            ins.then_inc(moved, 16)


def contextual_attention(nc, sem, chain_of, newton_rsqrt, b, x, X, ps, ident, ones, gmat, mm, left, right):
    with ExitStack() as tmp:
        def sbt(name, shape, dt=f32):
            return tmp.enter_context(nc.sbuf_tensor(name, shape, dt))
        xg = sbt("xg", [P, IMG + 1, IMG])
        low_hi = sbt("low_hi", [P, PAD, PAD], f32r)
        low_lo = sbt("low_lo", [P, PAD, PAD], f32r)
        sq = sbt("sq", [P, PAD, PAD])
        gst = sbt("gst", [P, NC, 6])
        gmv = sbt("gmv", [P, 2])
        ge2 = sbt("ge2", [P, 2])
        gsm = sbt("gsm", [P, 4])
        wgt = sbt("wgt", [P, LOC])
        e = [sbt(f"e{i}", [P, LOC]) for i in range(2)]
        nmx = sbt("nmx", [P, LT])
        zs = sbt("zs", [P, LT])
        rz = sbt("rz0", [P, LT])
        diag = [sbt(f"diag{i}", [P, P]) for i in range(2)]
        stage = [sbt(f"stage{i}", [P, LT, ROWS, PAD]) for i in range(2)]
        shuf = [sbt(f"shuf{i}", [P, PAD * PAD]) for i in range(2)]
        C = [sbt(f"C{i}", [P, LT, PAD, LOW]) for i in range(2)]
        shifted = [[sbt(f"shifted{k}{v}", [P, PAD, LOW], f32r) for v in range(3)] for k in range(2)]
        nextq = [s[:, 0:(PAD - 1) * LOW].rearrange("p (r c) -> p r c", c=LOW) for s in shuf]
        xs = C[1][:].rearrange("p a r c -> p (a r c)")[:, 0:4 * (LT + 1) * P].rearrange("p (a i n) -> p a i n", a=2, i=2)
        XT = sbt("XT", [P, 2, 2, LT + 1, P])
        xv = X[:].rearrange("p (r c) -> p r c", c=IMG)
        NX = 4 * LT + 2

        def xt_index(n):
            if n < 4 * LT:
                return n // (2 * LT), n // LT % 2, n % LT
            return 1, n - 4 * LT, LT

        with nc.Block() as block:
            @block.sync
            def _(sp):
                sp.dma_start(X[:], x[bass.ds(b, 1)].rearrange("a c h w -> (a c) (h w)")).then_inc(sem("load"), 16)

            @block.gpsimd
            def _(pool):
                nc.gpsimd.memset(xg[:, 0, :], 0.0)
                nc.gpsimd.memset(low_hi[:].bitcast(f32), 0.0)
                nc.gpsimd.memset(low_lo[:].bitcast(f32), 0.0)
                nc.gpsimd.memset(sq[:], 0.0)
                for i in range(2):
                    nc.gpsimd.memset(stage[i][:], 0.0)
                for i in range(2):
                    nc.gpsimd.memset(XT[0:P, 1, i, LT, :], 0.0)
                nc.gpsimd.memset(gsm[:, 3:4], 0.0).then_inc(sem("consts"), 1)
                pool.wait_ge(sem("tr"), (NX + 3) // 4)
                for i in range(2):
                    nc.gpsimd.memset(C[i][:, :, 0, :], 0.0)
                    nc.gpsimd.memset(C[i][:, :, PAD - 1, :], 0.0).then_inc(sem("consts"), 1)
                pool.wait_ge(sem("free_d"), 2 * LT)
                for i in range(2):
                    nc.gpsimd.memset(nextq[i][0:LOW], 0.0).then_inc(sem("consts"), 1)

            @block.vector
            def _(dve):
                chain = chain_of(dve, sem("chain_dve"))
                dve.wait_ge(sem("load"), 16)
                for k in range(NC):
                    last = nc.vector.bn_stats(gst[:, k, :], X[:, k * BANK:(k + 1) * BANK])
                chain(last)
                chain(nc.vector.bn_aggr(gmv[:], gst[:]))
                chain(nc.vector.tensor_copy(ge2[:, 0:1], gmv[:, 0:1]))
                nc.vector.scalar_tensor_tensor(ge2[:, 1:2], gmv[:, 0:1], gmv[:, 0:1], gmv[:, 1:2], ALU.mult, ALU.add).then_inc(sem("ready_a"), 1)
                dve.wait_ge(sem("mm_a"), 1)
                m, v, y, t = gmv[:, 0:1], gmv[:, 1:2], gsm[:, 0:1], gsm[:, 1:2]
                chain(nc.vector.tensor_copy(gmv[:], ps[:, 7, 0:2]))
                chain(nc.vector.tensor_tensor(t, m, m, ALU.mult))
                chain(nc.vector.tensor_tensor(v, v, t, ALU.subtract))
                chain(nc.vector.tensor_scalar(v, v, GN_EPS, None, ALU.add))
                nc.vector.tensor_copy(t, v).then_inc(sem("ready_b"), 1)
                dve.wait_ge(sem("ready_c"), 1)
                newton_rsqrt(dve, chain, y, v, t)
                dve.wait_ge(sem("consts"), 1)
                chain(nc.vector.tensor_scalar(xg[:, 1:IMG + 1, :], xv, m, y, ALU.subtract, ALU.mult))
                down = xg[:, 1:IMG + 1:2, 0:IMG:2]
                nc.vector.tensor_tensor(sq[:, 1:1 + LOW, 1:1 + LOW], down, down, ALU.mult).then_inc(sem("ready_d"), 1)
                chain(nc.vector.tensor_copy(low_hi[:, 1:1 + LOW, 1:1 + LOW], down))
                nc.vector.tensor_tensor(low_lo[:, 1:1 + LOW, 1:1 + LOW], down, low_hi[:, 1:1 + LOW, 1:1 + LOW].bitcast(f32),
                                        ALU.subtract).then_inc(sem("ready_e"), 1)
                dve.wait_ge(sem("mm_b"), 1)
                n2 = shuf[0][:, 0:PAD * PAD]
                nc.vector.tensor_copy(n2, ps[:, 4:7, :].rearrange("p a n -> p (a n)")[:, 0:PAD * PAD]).then_inc(sem("ready_f"), 1)
                dve.wait_ge(sem("ready_f"), 1)
                n2 = n2.rearrange("p (r c) -> p r c", c=PAD)
                rows = shuf[1][:, 0:PAD * LOW].rearrange("p (r c) -> p r c", c=LOW)
                chain(nc.vector.tensor_tensor(rows, n2[:, :, 0:LOW], n2[:, :, 1:1 + LOW], ALU.add))
                chain(nc.vector.tensor_tensor(rows, rows, n2[:, :, 2:2 + LOW], ALU.add))
                box = tile_order(e[0][:])
                chain(nc.vector.tensor_tensor(box, split_rows(rows[:, 0:LOW, :]), split_rows(rows[:, 1:1 + LOW, :]), ALU.add))
                chain(nc.vector.tensor_tensor(box, box, split_rows(rows[:, 2:2 + LOW, :]), ALU.add))
                chain(nc.vector.tensor_scalar(e[0][:], e[0][:], PATCH_EPS * PATCH_EPS, None, ALU.max))
                nc.vector.tensor_copy(gsm[:, 2:3], e[0][:, 0:1]).then_inc(sem("ready_g"), 1)
                dve.wait_ge(sem("ready_h"), 1)
                newton_rsqrt(dve, chain, wgt[:], e[0][:], e[1][:])
                chain(nc.vector.scalar_tensor_tensor(wgt[:], wgt[:], SCALE0, mm[:], ALU.mult, ALU.mult))

                def finish(pt):
                    dve.wait_ge(sem("exp_done"), pt + 1)
                    chain(nc.vector.reciprocal(rz[:, pt:pt + 1], zs[:, pt:pt + 1]))
                    if pt >= 2:
                        dve.wait_ge(sem("mm_d"), pt - 1)
                    nc.vector.tensor_scalar(diag[pt % 2][:], ident[:], rz[:, pt:pt + 1], None, ALU.mult)
                    nc.vector.tensor_tensor(e[pt % 2][:], e[pt % 2][:], mm[:], ALU.mult).then_inc(sem("free_b"), 1)

                def fold_columns(pt):
                    dve.wait_ge(sem("free_c"), pt + 1)
                    s = stage[pt % 2]
                    flat = s[:].rearrange("p a r c -> p (a r c)")
                    for i, lanes in enumerate(([max(j - 1, 0) for j in range(LOW)], [min(j + 1, LOW - 1) for j in range(LOW)])):
                        chain(nc.vector.stream_shuffle(shuf[i][:, 0:LT * ROWS * PAD], flat, lanes))
                        sh = shuf[i][:, 0:LT * ROWS * PAD].rearrange("p (a r c) -> p a r c", r=ROWS, c=PAD)
                        keep = (left, right)[i]
                        nc.vector.scalar_tensor_tensor(C[i][:, :, 1 + ROWS * pt:1 + ROWS * pt + ROWS, :], sh[:, :, :, 2 * i:2 * i + LOW],
                                                       keep[:], s[:, :, :, 1:1 + LOW], ALU.mult, ALU.add).then_inc(sem("free_d"), 1)

                for pt in range(LT):
                    dve.wait_ge(sem("mm_c"), pt + 1)
                    if pt >= 2:
                        dve.wait_ge(sem("mm_d"), pt - 1)
                    chain(nc.vector.tensor_tensor_reduce(out=e[pt % 2][:], in0=ps[:, 2 * (pt % 2):2 * (pt % 2) + 2, :].rearrange("p a n -> p (a n)"),
                                                         in1=wgt[:], scale=1.0, scalar=-3.0e38, op0=ALU.mult, op1=ALU.max,
                                                         accum_out=nmx[:, pt:pt + 1]))
                    nc.vector.tensor_scalar(nmx[:, pt:pt + 1], nmx[:, pt:pt + 1], -1.0, None, ALU.mult).then_inc(sem("free_a"), 1)
                    finish(pt)
                    if pt >= 1:
                        fold_columns(pt - 1)
                fold_columns(LT - 1)
                dve.wait_ge(sem("free_d"), 2 * LT)
                dve.wait_ge(sem("scores_done"), 2 * (ROWS - 1))
                dve.wait_ge(sem("consts"), 5)
                dve.wait_ge(sem("misc_pe"), 1)
                for t in range(LT - 1, -1, -1):
                    for i in range(2):
                        if t < LT - 1:
                            dve.wait_ge(sem("sum_dve"), 2 * (LT - 1 - t) + i - 1)
                        above = C[i][:, t - 1, 0:PAD - 1, :] if t else nextq[i][:]
                        nc.vector.tensor_tensor(C[i][:, t, 1:PAD, :], C[i][:, t, 1:PAD, :], above, ALU.add).then_inc(sem("sum_dve"), 1)
                dve.wait_ge(sem("pv_done"), 1)
                for a in range(2):
                    for i in range(2):
                        for n in range(2):
                            half = xv[:, a + LOW * n:LOW * n + LOW:2, i:IMG:2]
                            nc.vector.scalar_tensor_tensor(half, ps[:, 4 * a + 2 * i + n, :].rearrange("p (r c) -> p r c", c=LOW), 0.25, half,
                                                           ALU.mult, ALU.add).then_inc(sem("ready_a"), 1)

            @block.tensor
            def _(pe):
                pe.wait_ge(sem("ready_a"), 1)
                nc.tensor.matmul(ps[:, 7, 0:2], gmat[:], ge2[:], start=True, stop=True).then_inc(sem("mm_a"), 1)
                pe.wait_ge(sem("ready_d"), 1)
                flat = sq[:].rearrange("p r c -> p (r c)")
                for k in range(3):
                    n = min(BANK, PAD * PAD - k * BANK)
                    last = nc.tensor.matmul(ps[:, 4 + k, 0:n], ones[:], flat[:, k * BANK:k * BANK + n], start=True, stop=True)
                last.then_inc(sem("mm_b"), 1)

                def scores(pt):
                    if pt >= 2:
                        pe.wait_ge(sem("free_a"), pt - 1)
                    k = 0
                    for wt, mv in ((0, low_hi), (0, low_lo), (1, low_hi)):
                        for u in range(3):
                            for v in range(3):
                                for n in range(2):
                                    win = mv[:, u:u + LOW, v:v + LOW].rearrange("p (q t) c -> p t q c", t=LT)[:, 4 * n:4 * n + 4]
                                    last = nc.tensor.matmul(ps[:, 2 * (pt % 2) + n, :],
                                                            shifted[wt][v][:, ROWS * pt + u:ROWS * pt + u + ROWS, :].rearrange("p r c -> p (r c)"),
                                                            win, start=(k == 0), stop=(k == 26))
                                k += 1
                    last.then_inc(sem("mm_c"), 1)

                def transpose_exps(pt):
                    pe.wait_ge(sem("free_b"), pt + 1)
                    if pt >= 2:
                        pe.wait_ge(sem("free_c"), pt - 1)
                    for lt in range(LT):
                        k = 4 + 2 * (pt % 2) + lt // 4
                        last = nc.tensor.matmul(ps[:, k, (lt % 4) * P:(lt % 4 + 1) * P], e[pt % 2][:, lt * P:(lt + 1) * P], diag[pt % 2][:], start=True, stop=True)
                    last.then_inc(sem("mm_d"), 1)

                pe.wait_ge(sem("ready_e"), 1)
                pe.wait_ge(sem("ln_norm"), 6)
                scores(0)
                pe.wait_ge(sem("ln_tr"), 4)
                pe.wait_ge(sem("ready_f"), 1)
                for n in range(NX):
                    a, i, t = xt_index(n)
                    if n % 4 == 0 and n >= 16:
                        pe.wait_ge(sem("tr"), n // 4 - 3)
                    last = nc.tensor.transpose(ps[:, 4 + n // 4 % 4, (n % 4) * P:(n % 4 + 1) * P], xs[:, a, i, t * P:(t + 1) * P], ident[:])
                    if n % 4 == 3 or n == NX - 1:
                        last.then_inc(sem("move"), 1)
                scores(1)
                pe.wait_ge(sem("tr"), (NX + 3) // 4)
                for pt in range(LT):
                    transpose_exps(pt)
                    if pt + 2 < LT:
                        scores(pt + 2)
                pe.wait_ge(sem("free_c"), LT)
                pe.wait_ge(sem("free_a"), LT)
                pe.wait_ge(sem("free_d"), 2 * LT)
                for i in range(2):
                    for n in range(2):
                        last = nc.tensor.matmul(ps[:, 4 + 2 * i + n, :], XT[:, 1, i, LT, :], C[i][:, LT - 1, 16 * n + 1:16 * n + 17, :], start=True, stop=False)
                last.then_inc(sem("misc_pe"), 1)
                for t in range(LT - 1, -1, -1):
                    for i in range(2):
                        pe.wait_ge(sem("sum_dve"), 2 * (LT - 1 - t) + i + 1)
                        for a in range(2):
                            for n in range(2):
                                last = nc.tensor.matmul(ps[:, 4 * a + 2 * i + n, :], XT[:, a, i, t, :], C[i][:, t, 16 * n + 1 + a:16 * n + 17 + a, :],
                                                        start=(a == 0 and t == LT - 1), stop=(t == 0))
                last.then_inc(sem("pv_done"), 1)

            @block.scalar
            def _(act):
                act.wait_ge(sem("ready_b"), 1)
                nc.scalar.activation(gsm[:, 0:1], gmv[:, 1:2], ACT.Ln).then_inc(sem("chain_act"), 1)
                act.wait_ge(sem("chain_act"), 1)
                nc.scalar.activation(gsm[:, 0:1], gsm[:, 0:1], ACT.Exp, scale=-0.5).then_inc(sem("ready_c"), 1)
                act.wait_ge(sem("ready_e"), 1)
                for k, part in enumerate((low_hi, low_lo)):
                    for v in range(3):
                        nc.scalar.activation(shifted[k][v][:], part[:, :, v:v + LOW].bitcast(f32), ACT.Copy).then_inc(sem("ln_norm"), 1)
                for a in range(2):
                    tiles = LT + a
                    for i in range(2):
                        dst = xs[:, a, i, 0:tiles * P].rearrange("p (t q c) -> p t q c", q=ROWS, c=LOW)
                        for q in range(ROWS):
                            r0 = 2 * LT * q + 1 - a
                            ins = nc.scalar.activation(dst[:, :, q, :], xg[:, r0:r0 + 2 * tiles - 1:2, i:IMG:2], ACT.Copy)
                        ins.then_inc(sem("ln_tr"), 1)
                act.wait_ge(sem("ready_g"), 1)
                nc.scalar.activation(wgt[:], e[0][:], ACT.Ln).then_inc(sem("chain_act"), 1)
                act.wait_ge(sem("chain_act"), 2)
                nc.scalar.activation(wgt[:], wgt[:], ACT.Exp, scale=-0.5).then_inc(sem("ready_h"), 1)
                act.wait_ge(sem("consts"), 1)
                for k in range((NX + 3) // 4):
                    act.wait_ge(sem("move"), k + 1)
                    a, i, t = xt_index(4 * k)
                    if k < LT:
                        nc.scalar.activation(XT[:, a, i, t:t + 4, :], ps[:, 4 + k % 4, :].rearrange("p (r n) -> p r n", n=P), ACT.Copy).then_inc(sem("tr"), 1)
                    else:
                        q = P - LOW
                        nc.scalar.activation(XT[q:P, 1, :, LT, :], ps[q:P, 4 + k % 4, 0:2 * P].rearrange("p (r n) -> p r n", n=P), ACT.Copy).then_inc(sem("tr"), 1)
                for pt in range(LT + 1):
                    if pt < LT:
                        act.wait_ge(sem("free_a"), pt + 1)
                        nc.scalar.activation(e[pt % 2][:], e[pt % 2][:], ACT.Exp, bias=nmx[:, pt:pt + 1], accum_out=zs[:, pt:pt + 1]).then_inc(sem("exp_done"), 1)
                    if pt >= 1:
                        q = pt - 1
                        act.wait_ge(sem("mm_d"), q + 1)
                        if q >= 2:
                            act.wait_ge(sem("free_d"), 2 * (q - 1))
                        k = 4 + 2 * (q % 2)
                        nc.scalar.activation(stage[q % 2][:, :, :, 1:1 + LOW], ps[:, k:k + 2, :].rearrange("p k (a r c) -> p (k a) r c", r=ROWS, c=LOW),
                                             ACT.Copy).then_inc(sem("free_c"), 1)
                act.wait_ge(sem("free_d"), 2 * LT)
                act.wait_ge(sem("consts"), 3)
                for i in range(2):
                    for q in range(ROWS - 1):
                        nc.scalar.activation(nextq[i][(q + 1) * LOW:(q + 2) * LOW], C[i][q * LOW:(q + 1) * LOW, LT - 1, 0:PAD - 1, :],
                                             ACT.Copy).then_inc(sem("scores_done"), 1)


def bound_logits(nc, sem, chain_of, ps, ones, wq, wk, bq, bk, bounded):
    with ExitStack() as tmp:
        def sbt(name, shape, dt=f32):
            return tmp.enter_context(nc.sbuf_tensor(name, shape, dt))
        same = sbt("same", [P, P])
        gram = sbt("gram", [P, 2, P])
        square = sbt("square", [P, 2, P])
        scratch = sbt("scratch", [P, 2, P])
        rows = sbt("rows", [P, 4])
        norms = sbt("norms", [P, 4])
        roots = sbt("roots", [P, 4])
        length = sbt("length", [P, 2])
        fine = sbt("fine", [P, 5])
        good = sbt("good", [P, 1])
        with nc.Block() as block:
            @block.gpsimd
            def _(pool):
                chain = chain_of(pool, sem("chain_pool"))
                chain(nc.gpsimd.memset(same[:], 1.0))
                s3 = same[:].rearrange("p (h d) -> p h d", d=D)
                chain(nc.gpsimd.affine_select(out=s3, in_=s3, compare_op=ALU.is_ge, fill=0.0, base=0,
                                              pattern=[[-D, H], [0, D]], channel_multiplier=1))
                chain(nc.gpsimd.affine_select(out=s3, in_=s3, compare_op=ALU.is_ge, fill=0.0, base=D - 1,
                                              pattern=[[D, H], [0, D]], channel_multiplier=-1))

            @block.tensor
            def _(pe):
                for k, w in enumerate((wq, wk)):
                    nc.tensor.matmul(ps[:, k, 0:P], w[:], w[:], start=True, stop=True).then_inc(sem("mm_a"), 1)
                for k in range(2):
                    pe.wait_ge(sem("ready_a"), k + 1)
                    nc.tensor.matmul(ps[:, 2 + k, 0:P], gram[:, k, :], gram[:, k, :], start=True, stop=True).then_inc(sem("mm_b"), 1)
                pe.wait_ge(sem("ready_b"), 4)
                nc.tensor.matmul(ps[:, 4, 0:4], same[:], rows[:], start=True, stop=True).then_inc(sem("mm_c"), 1)
                pe.wait_ge(sem("ready_e"), 1)
                nc.tensor.matmul(ps[0:1, 5, 0:1], good[:], ones[:, 0:1], start=True, stop=True).then_inc(sem("mm_d"), 1)

            @block.scalar
            def _(act):
                act.wait_ge(sem("ready_c"), 1)
                nc.scalar.activation(roots[:], norms[:], ACT.Ln).then_inc(sem("chain_act"), 1)
                act.wait_ge(sem("chain_act"), 1)
                nc.scalar.activation(roots[:, 0:2], roots[:, 0:2], ACT.Exp, scale=0.125).then_inc(sem("ready_d"), 1)
                nc.scalar.activation(roots[:, 2:4], roots[:, 2:4], ACT.Exp, scale=0.5).then_inc(sem("ready_d"), 1)

            @block.vector
            def _(dve):
                chain = chain_of(dve, sem("chain_dve"))
                dve.wait_ge(sem("chain_pool"), 3)
                for k in range(2):
                    dve.wait_ge(sem("mm_a"), k + 1)
                    nc.vector.tensor_tensor(gram[:, k, :], ps[:, k, 0:P], same[:], ALU.mult).then_inc(sem("ready_a"), 1)
                for k, bias in enumerate((bq, bk)):
                    nc.vector.tensor_tensor(rows[:, 2 + k:3 + k], bias[:], bias[:], ALU.mult).then_inc(sem("ready_b"), 1)
                for k in range(2):
                    dve.wait_ge(sem("mm_b"), k + 1)
                    chain(nc.vector.tensor_copy(square[:, k, :], ps[:, 2 + k, 0:P]))
                    nc.vector.tensor_tensor_reduce(out=scratch[:, k, :], in0=square[:, k, :], in1=square[:, k, :], scale=1.0, scalar=0.0,
                                                   op0=ALU.mult, op1=ALU.add, accum_out=rows[:, k:k + 1]).then_inc(sem("ready_b"), 1)
                dve.wait_ge(sem("mm_c"), 1)
                chain(nc.vector.tensor_scalar(fine[:, 0:4], ps[:, 4, 0:4], 1.0e18, None, ALU.is_le))
                nc.vector.tensor_scalar(norms[:], ps[:, 4, 0:4], 1.0e-15, 1.0e18, ALU.max, ALU.min).then_inc(sem("ready_c"), 1)
                dve.wait_ge(sem("ready_d"), 2)
                chain(nc.vector.scalar_tensor_tensor(length[:], roots[:, 0:2], float(P) ** 0.5, roots[:, 2:4], ALU.mult, ALU.add))
                chain(nc.vector.tensor_tensor(fine[:, 4:5], length[:, 0:1], length[:, 1:2], ALU.mult))
                chain(nc.vector.tensor_scalar(fine[:, 4:5], fine[:, 4:5], LOGIT_BOUND / SCALE1, None, ALU.is_le))
                nc.vector.tensor_reduce(good[:], fine[:], AX.X, ALU.min).then_inc(sem("ready_e"), 1)
                dve.wait_ge(sem("mm_d"), 1)
                nc.vector.tensor_copy(bounded[:], ps[0:1, 5, 0:1]).then_inc(sem("ready_f"), 1)
                dve.wait_ge(sem("ready_f"), 1)


def self_attention_with_maximum(nc, sem, clear_all, X, ps, ident, wq, bq, wk, bk, wp, bp, xnT, V):
    with ExitStack() as tmp:
        def sbt(name, shape, dt=f32):
            return tmp.enter_context(nc.sbuf_tensor(name, shape, dt))
        kf = sbt("kf", [P, TOK])
        qf = sbt("qf", [P, TOK])
        qt = sbt("qt", [P, P])
        row = sbt("row", [P, TOK])
        pt = sbt("pt", [P, NT, P])
        nmax = sbt("nmaxg", [P, H])
        total = sbt("total", [P, H])
        rtotal = sbt("rtotal", [P, H])
        heads = sbt("heads", [P, P])
        headsT = sbt("headsT", [P, P])
        with nc.Block() as block:
            @block.tensor
            def _(pe):
                for g in range(2 * NC):
                    if g >= 8:
                        pe.wait_ge(sem("free_a"), g // 2 - 3)
                        pe.wait_ge(sem("free_b"), g // 2 - 3)
                    nc.tensor.matmul(ps[:, g % 8, :], (wk, wq)[g % 2][:], xnT[:, g // 2 * BANK:(g // 2 + 1) * BANK],
                                     start=True, stop=True).then_inc(sem("mm_a"), 1)

            @block.scalar
            def _(act):
                for g in range(NC):
                    act.wait_ge(sem("mm_a"), 2 * g + 1)
                    nc.scalar.activation(kf[:, g * BANK:(g + 1) * BANK], ps[:, 2 * g % 8, :], ACT.Identity, bias=bk[:]).then_inc(sem("free_a"), 1)

            @block.vector
            def _(dve):
                for g in range(NC):
                    dve.wait_ge(sem("mm_a"), 2 * g + 2)
                    nc.vector.tensor_scalar(qf[:, g * BANK:(g + 1) * BANK], ps[:, (2 * g + 1) % 8, :], bq[:], None, ALU.add).then_inc(sem("free_b"), 1)
        clear_all()
        with nc.Fori(0, NT) as t:
            with nc.Block() as block:
                @block.tensor
                def _(pe):
                    pe.wait_ge(sem("ready_a"), 1)
                    for h in range(H):
                        rows = slice(h * D, (h + 1) * D)
                        if h:
                            pe.wait_ge(sem("ready_f"), h)
                        for g in range(NC):
                            nc.tensor.matmul(ps[:, g, :], qt[rows, :], kf[rows, g * BANK:(g + 1) * BANK],
                                             start=True, stop=True).then_inc(sem("mm_a"), 1)
                        pe.wait_ge(sem("ready_d"), h + 1)
                        for g in range(NC):
                            for r in range(4):
                                k = 4 * g + r
                                last = nc.tensor.transpose(ps[:, g, r * P:(r + 1) * P], row[:, k * P:(k + 1) * P], ident[:])
                            last.then_inc(sem("mm_b"), 1)
                        pe.wait_ge(sem("ready_e"), NC * (h + 1))
                        for k in range(NT):
                            last = nc.tensor.matmul(ps[:, 0, 0:D], pt[:, k, :], V[:, k, rows], start=(k == 0), stop=(k == NT - 1))
                        last.then_inc(sem("mm_c"), 1)
                    pe.wait_ge(sem("ready_f"), H)
                    nc.tensor.transpose(ps[:, 1, 0:P], heads[:], ident[:]).then_inc(sem("mm_d"), 1)
                    pe.wait_ge(sem("ready_g"), 1)
                    nc.tensor.matmul(ps[:, 2, 0:P], wp[:], headsT[:], start=True, stop=True).then_inc(sem("mm_d"), 1)

                @block.scalar
                def _(act):
                    for h in range(H):
                        if h:
                            act.wait_ge(sem("mm_b"), NC * h)
                        for g in range(NC):
                            act.wait_ge(sem("mm_a"), NC * h + g + 1)
                            nc.scalar.activation(row[:, g * BANK:(g + 1) * BANK], ps[:, g, :], ACT.Copy).then_inc(sem("ready_b"), 1)
                        act.wait_ge(sem("ready_c"), h + 1)
                        nc.scalar.activation(row[:], row[:], ACT.Exp, bias=nmax[:, h:h + 1], scale=SCALE1, accum_out=total[:, h:h + 1]).then_inc(sem("ready_d"), 1)
                    act.wait_ge(sem("mm_d"), 1)
                    nc.scalar.activation(headsT[:], ps[:, 1, 0:P], ACT.Copy).then_inc(sem("ready_g"), 1)

                @block.vector
                def _(dve):
                    nc.vector.tensor_copy(qt[:], qf[:, bass.ds(t * P, P)]).then_inc(sem("ready_a"), 1)
                    for h in range(H):
                        dve.wait_ge(sem("ready_b"), NC * (h + 1))
                        nc.vector.reduce_max(nmax[:, h:h + 1], row[:], AX.X).then_inc(sem("chain_dve"), 1)
                        dve.wait_ge(sem("chain_dve"), 2 * h + 1)
                        nc.vector.tensor_scalar(nmax[:, h:h + 1], nmax[:, h:h + 1], -SCALE1, None, ALU.mult).then_inc(sem("ready_c"), 1)
                        dve.wait_ge(sem("ready_d"), h + 1)
                        nc.vector.reciprocal(rtotal[:, h:h + 1], total[:, h:h + 1]).then_inc(sem("chain_dve"), 1)
                        for g in range(NC):
                            dve.wait_ge(sem("mm_b"), NC * h + g + 1)
                            nc.vector.tensor_copy(pt[:, 4 * g:4 * g + 4, :], ps[:, g, :].rearrange("p (r n) -> p r n", n=P)).then_inc(sem("ready_e"), 1)
                        dve.wait_ge(sem("mm_c"), h + 1)
                        dve.wait_ge(sem("chain_dve"), 2 * h + 2)
                        nc.vector.tensor_scalar(heads[:, h * D:(h + 1) * D], ps[:, 0, 0:D], rtotal[:, h:h + 1], None, ALU.mult).then_inc(sem("ready_f"), 1)
                    dve.wait_ge(sem("mm_d"), 2)
                    xc = X[:, bass.ds(t * P, P)]
                    nc.vector.scalar_tensor_tensor(xc, ps[:, 2, 0:P], bp[:], xc, ALU.add, ALU.add).then_inc(sem("ready_h"), 1)
            clear_all()


def self_attention(nc, sem, X, ps, ones, wq, bq, wp, bp, xnT, KS, V):
    with ExitStack() as tmp:
        def sbt(name, shape, dt=f32):
            return tmp.enter_context(nc.sbuf_tensor(name, shape, dt))
        QS = sbt("QS", [3 * D, 2, H, BANK], f32r)
        qhi = sbt("qhi", [P, BANK], f32r)
        qlo = sbt("qlo", [P, BANK], f32r)
        PR = sbt("PR", [P, PBUFS, H * BANK])
        acc = sbt("acc", [P, 2, 2, H * BANK])
        raw = sbt("raw", [P, BANK])
        rz = sbt("rz", [P, BANK])
        U = 2 * NT
        ND, NP_ = len(DVE_TILES) - 1, len(POOL_TILES) - 1

        def sums_with(tiles, kt):
            return max(tiles.index(kt), 1)


        with nc.Block() as block:
            @block.sync
            def _(sp):
                def stack(c, par):
                    sp.wait_ge(sem("ready_a"), c + 1)
                    move_parts(sp, sem("move"), QS[:, par, :, :], qhi[:], qlo[:], (0, 1, 0))
                stack(0, 0)
                stack(1, 1)
                with sp.Fori(1, NC - 1, 2) as i:
                    stack(i + 1, 0)
                    stack(i + 2, 1)
                stack(NC, 0)
                sp.wait_ge(sem("move"), 16 * MOVES * (NC + 1))

            @block.tensor
            def _(pe):
                def queries(c):
                    nc.tensor.matmul(ps[:, 7, :], wq[:], xnT[:, bass.ds(c * BANK, BANK)], start=True, stop=True).then_inc(sem("misc_pe"), 1)

                def scores(u, par):
                    kt, hp = u // 2, u % 2
                    for h in (2 * hp, 2 * hp + 1):
                        last = nc.tensor.matmul(ps[:, 2 * slot_of(u) + h % 2, :], KS[:, h, kt * P:(kt + 1) * P],
                                                QS[:, par, h, :], start=True, stop=True)
                    last.then_inc(sem("scores_done"), 1)

                def finish(c, par):
                    pe.wait_ge(sem("ready_a"), c + 2)
                    pe.wait_ge(sem("sum_dve"), (c + 1) * ND)
                    pe.wait_ge(sem("sum_pool"), (c + 1) * NP_)
                    for h in range(H):
                        for k in range(2):
                            last = nc.tensor.matmul(ps[h * D:(h + 1) * D, 7, :], ones[:, 0:D],
                                                    acc[:, par, k, h * BANK:(h + 1) * BANK], start=(k == 0), stop=(k == 1))
                    last.then_inc(sem("misc_pe"), 1)

                def project(c):
                    pe.wait_ge(sem("ready_b"), c + 1)
                    nc.tensor.matmul(ps[:, 7, :], wp[:], rz[:], start=True, stop=True).then_inc(sem("misc_pe"), 1)

                def block_of(i, par, first):
                    nxt = 1 - par
                    for kt in range(NT):
                        for u in (2 * kt + 2, 2 * kt + 3):
                            if u < U:
                                if u >= 3:
                                    pe.wait_ge(sem("exp_done"), i * U + (U - 2 if u == U - 1 else u - 2))
                                scores(u, par)
                            elif u == U:
                                pe.wait_ge(sem("move"), (i + 2) * (16 * MOVES))
                                scores(0, nxt)
                            else:
                                pe.wait_ge(sem("exp_done"), (i + 1) * U)
                                scores(1, nxt)
                        if kt == 0 and not first:
                            pe.wait_ge(sem("free_a"), i)
                        pe.wait_ge(sem("exp_done"), i * U + (2 * kt + 2))
                        for h in range(H):
                            last = nc.tensor.matmul(ps[h * D:(h + 1) * D, 6, :], V[:, kt, h * D:(h + 1) * D],
                                                    PR[:, kt % PBUFS, h * BANK:(h + 1) * BANK], start=(kt == 0), stop=(kt == NT - 1))
                        last.then_inc(sem("pv_done"), 1)
                        if kt == 4 and not first:
                            finish(i - 1, 1 - par)
                        if kt == 9 and not first:
                            project(i - 1)
                        if kt == 13:
                            if first:
                                pe.wait_ge(sem("ready_a"), 1)
                            else:
                                pe.wait_ge(sem("misc_free"), i)
                            queries(i + 1)

                queries(0)
                pe.wait_ge(sem("move"), 16 * MOVES)
                scores(0, 0)
                scores(1, 0)
                block_of(0, 0, True)
                with pe.Fori(1, NC - 1, 2) as i:
                    block_of(i, 1, False)
                    block_of(i + 1, 0, False)
                block_of(NC - 1, 1, False)
                finish(NC - 1, 1)
                project(NC - 1)

            @block.scalar
            def _(act):
                def block_of(i, first):
                    for kt in range(NT):
                        if kt >= PBUFS:
                            k = kt - PBUFS
                            act.wait_ge(sem("pv_done"), i * NT + (k + 1))
                            if k in DVE_TILES:
                                act.wait_ge(sem("sum_dve"), i * ND + sums_with(DVE_TILES, k))
                            else:
                                act.wait_ge(sem("sum_pool"), i * NP_ + sums_with(POOL_TILES, k))
                        elif not first and kt == 0:
                            act.wait_ge(sem("pv_done"), i * NT - 1)
                            act.wait_ge(sem("sum_dve"), i * ND - 1)
                        elif not first and kt == 1:
                            act.wait_ge(sem("pv_done"), i * NT)
                            act.wait_ge(sem("sum_dve"), i * ND)
                        for hp in range(2):
                            u = 2 * kt + hp
                            act.wait_ge(sem("scores_done"), i * U + (u + 1))
                            s = 2 * slot_of(u)
                            nc.scalar.activation(PR[:, kt % PBUFS, hp * PAIR:(hp + 1) * PAIR], ps[:, s:s + 2, :].rearrange("p a n -> p (a n)"),
                                                 ACT.Exp, scale=SCALE1).then_inc(sem("exp_done"), 1)
                block_of(0, True)
                with act.Fori(1, NC) as i:
                    block_of(i, False)

            @block.gpsimd
            def _(pool):
                def block_of(i, par):
                    dst = acc[:, par, 1, :]
                    for k, kt in enumerate(POOL_TILES):
                        if k >= 1:
                            pool.wait_ge(sem("exp_done"), i * U + (2 * kt + 2))
                        if k == 1:
                            nc.gpsimd.tensor_tensor(dst, PR[:, POOL_TILES[0] % PBUFS, :], PR[:, kt % PBUFS, :], ALU.add).then_inc(sem("sum_pool"), 1)
                        elif k > 1:
                            pool.wait_ge(sem("sum_pool"), i * NP_ + (k - 1))
                            nc.gpsimd.tensor_tensor(dst, dst, PR[:, kt % PBUFS, :], ALU.add).then_inc(sem("sum_pool"), 1)
                with pool.Fori(0, NC, 2) as i:
                    block_of(i, 0)
                    block_of(i + 1, 1)

            @block.vector
            def _(dve):
                def queries_low(c):
                    dve.wait_ge(sem("ready_c"), c + 1)
                    nc.vector.scalar_tensor_tensor(qlo[:], ps[:, 7, :], bq[:], qhi[:].bitcast(f32), ALU.add, ALU.subtract).then_inc(sem("ready_a"), 1)

                def finish(i):
                    dve.wait_ge(sem("misc_pe"), 3 * i)
                    nc.vector.reciprocal(rz[:], ps[:, 7, :]).then_inc(sem("ready_d"), 1)
                    dve.wait_ge(sem("ready_d"), i)
                    nc.vector.tensor_tensor(rz[:], rz[:], raw[:], ALU.mult).then_inc(sem("ready_b"), 1)

                def add_out(i):
                    dve.wait_ge(sem("misc_pe"), 3 * i + 1)
                    xc = X[:, bass.ds(i * BANK - BANK, BANK)]
                    nc.vector.scalar_tensor_tensor(xc, ps[:, 7, :], bp[:], xc, ALU.add, ALU.add).then_inc(sem("misc_free"), 1)

                def block_of(i, par, first):
                    dst = acc[:, par, 0, :]
                    for kt in range(NT):
                        k = DVE_TILES.index(kt) if kt in DVE_TILES else 0
                        if k >= 1:
                            dve.wait_ge(sem("exp_done"), i * U + (2 * kt + 2))
                        if k == 1:
                            nc.vector.tensor_tensor(dst, PR[:, DVE_TILES[0] % PBUFS, :], PR[:, kt % PBUFS, :], ALU.add).then_inc(sem("sum_dve"), 1)
                        elif k > 1:
                            dve.wait_ge(sem("sum_dve"), i * ND + (k - 1))
                            nc.vector.tensor_tensor(dst, dst, PR[:, kt % PBUFS, :], ALU.add).then_inc(sem("sum_dve"), 1)
                        if kt == 6 and not first:
                            finish(i)
                        if kt == 10 and not first:
                            add_out(i)
                        if kt == 15:
                            dve.wait_ge(sem("misc_pe"), 3 * i + 2)
                            dve.wait_ge(sem("move"), (i + 1) * (16 * MOVES))
                            nc.vector.tensor_scalar(qhi[:], ps[:, 7, :], bq[:], None, ALU.add).then_inc(sem("ready_c"), 1)
                        if kt == 16:
                            queries_low(i + 1)
                    dve.wait_ge(sem("pv_done"), (i + 1) * NT)
                    nc.vector.tensor_copy(raw[:], ps[:, 6, :]).then_inc(sem("free_a"), 1)

                dve.wait_ge(sem("misc_pe"), 1)
                nc.vector.tensor_scalar(qhi[:], ps[:, 7, :], bq[:], None, ALU.add).then_inc(sem("ready_c"), 1)
                queries_low(0)
                block_of(0, 0, True)
                with dve.Fori(1, NC - 1, 2) as i:
                    block_of(i, 1, False)
                    block_of(i + 1, 0, False)
                block_of(NC - 1, 1, False)
                finish(NC)
                add_out(NC)


def experts(nc, sem, chain_of, ps, ident, poolT, t_d, sel_d, w1, w2, out):
    with ExitStack() as tmp:
        def sbt(name, shape, dt=f32):
            return tmp.enter_context(nc.sbuf_tensor(name, shape, dt))
        W1 = sbt("W1", [P, WBUFS, EG, HID])
        W2 = sbt("W2", [P, WBUFS, EG, HC, P])
        B1 = sbt("B1", [E, HID])
        B2 = sbt("B2", [E, P])
        b1T = sbt("b1T", [P, HC, E])
        hid = sbt("hid", [P, 2, EG, HC, NIMG])
        pre = sbt("pre", [P, 2, EG, HC, NIMG])
        outT = sbt("outT", [P, NIMG, E])
        outE = sbt("outE", [E, NIMG, P])
        tin = sbt("tin", [P, 2, TOK])
        sin = sbt("sin", [E, 2, TOK])
        w1_in = [sem(f"w1_in{k}") for k in range(WBUFS)]
        w2_in = [sem(f"w2_in{k}") for k in range(WBUFS)]
        out_done = [sem(f"out_done{k}") for k in range(2)]
        tok_in = [sem(f"tok_in{k}") for k in range(2)]
        with nc.Block() as block:
            @block.sync
            def _(sp):
                sp.dma_start(B1[:], w1[:, P, :]).then_inc(sem("load"), 16)
                sp.dma_start(B2[:], w2[:, HID, :]).then_inc(sem("load"), 16)
                for g in range(NEG):
                    if g >= WBUFS:
                        sp.wait_ge(sem("mm_b"), g - WBUFS + 1)
                    es = slice(g * EG, (g + 1) * EG)
                    sp.dma_start(W1[:, g % WBUFS], w1[es, 0:P, :].rearrange("e d h -> d e h")).then_inc(w1_in[g % WBUFS], 16)
                    sp.dma_start(W2[:, g % WBUFS], w2[es, 0:HID, :].rearrange("e (p c) o -> p e c o", c=HC)).then_inc(w2_in[g % WBUFS], 16)
                    if g == 3:
                        for b in range(2):
                            sp.dma_start(tin[:, b], t_d[b]).then_inc(tok_in[b % 2], 16)
                            sp.dma_start(sin[:, b], sel_d[b]).then_inc(tok_in[b % 2], 16)
                for b in range(2, NIMG):
                    sp.wait_ge(out_done[b % 2], 16 * (b // 2))
                    sp.dma_start(tin[:, b % 2], t_d[b]).then_inc(tok_in[b % 2], 16)
                    sp.dma_start(sin[:, b % 2], sel_d[b]).then_inc(tok_in[b % 2], 16)

            @block.tensor
            def _(pe):
                pe.wait_ge(sem("load"), 32)
                for c in range(HC):
                    last = nc.tensor.transpose(ps[:, 0, c * E:(c + 1) * E], B1[:].rearrange("e (p c) -> e p c", c=HC)[:, :, c], ident[0:E, 0:E])
                last.then_inc(sem("tr"), 1)

                def second(g):
                    pe.wait_ge(w2_in[g % WBUFS], 16 * (g // WBUFS + 1))
                    pe.wait_ge(sem("ready_f"), g + 1)
                    for k in range(EG):
                        n = (g * EG + k) * NIMG
                        for c in range(HC):
                            last = nc.tensor.matmul(ps[:, 3, n:n + NIMG], W2[:, g % WBUFS, k, c, :], hid[:, g % 2, k, c, :], start=(c == 0), stop=(c == HC - 1))
                    last.then_inc(sem("mm_b"), 1)

                for g in range(NEG):
                    pe.wait_ge(w1_in[g % WBUFS], 16 * (g // WBUFS + 1))
                    if g >= 2:
                        pe.wait_ge(sem("ready_d"), g - 1)
                    for k in range(EG):
                        for c in range(HC):
                            n = (k * HC + c) * NIMG
                            last = nc.tensor.matmul(ps[:, 1 + g % 2, n:n + NIMG], W1[:, g % WBUFS, k, :].rearrange("p (m c) -> p m c", c=HC)[:, :, c],
                                                    poolT[:, g * EG + k, :], start=True, stop=True)
                    last.then_inc(sem("mm_a"), 1)
                    if g >= 1:
                        second(g - 1)
                second(NEG - 1)
                pe.wait_ge(sem("ready_g"), 1)
                for b in range(NIMG):
                    last = nc.tensor.transpose(ps[0:E, 0, b * P:(b + 1) * P], outT[:, b, :], ident[:])
                last.then_inc(sem("tr"), 1)
                pe.wait_ge(sem("ready_h"), 1)
                for b in range(NIMG):
                    pe.wait_ge(tok_in[b % 2], 32 * (b // 2 + 1))
                    for c in range(NC):
                        n = b * NC + c
                        if n >= 4:
                            pe.wait_ge(sem("free_a"), n - 3)
                        nc.tensor.matmul(ps[:, 4 + n % 4, :], outE[:, b, :], sin[:, b % 2, c * BANK:(c + 1) * BANK], start=True, stop=True).then_inc(sem("mm_c"), 1)

            @block.scalar
            def _(act):
                for g in range(NEG):
                    act.wait_ge(sem("ready_d"), g + 1)
                    if g >= 2:
                        act.wait_ge(sem("mm_b"), g - 1)
                    nc.scalar.activation(hid[:, g % 2], pre[:, g % 2], ACT.Gelu).then_inc(sem("ready_f"), 1)
                for b in range(NIMG):
                    act.wait_ge(sem("free_a"), (b + 1) * NC)
                    act.dma_start(out[b].rearrange("c h w -> c (h w)"), tin[:, b % 2]).then_inc(out_done[b % 2], 16)
                for s in out_done:
                    act.wait_ge(s, 16 * (NIMG // 2))

            @block.vector
            def _(dve):
                chain = chain_of(dve, sem("chain_dve"))
                dve.wait_ge(sem("tr"), 1)
                chain(nc.vector.tensor_copy(b1T[:], ps[:, 0, 0:HC * E].rearrange("p (c e) -> p c e", e=E)))
                for g in range(NEG):
                    dve.wait_ge(sem("mm_a"), g + 1)
                    if g >= 2:
                        dve.wait_ge(sem("ready_f"), g - 1)
                    for k in range(EG):
                        e = g * EG + k
                        last = nc.vector.tensor_tensor(pre[:, g % 2, k], ps[:, 1 + g % 2, k * HC * NIMG:(k + 1) * HC * NIMG].rearrange("p (c b) -> p c b", b=NIMG),
                                                       b1T[:, :, e:e + 1].broadcast_to([P, HC, NIMG]), ALU.add)
                    last.then_inc(sem("ready_d"), 1)
                dve.wait_ge(sem("mm_b"), NEG)
                nc.vector.tensor_copy(outT[:].rearrange("p b e -> p e b"), ps[:, 3, 0:E * NIMG].rearrange("p (e b) -> p e b", b=NIMG)).then_inc(sem("ready_g"), 1)
                dve.wait_ge(sem("tr"), 2)
                nc.vector.tensor_tensor(outE[:], ps[0:E, 0, :].rearrange("e (b n) -> e b n", n=P),
                                        B2[:].rearrange("e (o n) -> e o n", o=1).broadcast_to([E, NIMG, P]), ALU.add).then_inc(sem("ready_h"), 1)
                for b in range(NIMG):
                    for c in range(NC):
                        n = b * NC + c
                        dve.wait_ge(sem("mm_c"), n + 1)
                        tc = tin[:, b % 2, c * BANK:(c + 1) * BANK]
                        nc.vector.tensor_tensor(tc, ps[:, 4 + n % 4, :], tc, ALU.add).then_inc(sem("free_a"), 1)


_INS = ['x', 'L0_conv_mask', 'L1_attn_W_qkv', 'L1_attn_b_qkv', 'L1_attn_W_proj', 'L1_attn_b_proj', 'L1_ffn_gate_w',
        'L1_ffn_gate_b', 'L1_ffn_weight1', 'L1_ffn_weight2']
_OUTS = [((4, 128, 64, 64), 'float32')]


def kernel(**inputs):
    import numpy as _np
    import concourse.bacc as _bacc
    from concourse import mybir as _mybir
    from concourse.bass_utils import run_bass_kernel_spmd as _run

    nc = _bacc.Bacc("TRN2", target_bir_lowering=False, num_devices=1)
    arrays, args = {}, []
    for name in _INS:
        a = _np.ascontiguousarray(inputs[name])
        arrays[f"in_{name}_dram"] = a
        args.append(nc.dram_tensor(f"in_{name}_dram", a.shape, _mybir.dt.from_np(a.dtype), kind="ExternalInput").ap())
    for i, (shape, dtype) in enumerate(_OUTS):
        dt = _mybir.dt.from_np(_np.dtype(dtype))
        args.append(nc.dram_tensor(f"out_{i}_dram", shape, dt, kind="ExternalOutput").ap())
    build(nc, *args)
    r = _run(nc, [arrays], core_ids=[0])
    got = tuple(r.results[0][f"out_{i}_dram"] for i in range(len(_OUTS)))
    return got[0]
```

```python
import concourse.bass as bass
from concourse import mybir
from contextlib import ExitStack

f32 = mybir.dt.float32
f32r = mybir.dt.float32r
ALU = mybir.AluOpType
ACT = mybir.ActivationFunctionType
AX = mybir.AxisListType

P = 128
NIMG = 4
IMG = 64
TOK = IMG * IMG
NT = TOK // P
BANK = 512
NC = TOK // BANK
H = 4
D = 32
G = 4
LOW = 32
LOC = LOW * LOW
PAD = LOW + 2
LT = LOC // P
ROWS = P // LOW
E = 64
HID = 512
HC = HID // P
GN_EPS, LN_EPS, PATCH_EPS = 1e-5, 1e-5, 1e-4
SCALE0 = 10.0
SCALE1 = float(P) ** -0.5
MOVES = 3 * H
PBUFS = 4
PAIR = 2 * BANK
POOL_TILES = (2, 3, 6, 9, 12, 15, 18, 21, 24, 27)
DVE_TILES = tuple(t for t in range(NT) if t not in POOL_TILES)
LOGIT_BOUND = 64.0
EG = 4
NEG = E // EG
WBUFS = 4
LANES = P // EG


def slot_of(u):
    return 1 if u == 2 * NT - 1 else u % 3


def split_rows(ap):
    return ap.rearrange("p (q t) c -> p q t c", t=LT)


def tile_order(ap):
    return ap.rearrange("p (t q c) -> p q t c", q=ROWS, c=LOW)


def build(nc, x, mask, w_qkv, b_qkv, w_proj, b_proj, gate_w, gate_b, w1, w2, out):
    ctx = ExitStack()
    sems = {}

    def sem(name):
        if name not in sems:
            sems[name] = ctx.enter_context(nc.semaphore(name))
        return sems[name]

    def clear_all():
        nums = [s.num for s in sems.values()]
        nc.all_engine_barrier(sems_to_clear=range(min(nums), max(nums) + 1))

    with ctx:
        def sb(name, shape, dt=f32):
            return ctx.enter_context(nc.sbuf_tensor(name, shape, dt))

        for n in ("load", "consts", "chain_pool", "chain_dve", "chain_act", "tr", "ready_a", "ready_b", "ready_c",
                  "ready_d", "ready_e", "ready_f", "ready_g", "ready_h", "store", "mm_a", "mm_b", "mm_c", "mm_d",
                  "free_a", "free_b", "free_c", "free_d", "exp_done", "scores_done", "pv_done", "sum_dve", "sum_pool",
                  "move", "misc_pe", "misc_free", "ln_tr", "ln_raw", "ln_var", "ln_log", "ln_exp", "ln_norm",
                  "ln_back", "ln_out"):
            sem(n)

        t_d = nc.dram_tensor("t_scratch", [NIMG, P, TOK], f32, kind="Internal").ap()
        sel_d = nc.dram_tensor("sel_scratch", [NIMG, E, TOK], f32, kind="Internal").ap()

        ps = ctx.enter_context(nc.psum_tensor("ps", [P, 8, BANK], f32))
        ident = sb("ident", [P, P])
        ones = sb("ones", [P, P])
        gmat = sb("gmat", [P, P])
        wq = sb("wq", [P, P])
        wk = sb("wk", [P, P])
        wv = sb("wv", [P, P])
        wp = sb("wp", [P, P])
        wgT = sb("wgT", [P, E])
        bq = sb("bq", [P, 1])
        bk = sb("bk", [P, 1])
        bp = sb("bp", [P, 1])
        bg = sb("bg", [E, 1])
        bv = sb("bv", [P, P])
        mm = sb("mm", [P, LOC])
        left = sb("left", [P, 1])
        right = sb("right", [P, 1])
        poolT = sb("poolT", [P, E, NIMG])
        bounded = sb("bounded", [1, 1], mybir.dt.int32)
        X = sb("X", [P, TOK])

        def newton_rsqrt(dve, chain, y, w, t):
            chain(nc.vector.tensor_tensor(t, y, y, ALU.mult))
            chain(nc.vector.tensor_tensor(t, t, w, ALU.mult))
            chain(nc.vector.tensor_scalar(t, t, -0.5, 1.5, ALU.mult, ALU.add))
            chain(nc.vector.tensor_tensor(y, y, t, ALU.mult))

        def chain_of(eng, s):
            n = [0]

            def chain(ins):
                n[0] += 1
                ins.then_inc(s, 1)
                eng.wait_ge(s, n[0])
            return chain

        with ExitStack() as tmp:
            wqkv = tmp.enter_context(nc.sbuf_tensor("wqkv", [P, 3 * P], f32))
            bqkv = tmp.enter_context(nc.sbuf_tensor("bqkv", [P, 3 * P], f32))
            gw = tmp.enter_context(nc.sbuf_tensor("gw", [E, P], f32))
            mrow = tmp.enter_context(nc.sbuf_tensor("mrow", [1, LOW, 256], f32))
            mpad = tmp.enter_context(nc.sbuf_tensor("mpad", [P, PAD, PAD], f32))
            mbox = tmp.enter_context(nc.sbuf_tensor("mbox", [P, PAD, LOW], f32))
            with nc.Block() as block:
                @block.sync
                def _(sp):
                    sp.dma_start(wqkv[:], w_qkv).then_inc(sem("load"), 16)
                    sp.dma_start(bqkv[:], b_qkv.rearrange("(a n) -> a n", a=1).broadcast_to([P, 3 * P])).then_inc(sem("load"), 16)
                    sp.dma_start(gw[:], gate_w).then_inc(sem("load"), 16)
                    sp.dma_start(wp[:], w_proj).then_inc(sem("load"), 16)
                    b3 = b_qkv.rearrange("(p k) -> p k", k=3)
                    with nc.allow_non_contiguous_dma("128 bias values, once"):
                        sp.dma_start(bq[:], b3[:, 0:1]).then_inc(sem("load"), 16)
                        sp.dma_start(bk[:], b3[:, 1:2]).then_inc(sem("load"), 16)
                        sp.dma_start(bp[:], b_proj.rearrange("(p k) -> p k", k=1)).then_inc(sem("load"), 16)
                        sp.dma_start(bg[:], gate_b.rearrange("(p k) -> p k", k=1)).then_inc(sem("load"), 16)
                    sp.dma_start(mrow[:], mask[0:1, 0, :, :].rearrange("a (r s) c -> a r s c", s=8)[:, :, 0, :]).then_inc(sem("load"), 16)

                @block.gpsimd
                def _(pool):
                    chain = chain_of(pool, sem("chain_pool"))
                    chain(nc.gpsimd.memset(ident[:], 0.0))
                    chain(nc.gpsimd.affine_select(out=ident[:], in_=ident[:], compare_op=ALU.not_equal, fill=1.0,
                                                  base=0, pattern=[[-1, P]], channel_multiplier=1))
                    nc.gpsimd.memset(ones[:], 1.0).then_inc(sem("consts"), 1)
                    chain(nc.gpsimd.memset(gmat[:], 1.0 / G))
                    g3 = gmat[:].rearrange("p (g r) -> p g r", r=G)
                    chain(nc.gpsimd.affine_select(out=g3, in_=g3, compare_op=ALU.is_ge, fill=0.0, base=0,
                                                  pattern=[[-G, P // G], [0, G]], channel_multiplier=1))
                    chain(nc.gpsimd.affine_select(out=g3, in_=g3, compare_op=ALU.is_ge, fill=0.0, base=G - 1,
                                                  pattern=[[G, P // G], [0, G]], channel_multiplier=-1))
                    chain(nc.gpsimd.memset(left[:], 1.0))
                    for q in range(ROWS):
                        chain(nc.gpsimd.memset(left[q * LOW:q * LOW + 1, :], 0.0))
                    nc.gpsimd.memset(mpad[:], 0.0).then_inc(sem("consts"), 1)

                @block.tensor
                def _(pe):
                    pe.wait_ge(sem("load"), 9 * 16)
                    pe.wait_ge(sem("consts"), 2)
                    pe.wait_ge(sem("chain_pool"), 6 + ROWS)
                    nc.tensor.transpose(ps[:, 0, 0:E], gw[:], ident[0:E, 0:E]).then_inc(sem("tr"), 1)
                    picked = mrow[:].rearrange("a r (c s) -> a r c s", s=8)[:, :, :, 0]
                    for n in range(2):
                        nc.tensor.matmul(ps[:, 1 + n, :], ones[0:1, :], picked[:, 16 * n:16 * n + 16, :],
                                         start=True, stop=True).then_inc(sem("tr"), 1)

                @block.vector
                def _(dve):
                    chain = chain_of(dve, sem("chain_dve"))
                    dve.wait_ge(sem("load"), 9 * 16)
                    w3 = wqkv[:].rearrange("p (n k) -> p n k", k=3)
                    for k, w in enumerate((wq, wk, wv)):
                        nc.vector.tensor_copy(w[:], w3[:, :, k]).then_inc(sem("ready_a"), 1)
                    nc.vector.tensor_copy(bv[:], bqkv[:].rearrange("p (n k) -> p n k", k=3)[:, :, 2]).then_inc(sem("ready_a"), 1)
                    dve.wait_ge(sem("chain_pool"), 6 + ROWS)
                    nc.vector.stream_shuffle(right[:], left[:], [(j + 1) % LOW for j in range(LOW)]).then_inc(sem("ready_a"), 1)
                    dve.wait_ge(sem("tr"), 3)
                    dve.wait_ge(sem("consts"), 2)
                    nc.vector.tensor_copy(wgT[:], ps[:, 0, 0:E]).then_inc(sem("ready_a"), 1)
                    chain(nc.vector.tensor_copy(mpad[:, 1:1 + LOW, 1:1 + LOW], ps[:, 1:3, :].rearrange("p n (r c) -> p (n r) c", c=LOW)))
                    chain(nc.vector.tensor_tensor(mbox[:], mpad[:, :, 0:LOW], mpad[:, :, 1:1 + LOW], ALU.add))
                    chain(nc.vector.tensor_tensor(mbox[:], mbox[:], mpad[:, :, 2:2 + LOW], ALU.add))
                    by_tile = tile_order(mm[:])
                    chain(nc.vector.tensor_tensor(by_tile, split_rows(mbox[:, 0:LOW, :]), split_rows(mbox[:, 1:1 + LOW, :]), ALU.add))
                    chain(nc.vector.tensor_tensor(by_tile, by_tile, split_rows(mbox[:, 2:2 + LOW, :]), ALU.add))
                    chain(nc.vector.tensor_scalar(mm[:], mm[:], 0.0, None, ALU.is_equal))
        clear_all()
        bound_logits(nc, sem, chain_of, ps, ones, wq, wk, bq, bk, bounded)
        clear_all()

        def ln_tensor(pe):
            for g in range(NC):
                if g >= 4:
                    pe.wait_ge(sem("ln_raw"), g - 3)
                for r in range(4):
                    j = 4 * g + r
                    last = nc.tensor.transpose(ps[:, g % 4, r * P:(r + 1) * P], X[:, j * P:(j + 1) * P], ident[:])
                last.then_inc(sem("ln_tr"), 1)
            return

        def ln_tensor_back(pe, tok):
            for g in range(NC):
                pe.wait_ge(sem("ln_norm"), g + 1)
                if g >= 4:
                    pe.wait_ge(sem("ln_out"), g - 3)
                for r in range(4):
                    last = nc.tensor.transpose(ps[:, 4 + g % 4, r * P:(r + 1) * P], tok[:, 4 * g + r, :], ident[:])
                last.then_inc(sem("ln_back"), 1)

        def ln_scalar(act, tok, wv_, yv_, xnT):
            for g in range(NC):
                act.wait_ge(sem("ln_tr"), g + 1)
                nc.scalar.activation(tok[:, 4 * g:4 * g + 4, :], ps[:, g % 4, :].rearrange("p (r n) -> p r n", n=P),
                                     ACT.Copy).then_inc(sem("ln_raw"), 1)
            act.wait_ge(sem("ln_var"), 1)
            nc.scalar.activation(yv_, wv_, ACT.Ln).then_inc(sem("ln_log"), 1)
            act.wait_ge(sem("ln_log"), 1)
            nc.scalar.activation(yv_, yv_, ACT.Exp, scale=-0.5).then_inc(sem("ln_exp"), 1)
            for g in range(NC):
                act.wait_ge(sem("ln_back"), g + 1)
                nc.scalar.activation(xnT[:, g * BANK:(g + 1) * BANK], ps[:, 4 + g % 4, :], ACT.Copy).then_inc(sem("ln_out"), 1)

        def ln_vector(dve, chain, tok, st, mv, w, y, t):
            for g in range(NC):
                dve.wait_ge(sem("ln_raw"), g + 1)
                for r in range(4):
                    last = nc.vector.bn_stats(st[:, 4 * g + r, :], tok[:, 4 * g + r, :])
            chain(last)
            for j in range(NT):
                last = nc.vector.bn_aggr(mv[:, j, :], st[:, j, :])
            chain(last)
            chain(nc.vector.tensor_scalar(w[:], mv[:, :, 1], LN_EPS, None, ALU.add))
            nc.vector.tensor_copy(t[:], w[:]).then_inc(sem("ln_var"), 1)
            dve.wait_ge(sem("ln_exp"), 1)
            newton_rsqrt(dve, chain, y[:], w[:], t[:])
            for g in range(NC):
                for r in range(4):
                    j = 4 * g + r
                    last = nc.vector.tensor_scalar(tok[:, j, :], tok[:, j, :], mv[:, j, 0:1], y[:, j:j + 1],
                                                   ALU.subtract, ALU.mult)
                last.then_inc(sem("ln_norm"), 1)

        with nc.Fori(0, NIMG) as b:
            contextual_attention(nc, sem, chain_of, newton_rsqrt, b, x, X, ps, ident, ones, gmat, mm, left, right)
            clear_all()
            with ExitStack() as big:
                def sbb(name, shape, dt=f32):
                    return big.enter_context(nc.sbuf_tensor(name, shape, dt))
                xnT = sbb("xnT", [P, TOK + BANK])
                KS = sbb("KS", [3 * D, H, TOK], f32r)
                V = sbb("V", [P, NT, P])
                with ExitStack() as tmp:
                    def sbt(name, shape, dt=f32):
                        return tmp.enter_context(nc.sbuf_tensor(name, shape, dt))
                    tok = sbt("tok", [P, NT, P])
                    st = sbt("st", [P, NT, 6])
                    mv = sbt("mv", [P, NT, 2])
                    w = sbt("w", [P, NT])
                    y = sbt("y", [P, NT])
                    t = sbt("t", [P, NT])
                    khi = sbt("khi", [P, TOK], f32r)
                    klo = sbt("klo", [P, TOK], f32r)
                    with nc.Block() as block:
                        @block.gpsimd
                        def _(pool):
                            nc.gpsimd.memset(xnT[:, TOK:TOK + BANK], 0.0).then_inc(sem("consts"), 1)

                        @block.tensor
                        def _(pe):
                            ln_tensor(pe)
                            ln_tensor_back(pe, tok)
                            for g in range(NC):
                                pe.wait_ge(sem("ln_out"), g + 1)
                                if g >= 2:
                                    pe.wait_ge(sem("free_a"), g - 1)
                                    pe.wait_ge(sem("free_b"), g - 1)
                                nc.tensor.matmul(ps[:, g % 2, :], wk[:], xnT[:, g * BANK:(g + 1) * BANK],
                                                 start=True, stop=True).then_inc(sem("mm_a"), 1)
                                for r in range(4):
                                    j = 4 * g + r
                                    last = nc.tensor.matmul(ps[:, 2 + g % 2, r * P:(r + 1) * P], xnT[:, j * P:(j + 1) * P],
                                                            wv[:], start=True, stop=True)
                                last.then_inc(sem("mm_b"), 1)

                        @block.scalar
                        def _(act):
                            ln_scalar(act, tok, w[:], y[:], xnT)
                            for g in range(NC):
                                act.wait_ge(sem("mm_a"), g + 1)
                                nc.scalar.activation(khi[:, g * BANK:(g + 1) * BANK], ps[:, g % 2, :], ACT.Identity, bias=bk[:]).then_inc(sem("ready_a"), 1)

                        @block.vector
                        def _(dve):
                            chain = chain_of(dve, sem("chain_dve"))
                            ln_vector(dve, chain, tok, st, mv, w, y, t)
                            for g in range(NC):
                                dve.wait_ge(sem("ready_a"), g + 1)
                                nc.vector.scalar_tensor_tensor(klo[:, g * BANK:(g + 1) * BANK], ps[:, g % 2, :], bk[:], khi[:, g * BANK:(g + 1) * BANK].bitcast(f32),
                                                               ALU.add, ALU.subtract).then_inc(sem("free_a"), 1)
                                dve.wait_ge(sem("mm_b"), g + 1)
                                nc.vector.tensor_tensor(V[:, 4 * g:4 * g + 4, :], ps[:, 2 + g % 2, :].rearrange("p (r n) -> p r n", n=P),
                                                        bv[:].rearrange("p (o n) -> p o n", o=1).broadcast_to([P, 4, P]),
                                                        ALU.add).then_inc(sem("free_b"), 1)

                        @block.sync
                        def _(sp):
                            for k in range(2):
                                half = slice(k * (TOK // 2), (k + 1) * (TOK // 2))
                                sp.wait_ge(sem("free_a"), (k + 1) * NC // 2)
                                move_parts(sp, sem("move"), KS[:, :, half], khi[:, half], klo[:, half], (0, 0, 1))
                            sp.wait_ge(sem("move"), 16 * MOVES * 2)
                clear_all()
                flag = nc.values_load(bounded[0:1, 0:1], min_val=0, max_val=P)
                with nc.If(flag >= P):
                    self_attention(nc, sem, X, ps, ones, wq, bq, wp, bp, xnT, KS, V)
                    clear_all()
                with nc.Else():
                    self_attention_with_maximum(nc, sem, clear_all, X, ps, ident, wq, bq, wk, bk, wp, bp, xnT, V)
                    clear_all()

            with ExitStack() as tmp:
                def sbt(name, shape, dt=f32):
                    return tmp.enter_context(nc.sbuf_tensor(name, shape, dt))
                tok = sbt("tok2", [P, NT, P])
                xnT = sbt("xnT2", [P, TOK])
                st = sbt("st2", [P, NT, 6])
                mv = sbt("mv2", [P, NT, 2])
                w = sbt("w2s", [P, NT])
                y = sbt("y2", [P, NT])
                t = sbt("t2", [P, NT])
                logit = sbt("logit", [E, TOK])
                prob = sbt("prob", [E, TOK])
                rest = sbt("rest", [E, TOK])
                top = sbt("top", [E, 8])
                nmax = sbt("nmax", [E, 1])
                zsum = sbt("zsum", [E, 1])
                rz = sbt("rzg", [E, 1])
                selT = sbt("selT", [P, NT, E])
                with nc.Block() as block:
                    @block.sync
                    def _(sp):
                        sp.dma_start(t_d[bass.ds(b, 1)].rearrange("a p n -> (a p) n"), X[:]).then_inc(sem("store"), 16)
                        sp.wait_ge(sem("ready_d"), 1)
                        sp.dma_start(sel_d[bass.ds(b, 1)].rearrange("a p n -> (a p) n"), rest[:]).then_inc(sem("store"), 16)
                        sp.wait_ge(sem("store"), 32)

                    @block.tensor
                    def _(pe):
                        ln_tensor(pe)
                        ln_tensor_back(pe, tok)
                        for g in range(NC):
                            pe.wait_ge(sem("ln_out"), NC if g >= 4 else g + 1)
                            nc.tensor.matmul(ps[0:E, g, :], wgT[:], xnT[:, g * BANK:(g + 1) * BANK],
                                             start=True, stop=True).then_inc(sem("mm_a"), 1)
                        pe.wait_ge(sem("ready_d"), 1)
                        for j in range(NT):
                            last = nc.tensor.transpose(ps[:, j // 8, (j % 8) * E:(j % 8 + 1) * E], rest[:, j * P:(j + 1) * P], ident[0:E, 0:E])
                            if j % 8 == 7:
                                last.then_inc(sem("mm_b"), 1)
                        for j in range(NT):
                            if j % 8 == 0:
                                pe.wait_ge(sem("ready_e"), j // 8 + 1)
                            last = nc.tensor.matmul(ps[:, 4, 0:E], tok[:, j, :], selT[:, j, :], start=(j == 0), stop=(j == NT - 1))
                        last.then_inc(sem("mm_c"), 1)

                    @block.scalar
                    def _(act):
                        ln_scalar(act, tok, w[:], y[:], xnT)
                        for g in range(NC):
                            act.wait_ge(sem("mm_a"), g + 1)
                            nc.scalar.activation(logit[:, g * BANK:(g + 1) * BANK], ps[0:E, g, :], ACT.Identity, bias=bg[:]).then_inc(sem("ready_a"), 1)
                        act.wait_ge(sem("ready_b"), 1)
                        nc.scalar.activation(prob[:], logit[:], ACT.Exp, bias=nmax[:], accum_out=zsum[:]).then_inc(sem("ready_c"), 1)
                        for k in range(4):
                            act.wait_ge(sem("mm_b"), k + 1)
                            nc.scalar.activation(selT[:, 8 * k:8 * k + 8, :], ps[:, k, :].rearrange("p (r n) -> p r n", n=E), ACT.Copy).then_inc(sem("ready_e"), 1)

                    @block.vector
                    def _(dve):
                        chain = chain_of(dve, sem("chain_dve"))
                        ln_vector(dve, chain, tok, st, mv, w, y, t)
                        dve.wait_ge(sem("ready_a"), NC)
                        chain(nc.vector.reduce_max(nmax[:], logit[:], AX.X))
                        nc.vector.tensor_scalar(nmax[:], nmax[:], -1.0, None, ALU.mult).then_inc(sem("ready_b"), 1)
                        dve.wait_ge(sem("ready_c"), 1)
                        chain(nc.vector.reciprocal(rz[:], zsum[:]))
                        chain(nc.vector.tensor_scalar(prob[:], prob[:], rz[:], None, ALU.mult))
                        chain(nc.vector.max(out=top[:], in_=prob[:]))
                        chain(nc.vector.match_replace(out=rest[:], in_to_replace=top[:], in_values=prob[:], imm_value=0.0))
                        nc.vector.tensor_tensor(rest[:], prob[:], rest[:], ALU.subtract).then_inc(sem("ready_d"), 1)
                        dve.wait_ge(sem("mm_c"), 1)
                        nc.vector.tensor_copy(poolT[:, :, bass.ds(b, 1)], ps[:, 4, 0:E].rearrange("p (e o) -> p e o", o=1)).then_inc(sem("ready_f"), 1)
            clear_all()

        experts(nc, sem, ps, ident, poolT, X, t_d, sel_d, w1, w2, out)


def move_parts(sp, moved, stack, high, low, parts):
    for k, part in enumerate(parts):
        for h in range(H):
            src = (high, low)[part][h * D:(h + 1) * D, :].bitcast(f32)
            sp.dma_start(stack[k * D:(k + 1) * D, h, :].bitcast(f32), src).then_inc(moved, 16)


def contextual_attention(nc, sem, chain_of, newton_rsqrt, b, x, X, ps, ident, ones, gmat, mm, left, right):
    with ExitStack() as tmp:
        def sbt(name, shape, dt=f32):
            return tmp.enter_context(nc.sbuf_tensor(name, shape, dt))
        xg = sbt("xg", [P, IMG + 1, IMG])
        low_hi = sbt("low_hi", [P, PAD, PAD], f32r)
        low_lo = sbt("low_lo", [P, PAD, PAD], f32r)
        sq = sbt("sq", [P, PAD, PAD])
        gst = sbt("gst", [P, NC, 6])
        gmv = sbt("gmv", [P, 2])
        ge2 = sbt("ge2", [P, 2])
        gsm = sbt("gsm", [P, 4])
        wgt = sbt("wgt", [P, LOC])
        e = [sbt(f"e{i}", [P, LOC]) for i in range(2)]
        nmx = sbt("nmx", [P, LT])
        zs = sbt("zs", [P, LT])
        rz = sbt("rz0", [P, LT])
        diag = [sbt(f"diag{i}", [P, P]) for i in range(2)]
        stage = [sbt(f"stage{i}", [P, LT, ROWS, PAD]) for i in range(2)]
        shuf = [sbt(f"shuf{i}", [P, PAD * PAD]) for i in range(2)]
        C = [sbt(f"C{i}", [P, LT, PAD, LOW]) for i in range(2)]
        shifted = [[sbt(f"shifted{k}{v}", [P, PAD, LOW], f32r) for v in range(3)] for k in range(2)]
        nextq = [s[:, 0:(PAD - 1) * LOW].rearrange("p (r c) -> p r c", c=LOW) for s in shuf]
        xs = C[1][:].rearrange("p a r c -> p (a r c)")[:, 0:4 * (LT + 1) * P].rearrange("p (a i n) -> p a i n", a=2, i=2)
        XT = sbt("XT", [P, 2, 2, LT + 1, P])
        xv = X[:].rearrange("p (r c) -> p r c", c=IMG)
        NX = 4 * LT + 2

        def xt_index(n):
            if n < 4 * LT:
                return n // (2 * LT), n // LT % 2, n % LT
            return 1, n - 4 * LT, LT

        with nc.Block() as block:
            @block.sync
            def _(sp):
                sp.dma_start(X[:], x[bass.ds(b, 1)].rearrange("a c h w -> (a c) (h w)")).then_inc(sem("load"), 16)

            @block.gpsimd
            def _(pool):
                nc.gpsimd.memset(xg[:, 0, :], 0.0)
                nc.gpsimd.memset(low_hi[:].bitcast(f32), 0.0)
                nc.gpsimd.memset(low_lo[:].bitcast(f32), 0.0)
                nc.gpsimd.memset(sq[:], 0.0)
                for i in range(2):
                    nc.gpsimd.memset(stage[i][:], 0.0)
                for i in range(2):
                    nc.gpsimd.memset(XT[0:P, 1, i, LT, :], 0.0)
                nc.gpsimd.memset(gsm[:, 3:4], 0.0).then_inc(sem("consts"), 1)
                pool.wait_ge(sem("tr"), (NX + 3) // 4)
                for i in range(2):
                    nc.gpsimd.memset(C[i][:, :, 0, :], 0.0)
                    nc.gpsimd.memset(C[i][:, :, PAD - 1, :], 0.0).then_inc(sem("consts"), 1)
                pool.wait_ge(sem("free_d"), 2 * LT)
                for i in range(2):
                    nc.gpsimd.memset(nextq[i][0:LOW], 0.0).then_inc(sem("consts"), 1)

            @block.vector
            def _(dve):
                chain = chain_of(dve, sem("chain_dve"))
                dve.wait_ge(sem("load"), 16)
                for k in range(NC):
                    last = nc.vector.bn_stats(gst[:, k, :], X[:, k * BANK:(k + 1) * BANK])
                chain(last)
                chain(nc.vector.bn_aggr(gmv[:], gst[:]))
                chain(nc.vector.tensor_copy(ge2[:, 0:1], gmv[:, 0:1]))
                nc.vector.scalar_tensor_tensor(ge2[:, 1:2], gmv[:, 0:1], gmv[:, 0:1], gmv[:, 1:2], ALU.mult, ALU.add).then_inc(sem("ready_a"), 1)
                dve.wait_ge(sem("mm_a"), 1)
                m, v, y, t = gmv[:, 0:1], gmv[:, 1:2], gsm[:, 0:1], gsm[:, 1:2]
                chain(nc.vector.tensor_copy(gmv[:], ps[:, 7, 0:2]))
                chain(nc.vector.tensor_tensor(t, m, m, ALU.mult))
                chain(nc.vector.tensor_tensor(v, v, t, ALU.subtract))
                chain(nc.vector.tensor_scalar(v, v, GN_EPS, None, ALU.add))
                nc.vector.tensor_copy(t, v).then_inc(sem("ready_b"), 1)
                dve.wait_ge(sem("ready_c"), 1)
                newton_rsqrt(dve, chain, y, v, t)
                dve.wait_ge(sem("consts"), 1)
                chain(nc.vector.tensor_scalar(xg[:, 1:IMG + 1, :], xv, m, y, ALU.subtract, ALU.mult))
                down = xg[:, 1:IMG + 1:2, 0:IMG:2]
                nc.vector.tensor_tensor(sq[:, 1:1 + LOW, 1:1 + LOW], down, down, ALU.mult).then_inc(sem("ready_d"), 1)
                chain(nc.vector.tensor_copy(low_hi[:, 1:1 + LOW, 1:1 + LOW], down))
                nc.vector.tensor_tensor(low_lo[:, 1:1 + LOW, 1:1 + LOW], down, low_hi[:, 1:1 + LOW, 1:1 + LOW].bitcast(f32),
                                        ALU.subtract).then_inc(sem("ready_e"), 1)
                dve.wait_ge(sem("mm_b"), 1)
                n2 = shuf[0][:, 0:PAD * PAD]
                nc.vector.tensor_copy(n2, ps[:, 4:7, :].rearrange("p a n -> p (a n)")[:, 0:PAD * PAD]).then_inc(sem("ready_f"), 1)
                dve.wait_ge(sem("ready_f"), 1)
                n2 = n2.rearrange("p (r c) -> p r c", c=PAD)
                rows = shuf[1][:, 0:PAD * LOW].rearrange("p (r c) -> p r c", c=LOW)
                chain(nc.vector.tensor_tensor(rows, n2[:, :, 0:LOW], n2[:, :, 1:1 + LOW], ALU.add))
                chain(nc.vector.tensor_tensor(rows, rows, n2[:, :, 2:2 + LOW], ALU.add))
                box = tile_order(e[0][:])
                chain(nc.vector.tensor_tensor(box, split_rows(rows[:, 0:LOW, :]), split_rows(rows[:, 1:1 + LOW, :]), ALU.add))
                chain(nc.vector.tensor_tensor(box, box, split_rows(rows[:, 2:2 + LOW, :]), ALU.add))
                chain(nc.vector.tensor_scalar(e[0][:], e[0][:], PATCH_EPS * PATCH_EPS, None, ALU.max))
                nc.vector.tensor_copy(gsm[:, 2:3], e[0][:, 0:1]).then_inc(sem("ready_g"), 1)
                dve.wait_ge(sem("ready_h"), 1)
                newton_rsqrt(dve, chain, wgt[:], e[0][:], e[1][:])
                chain(nc.vector.scalar_tensor_tensor(wgt[:], wgt[:], SCALE0, mm[:], ALU.mult, ALU.mult))

                def finish(pt):
                    dve.wait_ge(sem("exp_done"), pt + 1)
                    chain(nc.vector.reciprocal(rz[:, pt:pt + 1], zs[:, pt:pt + 1]))
                    if pt >= 2:
                        dve.wait_ge(sem("mm_d"), pt - 1)
                    nc.vector.tensor_scalar(diag[pt % 2][:], ident[:], rz[:, pt:pt + 1], None, ALU.mult)
                    nc.vector.tensor_tensor(e[pt % 2][:], e[pt % 2][:], mm[:], ALU.mult).then_inc(sem("free_b"), 1)

                def fold_columns(pt):
                    dve.wait_ge(sem("free_c"), pt + 1)
                    s = stage[pt % 2]
                    flat = s[:].rearrange("p a r c -> p (a r c)")
                    for i, lanes in enumerate(([max(j - 1, 0) for j in range(LOW)], [min(j + 1, LOW - 1) for j in range(LOW)])):
                        chain(nc.vector.stream_shuffle(shuf[i][:, 0:LT * ROWS * PAD], flat, lanes))
                        sh = shuf[i][:, 0:LT * ROWS * PAD].rearrange("p (a r c) -> p a r c", r=ROWS, c=PAD)
                        keep = (left, right)[i]
                        nc.vector.scalar_tensor_tensor(C[i][:, :, 1 + ROWS * pt:1 + ROWS * pt + ROWS, :], sh[:, :, :, 2 * i:2 * i + LOW],
                                                       keep[:], s[:, :, :, 1:1 + LOW], ALU.mult, ALU.add).then_inc(sem("free_d"), 1)

                for pt in range(LT):
                    dve.wait_ge(sem("mm_c"), pt + 1)
                    if pt >= 2:
                        dve.wait_ge(sem("mm_d"), pt - 1)
                    chain(nc.vector.tensor_tensor_reduce(out=e[pt % 2][:], in0=ps[:, 2 * (pt % 2):2 * (pt % 2) + 2, :].rearrange("p a n -> p (a n)"),
                                                         in1=wgt[:], scale=1.0, scalar=-3.0e38, op0=ALU.mult, op1=ALU.max,
                                                         accum_out=nmx[:, pt:pt + 1]))
                    nc.vector.tensor_scalar(nmx[:, pt:pt + 1], nmx[:, pt:pt + 1], -1.0, None, ALU.mult).then_inc(sem("free_a"), 1)
                    finish(pt)
                    if pt >= 1:
                        fold_columns(pt - 1)
                fold_columns(LT - 1)
                dve.wait_ge(sem("free_d"), 2 * LT)
                dve.wait_ge(sem("scores_done"), 2 * (ROWS - 1))
                dve.wait_ge(sem("consts"), 5)
                dve.wait_ge(sem("misc_pe"), 1)
                for t in range(LT - 1, -1, -1):
                    for i in range(2):
                        if t < LT - 1:
                            dve.wait_ge(sem("sum_dve"), 2 * (LT - 1 - t) + i - 1)
                        above = C[i][:, t - 1, 0:PAD - 1, :] if t else nextq[i][:]
                        nc.vector.tensor_tensor(C[i][:, t, 1:PAD, :], C[i][:, t, 1:PAD, :], above, ALU.add).then_inc(sem("sum_dve"), 1)
                dve.wait_ge(sem("pv_done"), 1)
                for a in range(2):
                    for i in range(2):
                        for n in range(2):
                            half = xv[:, a + LOW * n:LOW * n + LOW:2, i:IMG:2]
                            nc.vector.scalar_tensor_tensor(half, ps[:, 4 * a + 2 * i + n, :].rearrange("p (r c) -> p r c", c=LOW), 0.25, half,
                                                           ALU.mult, ALU.add).then_inc(sem("ready_a"), 1)

            @block.tensor
            def _(pe):
                pe.wait_ge(sem("ready_a"), 1)
                nc.tensor.matmul(ps[:, 7, 0:2], gmat[:], ge2[:], start=True, stop=True).then_inc(sem("mm_a"), 1)
                pe.wait_ge(sem("ready_d"), 1)
                flat = sq[:].rearrange("p r c -> p (r c)")
                for k in range(3):
                    n = min(BANK, PAD * PAD - k * BANK)
                    last = nc.tensor.matmul(ps[:, 4 + k, 0:n], ones[:], flat[:, k * BANK:k * BANK + n], start=True, stop=True)
                last.then_inc(sem("mm_b"), 1)

                def scores(pt):
                    if pt >= 2:
                        pe.wait_ge(sem("free_a"), pt - 1)
                    k = 0
                    for wt, mv in ((0, low_hi), (0, low_lo), (1, low_hi)):
                        for u in range(3):
                            for v in range(3):
                                for n in range(2):
                                    win = mv[:, u:u + LOW, v:v + LOW].rearrange("p (q t) c -> p t q c", t=LT)[:, 4 * n:4 * n + 4]
                                    last = nc.tensor.matmul(ps[:, 2 * (pt % 2) + n, :],
                                                            shifted[wt][v][:, ROWS * pt + u:ROWS * pt + u + ROWS, :].rearrange("p r c -> p (r c)"),
                                                            win, start=(k == 0), stop=(k == 26))
                                k += 1
                    last.then_inc(sem("mm_c"), 1)

                def transpose_exps(pt):
                    pe.wait_ge(sem("free_b"), pt + 1)
                    if pt >= 2:
                        pe.wait_ge(sem("free_c"), pt - 1)
                    for lt in range(LT):
                        k = 4 + 2 * (pt % 2) + lt // 4
                        last = nc.tensor.matmul(ps[:, k, (lt % 4) * P:(lt % 4 + 1) * P], e[pt % 2][:, lt * P:(lt + 1) * P], diag[pt % 2][:], start=True, stop=True)
                    last.then_inc(sem("mm_d"), 1)

                pe.wait_ge(sem("ready_e"), 1)
                pe.wait_ge(sem("ln_norm"), 6)
                scores(0)
                pe.wait_ge(sem("ln_tr"), 4)
                pe.wait_ge(sem("ready_f"), 1)
                for n in range(NX):
                    a, i, t = xt_index(n)
                    if n % 4 == 0 and n >= 16:
                        pe.wait_ge(sem("tr"), n // 4 - 3)
                    last = nc.tensor.transpose(ps[:, 4 + n // 4 % 4, (n % 4) * P:(n % 4 + 1) * P], xs[:, a, i, t * P:(t + 1) * P], ident[:])
                    if n % 4 == 3 or n == NX - 1:
                        last.then_inc(sem("move"), 1)
                scores(1)
                pe.wait_ge(sem("tr"), (NX + 3) // 4)
                for pt in range(LT):
                    transpose_exps(pt)
                    if pt + 2 < LT:
                        scores(pt + 2)
                pe.wait_ge(sem("free_c"), LT)
                pe.wait_ge(sem("free_a"), LT)
                pe.wait_ge(sem("free_d"), 2 * LT)
                for i in range(2):
                    for n in range(2):
                        last = nc.tensor.matmul(ps[:, 4 + 2 * i + n, :], XT[:, 1, i, LT, :], C[i][:, LT - 1, 16 * n + 1:16 * n + 17, :], start=True, stop=False)
                last.then_inc(sem("misc_pe"), 1)
                for t in range(LT - 1, -1, -1):
                    for i in range(2):
                        pe.wait_ge(sem("sum_dve"), 2 * (LT - 1 - t) + i + 1)
                        for a in range(2):
                            for n in range(2):
                                last = nc.tensor.matmul(ps[:, 4 * a + 2 * i + n, :], XT[:, a, i, t, :], C[i][:, t, 16 * n + 1 + a:16 * n + 17 + a, :],
                                                        start=(a == 0 and t == LT - 1), stop=(t == 0))
                last.then_inc(sem("pv_done"), 1)

            @block.scalar
            def _(act):
                act.wait_ge(sem("ready_b"), 1)
                nc.scalar.activation(gsm[:, 0:1], gmv[:, 1:2], ACT.Ln).then_inc(sem("chain_act"), 1)
                act.wait_ge(sem("chain_act"), 1)
                nc.scalar.activation(gsm[:, 0:1], gsm[:, 0:1], ACT.Exp, scale=-0.5).then_inc(sem("ready_c"), 1)
                act.wait_ge(sem("ready_e"), 1)
                for k, part in enumerate((low_hi, low_lo)):
                    for v in range(3):
                        nc.scalar.activation(shifted[k][v][:], part[:, :, v:v + LOW].bitcast(f32), ACT.Copy).then_inc(sem("ln_norm"), 1)
                for a in range(2):
                    tiles = LT + a
                    for i in range(2):
                        dst = xs[:, a, i, 0:tiles * P].rearrange("p (t q c) -> p t q c", q=ROWS, c=LOW)
                        for q in range(ROWS):
                            r0 = 2 * LT * q + 1 - a
                            ins = nc.scalar.activation(dst[:, :, q, :], xg[:, r0:r0 + 2 * tiles - 1:2, i:IMG:2], ACT.Copy)
                        ins.then_inc(sem("ln_tr"), 1)
                act.wait_ge(sem("ready_g"), 1)
                nc.scalar.activation(wgt[:], e[0][:], ACT.Ln).then_inc(sem("chain_act"), 1)
                act.wait_ge(sem("chain_act"), 2)
                nc.scalar.activation(wgt[:], wgt[:], ACT.Exp, scale=-0.5).then_inc(sem("ready_h"), 1)
                act.wait_ge(sem("consts"), 1)
                for k in range((NX + 3) // 4):
                    act.wait_ge(sem("move"), k + 1)
                    a, i, t = xt_index(4 * k)
                    if k < LT:
                        nc.scalar.activation(XT[:, a, i, t:t + 4, :], ps[:, 4 + k % 4, :].rearrange("p (r n) -> p r n", n=P), ACT.Copy).then_inc(sem("tr"), 1)
                    else:
                        q = P - LOW
                        nc.scalar.activation(XT[q:P, 1, :, LT, :], ps[q:P, 4 + k % 4, 0:2 * P].rearrange("p (r n) -> p r n", n=P), ACT.Copy).then_inc(sem("tr"), 1)
                for pt in range(LT + 1):
                    if pt < LT:
                        act.wait_ge(sem("free_a"), pt + 1)
                        nc.scalar.activation(e[pt % 2][:], e[pt % 2][:], ACT.Exp, bias=nmx[:, pt:pt + 1], accum_out=zs[:, pt:pt + 1]).then_inc(sem("exp_done"), 1)
                    if pt >= 1:
                        q = pt - 1
                        act.wait_ge(sem("mm_d"), q + 1)
                        if q >= 2:
                            act.wait_ge(sem("free_d"), 2 * (q - 1))
                        k = 4 + 2 * (q % 2)
                        nc.scalar.activation(stage[q % 2][:, :, :, 1:1 + LOW], ps[:, k:k + 2, :].rearrange("p k (a r c) -> p (k a) r c", r=ROWS, c=LOW),
                                             ACT.Copy).then_inc(sem("free_c"), 1)
                act.wait_ge(sem("free_d"), 2 * LT)
                act.wait_ge(sem("consts"), 3)
                for i in range(2):
                    for q in range(ROWS - 1):
                        nc.scalar.activation(nextq[i][(q + 1) * LOW:(q + 2) * LOW], C[i][q * LOW:(q + 1) * LOW, LT - 1, 0:PAD - 1, :],
                                             ACT.Copy).then_inc(sem("scores_done"), 1)


def bound_logits(nc, sem, chain_of, ps, ones, wq, wk, bq, bk, bounded):
    with ExitStack() as tmp:
        def sbt(name, shape, dt=f32):
            return tmp.enter_context(nc.sbuf_tensor(name, shape, dt))
        same = sbt("same", [P, P])
        gram = sbt("gram", [P, 2, P])
        square = sbt("square", [P, 2, P])
        scratch = sbt("scratch", [P, 2, P])
        rows = sbt("rows", [P, 4])
        norms = sbt("norms", [P, 4])
        roots = sbt("roots", [P, 4])
        length = sbt("length", [P, 2])
        fine = sbt("fine", [P, 5])
        good = sbt("good", [P, 1])
        with nc.Block() as block:
            @block.gpsimd
            def _(pool):
                chain = chain_of(pool, sem("chain_pool"))
                chain(nc.gpsimd.memset(same[:], 1.0))
                s3 = same[:].rearrange("p (h d) -> p h d", d=D)
                chain(nc.gpsimd.affine_select(out=s3, in_=s3, compare_op=ALU.is_ge, fill=0.0, base=0,
                                              pattern=[[-D, H], [0, D]], channel_multiplier=1))
                chain(nc.gpsimd.affine_select(out=s3, in_=s3, compare_op=ALU.is_ge, fill=0.0, base=D - 1,
                                              pattern=[[D, H], [0, D]], channel_multiplier=-1))

            @block.tensor
            def _(pe):
                for k, w in enumerate((wq, wk)):
                    nc.tensor.matmul(ps[:, k, 0:P], w[:], w[:], start=True, stop=True).then_inc(sem("mm_a"), 1)
                for k in range(2):
                    pe.wait_ge(sem("ready_a"), k + 1)
                    nc.tensor.matmul(ps[:, 2 + k, 0:P], gram[:, k, :], gram[:, k, :], start=True, stop=True).then_inc(sem("mm_b"), 1)
                pe.wait_ge(sem("ready_b"), 4)
                nc.tensor.matmul(ps[:, 4, 0:4], same[:], rows[:], start=True, stop=True).then_inc(sem("mm_c"), 1)
                pe.wait_ge(sem("ready_e"), 1)
                nc.tensor.matmul(ps[0:1, 5, 0:1], good[:], ones[:, 0:1], start=True, stop=True).then_inc(sem("mm_d"), 1)

            @block.scalar
            def _(act):
                act.wait_ge(sem("ready_c"), 1)
                nc.scalar.activation(roots[:], norms[:], ACT.Ln).then_inc(sem("chain_act"), 1)
                act.wait_ge(sem("chain_act"), 1)
                nc.scalar.activation(roots[:, 0:2], roots[:, 0:2], ACT.Exp, scale=0.125).then_inc(sem("ready_d"), 1)
                nc.scalar.activation(roots[:, 2:4], roots[:, 2:4], ACT.Exp, scale=0.5).then_inc(sem("ready_d"), 1)

            @block.vector
            def _(dve):
                chain = chain_of(dve, sem("chain_dve"))
                dve.wait_ge(sem("chain_pool"), 3)
                for k in range(2):
                    dve.wait_ge(sem("mm_a"), k + 1)
                    nc.vector.tensor_tensor(gram[:, k, :], ps[:, k, 0:P], same[:], ALU.mult).then_inc(sem("ready_a"), 1)
                for k, bias in enumerate((bq, bk)):
                    nc.vector.tensor_tensor(rows[:, 2 + k:3 + k], bias[:], bias[:], ALU.mult).then_inc(sem("ready_b"), 1)
                for k in range(2):
                    dve.wait_ge(sem("mm_b"), k + 1)
                    chain(nc.vector.tensor_copy(square[:, k, :], ps[:, 2 + k, 0:P]))
                    nc.vector.tensor_tensor_reduce(out=scratch[:, k, :], in0=square[:, k, :], in1=square[:, k, :], scale=1.0, scalar=0.0,
                                                   op0=ALU.mult, op1=ALU.add, accum_out=rows[:, k:k + 1]).then_inc(sem("ready_b"), 1)
                dve.wait_ge(sem("mm_c"), 1)
                chain(nc.vector.tensor_scalar(fine[:, 0:4], ps[:, 4, 0:4], 1.0e18, None, ALU.is_le))
                nc.vector.tensor_scalar(norms[:], ps[:, 4, 0:4], 1.0e-15, 1.0e18, ALU.max, ALU.min).then_inc(sem("ready_c"), 1)
                dve.wait_ge(sem("ready_d"), 2)
                chain(nc.vector.scalar_tensor_tensor(length[:], roots[:, 0:2], float(P) ** 0.5, roots[:, 2:4], ALU.mult, ALU.add))
                chain(nc.vector.tensor_tensor(fine[:, 4:5], length[:, 0:1], length[:, 1:2], ALU.mult))
                chain(nc.vector.tensor_scalar(fine[:, 4:5], fine[:, 4:5], LOGIT_BOUND / SCALE1, None, ALU.is_le))
                nc.vector.tensor_reduce(good[:], fine[:], AX.X, ALU.min).then_inc(sem("ready_e"), 1)
                dve.wait_ge(sem("mm_d"), 1)
                nc.vector.tensor_copy(bounded[:], ps[0:1, 5, 0:1]).then_inc(sem("ready_f"), 1)
                dve.wait_ge(sem("ready_f"), 1)


def self_attention_with_maximum(nc, sem, clear_all, X, ps, ident, wq, bq, wk, bk, wp, bp, xnT, V):
    with ExitStack() as tmp:
        def sbt(name, shape, dt=f32):
            return tmp.enter_context(nc.sbuf_tensor(name, shape, dt))
        kf = sbt("kf", [P, TOK])
        qf = sbt("qf", [P, TOK])
        qt = sbt("qt", [P, P])
        row = sbt("row", [P, TOK])
        pt = sbt("pt", [P, NT, P])
        nmax = sbt("nmaxg", [P, H])
        total = sbt("total", [P, H])
        rtotal = sbt("rtotal", [P, H])
        heads = sbt("heads", [P, P])
        headsT = sbt("headsT", [P, P])
        with nc.Block() as block:
            @block.tensor
            def _(pe):
                for g in range(2 * NC):
                    if g >= 8:
                        pe.wait_ge(sem("free_a"), g // 2 - 3)
                        pe.wait_ge(sem("free_b"), g // 2 - 3)
                    nc.tensor.matmul(ps[:, g % 8, :], (wk, wq)[g % 2][:], xnT[:, g // 2 * BANK:(g // 2 + 1) * BANK],
                                     start=True, stop=True).then_inc(sem("mm_a"), 1)

            @block.scalar
            def _(act):
                for g in range(NC):
                    act.wait_ge(sem("mm_a"), 2 * g + 1)
                    nc.scalar.activation(kf[:, g * BANK:(g + 1) * BANK], ps[:, 2 * g % 8, :], ACT.Identity, bias=bk[:]).then_inc(sem("free_a"), 1)

            @block.vector
            def _(dve):
                for g in range(NC):
                    dve.wait_ge(sem("mm_a"), 2 * g + 2)
                    nc.vector.tensor_scalar(qf[:, g * BANK:(g + 1) * BANK], ps[:, (2 * g + 1) % 8, :], bq[:], None, ALU.add).then_inc(sem("free_b"), 1)
        clear_all()
        with nc.Fori(0, NT) as t:
            with nc.Block() as block:
                @block.tensor
                def _(pe):
                    pe.wait_ge(sem("ready_a"), 1)
                    for h in range(H):
                        rows = slice(h * D, (h + 1) * D)
                        if h:
                            pe.wait_ge(sem("ready_f"), h)
                        for g in range(NC):
                            nc.tensor.matmul(ps[:, g, :], qt[rows, :], kf[rows, g * BANK:(g + 1) * BANK],
                                             start=True, stop=True).then_inc(sem("mm_a"), 1)
                        pe.wait_ge(sem("ready_d"), h + 1)
                        for g in range(NC):
                            for r in range(4):
                                k = 4 * g + r
                                last = nc.tensor.transpose(ps[:, g, r * P:(r + 1) * P], row[:, k * P:(k + 1) * P], ident[:])
                            last.then_inc(sem("mm_b"), 1)
                        pe.wait_ge(sem("ready_e"), NC * (h + 1))
                        for k in range(NT):
                            last = nc.tensor.matmul(ps[:, 0, 0:D], pt[:, k, :], V[:, k, rows], start=(k == 0), stop=(k == NT - 1))
                        last.then_inc(sem("mm_c"), 1)
                    pe.wait_ge(sem("ready_f"), H)
                    nc.tensor.transpose(ps[:, 1, 0:P], heads[:], ident[:]).then_inc(sem("mm_d"), 1)
                    pe.wait_ge(sem("ready_g"), 1)
                    nc.tensor.matmul(ps[:, 2, 0:P], wp[:], headsT[:], start=True, stop=True).then_inc(sem("mm_d"), 1)

                @block.scalar
                def _(act):
                    for h in range(H):
                        if h:
                            act.wait_ge(sem("mm_b"), NC * h)
                        for g in range(NC):
                            act.wait_ge(sem("mm_a"), NC * h + g + 1)
                            nc.scalar.activation(row[:, g * BANK:(g + 1) * BANK], ps[:, g, :], ACT.Copy).then_inc(sem("ready_b"), 1)
                        act.wait_ge(sem("ready_c"), h + 1)
                        nc.scalar.activation(row[:], row[:], ACT.Exp, bias=nmax[:, h:h + 1], scale=SCALE1, accum_out=total[:, h:h + 1]).then_inc(sem("ready_d"), 1)
                    act.wait_ge(sem("mm_d"), 1)
                    nc.scalar.activation(headsT[:], ps[:, 1, 0:P], ACT.Copy).then_inc(sem("ready_g"), 1)

                @block.vector
                def _(dve):
                    nc.vector.tensor_copy(qt[:], qf[:, bass.ds(t * P, P)]).then_inc(sem("ready_a"), 1)
                    for h in range(H):
                        dve.wait_ge(sem("ready_b"), NC * (h + 1))
                        nc.vector.reduce_max(nmax[:, h:h + 1], row[:], AX.X).then_inc(sem("chain_dve"), 1)
                        dve.wait_ge(sem("chain_dve"), 2 * h + 1)
                        nc.vector.tensor_scalar(nmax[:, h:h + 1], nmax[:, h:h + 1], -SCALE1, None, ALU.mult).then_inc(sem("ready_c"), 1)
                        dve.wait_ge(sem("ready_d"), h + 1)
                        nc.vector.reciprocal(rtotal[:, h:h + 1], total[:, h:h + 1]).then_inc(sem("chain_dve"), 1)
                        for g in range(NC):
                            dve.wait_ge(sem("mm_b"), NC * h + g + 1)
                            nc.vector.tensor_copy(pt[:, 4 * g:4 * g + 4, :], ps[:, g, :].rearrange("p (r n) -> p r n", n=P)).then_inc(sem("ready_e"), 1)
                        dve.wait_ge(sem("mm_c"), h + 1)
                        dve.wait_ge(sem("chain_dve"), 2 * h + 2)
                        nc.vector.tensor_scalar(heads[:, h * D:(h + 1) * D], ps[:, 0, 0:D], rtotal[:, h:h + 1], None, ALU.mult).then_inc(sem("ready_f"), 1)
                    dve.wait_ge(sem("mm_d"), 2)
                    xc = X[:, bass.ds(t * P, P)]
                    nc.vector.scalar_tensor_tensor(xc, ps[:, 2, 0:P], bp[:], xc, ALU.add, ALU.add).then_inc(sem("ready_h"), 1)
            clear_all()


def self_attention(nc, sem, X, ps, ones, wq, bq, wp, bp, xnT, KS, V):
    with ExitStack() as tmp:
        def sbt(name, shape, dt=f32):
            return tmp.enter_context(nc.sbuf_tensor(name, shape, dt))
        QS = sbt("QS", [3 * D, 2, H, BANK], f32r)
        qhi = sbt("qhi", [P, BANK], f32r)
        qlo = sbt("qlo", [P, BANK], f32r)
        PR = sbt("PR", [P, PBUFS, H * BANK])
        acc = sbt("acc", [P, 2, H * BANK])
        raw = sbt("raw", [P, BANK])
        rz = sbt("rz", [P, BANK])
        U = 2 * NT
        ND, NP_ = len(DVE_TILES) - 1, len(POOL_TILES) - 1

        def sums_with(tiles, kt):
            return max(tiles.index(kt), 1)


        with nc.Block() as block:
            @block.sync
            def _(sp):
                def stack(c, par):
                    sp.wait_ge(sem("ready_a"), c + 1)
                    move_parts(sp, sem("move"), QS[:, par, :, :], qhi[:], qlo[:], (0, 1, 0))
                stack(0, 0)
                stack(1, 1)
                with sp.Fori(1, NC - 1, 2) as i:
                    stack(i + 1, 0)
                    stack(i + 2, 1)
                stack(NC, 0)
                sp.wait_ge(sem("move"), 16 * MOVES * (NC + 1))

            @block.tensor
            def _(pe):
                def queries(c):
                    nc.tensor.matmul(ps[:, 7, :], wq[:], xnT[:, bass.ds(c * BANK, BANK)], start=True, stop=True).then_inc(sem("misc_pe"), 1)

                def scores(u, par):
                    kt, hp = u // 2, u % 2
                    for h in (2 * hp, 2 * hp + 1):
                        last = nc.tensor.matmul(ps[:, 2 * slot_of(u) + h % 2, :], KS[:, h, kt * P:(kt + 1) * P],
                                                QS[:, par, h, :], start=True, stop=True)
                    last.then_inc(sem("scores_done"), 1)

                def finish(c):
                    pe.wait_ge(sem("ready_a"), c + 2)
                    pe.wait_ge(sem("sum_dve"), (c + 1) * ND)
                    pe.wait_ge(sem("sum_pool"), (c + 1) * NP_)
                    for h in range(H):
                        for k in range(2):
                            last = nc.tensor.matmul(ps[h * D:(h + 1) * D, 7, :], ones[:, 0:D],
                                                    acc[:, k, h * BANK:(h + 1) * BANK], start=(k == 0), stop=(k == 1))
                    last.then_inc(sem("misc_pe"), 1)

                def project(c):
                    pe.wait_ge(sem("ready_b"), c + 1)
                    nc.tensor.matmul(ps[:, 7, :], wp[:], rz[:], start=True, stop=True).then_inc(sem("misc_pe"), 1)

                def block_of(i, par, first):
                    nxt = 1 - par
                    for kt in range(NT):
                        for u in (2 * kt + 2, 2 * kt + 3):
                            if u < U:
                                if u >= 3:
                                    pe.wait_ge(sem("exp_done"), i * U + (U - 2 if u == U - 1 else u - 2))
                                scores(u, par)
                            elif u == U:
                                pe.wait_ge(sem("move"), (i + 2) * (16 * MOVES))
                                scores(0, nxt)
                            else:
                                pe.wait_ge(sem("exp_done"), (i + 1) * U)
                                scores(1, nxt)
                        if kt == 0 and not first:
                            pe.wait_ge(sem("free_a"), i)
                        pe.wait_ge(sem("exp_done"), i * U + (2 * kt + 2))
                        for h in range(H):
                            last = nc.tensor.matmul(ps[h * D:(h + 1) * D, 6, :], V[:, kt, h * D:(h + 1) * D],
                                                    PR[:, kt % PBUFS, h * BANK:(h + 1) * BANK], start=(kt == 0), stop=(kt == NT - 1))
                        last.then_inc(sem("pv_done"), 1)
                        if kt == 1 and not first:
                            finish(i - 1)
                        if kt == 7 and not first:
                            project(i - 1)
                        if kt == 13:
                            if first:
                                pe.wait_ge(sem("ready_a"), 1)
                            else:
                                pe.wait_ge(sem("misc_free"), i)
                            queries(i + 1)

                queries(0)
                pe.wait_ge(sem("move"), 16 * MOVES)
                scores(0, 0)
                scores(1, 0)
                block_of(0, 0, True)
                with pe.Fori(1, NC - 1, 2) as i:
                    block_of(i, 1, False)
                    block_of(i + 1, 0, False)
                block_of(NC - 1, 1, False)
                finish(NC - 1)
                project(NC - 1)

            @block.scalar
            def _(act):
                def block_of(i, first):
                    for kt in range(NT):
                        if kt >= PBUFS:
                            k = kt - PBUFS
                            act.wait_ge(sem("pv_done"), i * NT + (k + 1))
                            if k in DVE_TILES:
                                act.wait_ge(sem("sum_dve"), i * ND + sums_with(DVE_TILES, k))
                            else:
                                act.wait_ge(sem("sum_pool"), i * NP_ + sums_with(POOL_TILES, k))
                        elif not first:
                            act.wait_ge(sem("pv_done"), i * NT - (PBUFS - 1 - kt))
                            act.wait_ge(sem("sum_dve"), i * ND - (PBUFS - 1 - kt))
                        for hp in range(2):
                            u = 2 * kt + hp
                            act.wait_ge(sem("scores_done"), i * U + (u + 1))
                            s = 2 * slot_of(u)
                            nc.scalar.activation(PR[:, kt % PBUFS, hp * PAIR:(hp + 1) * PAIR], ps[:, s:s + 2, :].rearrange("p a n -> p (a n)"),
                                                 ACT.Exp, scale=SCALE1).then_inc(sem("exp_done"), 1)
                block_of(0, True)
                with act.Fori(1, NC) as i:
                    block_of(i, False)

            @block.gpsimd
            def _(pool):
                def block_of(i, first):
                    dst = acc[:, 1, :]
                    for k, kt in enumerate(POOL_TILES):
                        if k >= 1:
                            pool.wait_ge(sem("exp_done"), i * U + (2 * kt + 2))
                        if k == 1:
                            if not first:
                                pool.wait_ge(sem("misc_pe"), 3 * i)
                            nc.gpsimd.tensor_tensor(dst, PR[:, POOL_TILES[0] % PBUFS, :], PR[:, kt % PBUFS, :], ALU.add).then_inc(sem("sum_pool"), 1)
                        elif k > 1:
                            pool.wait_ge(sem("sum_pool"), i * NP_ + (k - 1))
                            nc.gpsimd.tensor_tensor(dst, dst, PR[:, kt % PBUFS, :], ALU.add).then_inc(sem("sum_pool"), 1)
                block_of(0, True)
                with pool.Fori(1, NC) as i:
                    block_of(i, False)

            @block.vector
            def _(dve):
                def queries_low(c):
                    dve.wait_ge(sem("ready_c"), c + 1)
                    nc.vector.scalar_tensor_tensor(qlo[:], ps[:, 7, :], bq[:], qhi[:].bitcast(f32), ALU.add, ALU.subtract).then_inc(sem("ready_a"), 1)

                def finish(i):
                    dve.wait_ge(sem("misc_pe"), 3 * i)
                    nc.vector.reciprocal(rz[:], ps[:, 7, :]).then_inc(sem("ready_d"), 1)
                    dve.wait_ge(sem("ready_d"), i)
                    nc.vector.tensor_tensor(rz[:], rz[:], raw[:], ALU.mult).then_inc(sem("ready_b"), 1)

                def add_out(i):
                    dve.wait_ge(sem("misc_pe"), 3 * i + 1)
                    xc = X[:, bass.ds(i * BANK - BANK, BANK)]
                    nc.vector.scalar_tensor_tensor(xc, ps[:, 7, :], bp[:], xc, ALU.add, ALU.add).then_inc(sem("misc_free"), 1)

                def block_of(i, first):
                    dst = acc[:, 0, :]
                    for kt in range(NT):
                        k = DVE_TILES.index(kt) if kt in DVE_TILES else 0
                        if k >= 1:
                            dve.wait_ge(sem("exp_done"), i * U + (2 * kt + 2))
                        if k == 1:
                            if not first:
                                dve.wait_ge(sem("misc_pe"), 3 * i)
                            nc.vector.tensor_tensor(dst, PR[:, DVE_TILES[0] % PBUFS, :], PR[:, kt % PBUFS, :], ALU.add).then_inc(sem("sum_dve"), 1)
                        elif k > 1:
                            dve.wait_ge(sem("sum_dve"), i * ND + (k - 1))
                            nc.vector.tensor_tensor(dst, dst, PR[:, kt % PBUFS, :], ALU.add).then_inc(sem("sum_dve"), 1)
                        if kt == 4 and not first:
                            finish(i)
                        if kt == 8 and not first:
                            add_out(i)
                        if kt == 15:
                            dve.wait_ge(sem("misc_pe"), 3 * i + 2)
                            dve.wait_ge(sem("move"), (i + 1) * (16 * MOVES))
                            nc.vector.tensor_scalar(qhi[:], ps[:, 7, :], bq[:], None, ALU.add).then_inc(sem("ready_c"), 1)
                        if kt == 16:
                            queries_low(i + 1)
                    dve.wait_ge(sem("pv_done"), (i + 1) * NT)
                    nc.vector.tensor_copy(raw[:], ps[:, 6, :]).then_inc(sem("free_a"), 1)

                dve.wait_ge(sem("misc_pe"), 1)
                nc.vector.tensor_scalar(qhi[:], ps[:, 7, :], bq[:], None, ALU.add).then_inc(sem("ready_c"), 1)
                queries_low(0)
                block_of(0, True)
                with dve.Fori(1, NC) as i:
                    block_of(i, False)
                finish(NC)
                add_out(NC)


def experts(nc, sem, ps, ident, poolT, X, t_d, sel_d, w1, w2, out):
    with ExitStack() as tmp:
        def sbt(name, shape, dt=f32):
            return tmp.enter_context(nc.sbuf_tensor(name, shape, dt))
        W1 = sbt("W1", [P, WBUFS, EG, HID])
        W2 = sbt("W2", [P, WBUFS, EG, HC, P])
        B1 = sbt("B1", [E, HID])
        B2 = sbt("B2", [E, P])
        pick = sbt("pick", [E, E, LANES])
        pooled = sbt("pooled", [P, E, LANES])
        hid = sbt("hid", [P, 2, HID])
        hidT = sbt("hidT", [P, 2, HC, P])
        res = sbt("res", [P, 2, P])
        outT = sbt("outT", [P, NIMG, E])
        outE = sbt("outE", [P, NIMG // 2, P])
        tin = sbt("tin", [P, NIMG - 1, TOK])
        sin = sbt("sin", [P, NIMG // 2, TOK])
        w1_in = [sem(f"w1_in{k}") for k in range(WBUFS)]
        w2_in = [sem(f"w2_in{k}") for k in range(WBUFS)]
        tok_in = [sem(f"tok_in{b}") for b in range(NIMG)]
        images = [tin[:, b] for b in range(NIMG - 1)] + [X[:]]
        with nc.Block() as block:
            @block.sync
            def _(sp):
                sp.dma_start(B1[:], w1[:, P, :]).then_inc(sem("bias_in"), 16)
                sp.dma_start(B2[:], w2[:, HID, :]).then_inc(sem("bias_in"), 16)
                for g in range(NEG):
                    if g >= WBUFS:
                        sp.wait_ge(sem("first_done"), g - WBUFS + 1)
                    es = slice(g * EG, (g + 1) * EG)
                    sp.dma_start(W1[:, g % WBUFS], w1[es, 0:P, :].rearrange("e d h -> d e h")).then_inc(w1_in[g % WBUFS], 16)
                for b in range(NIMG):
                    sp.dma_start(sin[E * (b % 2):E * (b % 2) + E, b // 2], sel_d[b]).then_inc(tok_in[b], 16)
                    if b < NIMG - 1:
                        sp.dma_start(tin[:, b], t_d[b]).then_inc(tok_in[b], 16)

            @block.gpsimd
            def _(pool):
                for g in range(NEG):
                    if g >= WBUFS:
                        pool.wait_ge(sem("second_done"), g - WBUFS + 1)
                    es = slice(g * EG, (g + 1) * EG)
                    pool.dma_start(W2[:, g % WBUFS], w2[es, 0:HID, :].rearrange("e (p c) o -> p e c o", c=HC)).then_inc(w2_in[g % WBUFS], 16)

            @block.tensor
            def _(pe):
                def first(g):
                    pe.wait_ge(w1_in[g % WBUFS], 16 * (g // WBUFS + 1))
                    if g >= 2:
                        pe.wait_ge(sem("gelu_done"), g - 1)
                    nc.tensor.matmul(ps[:, g % 2, :], pick[:, g * EG:(g + 1) * EG, :].rearrange("p e l -> p (e l)"), B1[:],
                                     start=True, stop=False)
                    for j in range(EG):
                        last = nc.tensor.matmul(ps[j * LANES:(j + 1) * LANES, g % 2, :], pooled[:, g * EG + j, :],
                                                W1[:, g % WBUFS, j, :], start=False, stop=True)
                    last.then_inc(sem("first_done"), 1)

                def turn(g):
                    pe.wait_ge(sem("gelu_done"), g + 1)
                    if g >= 2:
                        pe.wait_ge(sem("turned_out"), g - 1)
                    for c in range(HC):
                        last = nc.tensor.transpose(ps[:, 2 + g % 2, c * P:(c + 1) * P],
                                                   hid[:, g % 2, :].rearrange("p (m c) -> p m c", c=HC)[:, :, c], ident[:])
                    last.then_inc(sem("turned"), 1)

                def second(g):
                    pe.wait_ge(w2_in[g % WBUFS], 16 * (g // WBUFS + 1))
                    pe.wait_ge(sem("turned_out"), g + 1)
                    if g >= 2:
                        pe.wait_ge(sem("result_out"), g - 1)
                    nc.tensor.matmul(ps[:, 4 + g % 2, 0:P], pick[:, g * EG:(g + 1) * EG, :].rearrange("p e l -> p (e l)"), B2[:],
                                     start=True, stop=False)
                    for j in range(EG):
                        for c in range(HC):
                            last = nc.tensor.matmul(ps[j * LANES:(j + 1) * LANES, 4 + g % 2, 0:P],
                                                    hidT[:, g % 2, c, j * LANES:(j + 1) * LANES],
                                                    W2[:, g % WBUFS, j, c, :], start=False, stop=(c == HC - 1))
                    last.then_inc(sem("second_done"), 1)

                def turn_result(g):
                    pe.wait_ge(sem("result_out"), g + 1)
                    if g >= 2:
                        pe.wait_ge(sem("result_kept"), g - 1)
                    nc.tensor.transpose(ps[:, 6 + g % 2, 0:P], res[:, g % 2, :], ident[:]).then_inc(sem("result_turned"), 1)

                pe.wait_ge(sem("bias_in"), 32)
                pe.wait_ge(sem("lanes_ready"), 2)
                for g in range(NEG + 3):
                    if g < NEG:
                        first(g)
                    if 1 <= g <= NEG:
                        turn(g - 1)
                    if 2 <= g <= NEG + 1:
                        second(g - 2)
                    if g >= 3:
                        turn_result(g - 3)
                pe.wait_ge(sem("result_kept"), NEG)
                for a in range(NIMG // 2):
                    last = nc.tensor.transpose(ps[:, 0, a * P:(a + 1) * P], outT[:, 2 * a:2 * a + 2, :].rearrange("p b e -> p (b e)"), ident[:])
                last.then_inc(sem("outputs_turned"), 1)
                pe.wait_ge(sem("outputs_ready"), 1)
                for b in range(NIMG):
                    half = slice(E * (b % 2), E * (b % 2) + E)
                    pe.wait_ge(tok_in[b], 32 if b < NIMG - 1 else 16)
                    for c in range(NC):
                        n = b * NC + c
                        if n >= 4:
                            pe.wait_ge(sem("added"), n - 3)
                        nc.tensor.matmul(ps[:, 4 + n % 4, :], outE[half, b // 2, :], sin[half, b // 2, c * BANK:(c + 1) * BANK],
                                         start=True, stop=True).then_inc(sem("spread"), 1)

            @block.scalar
            def _(act):
                for g in range(NEG):
                    act.wait_ge(sem("first_done"), g + 1)
                    if g >= 2:
                        act.wait_ge(sem("turned"), g - 1)
                    nc.scalar.activation(hid[:, g % 2, :], ps[:, g % 2, :], ACT.Gelu).then_inc(sem("gelu_done"), 1)
                for b in range(NIMG):
                    act.wait_ge(sem("added"), (b + 1) * NC)
                    act.dma_start(out[b].rearrange("c h w -> c (h w)"), images[b]).then_inc(sem("out_stored"), 16)
                act.wait_ge(sem("out_stored"), 16 * NIMG)

            @block.vector
            def _(dve):
                nc.vector.memset(pooled[:], 0.0).then_inc(sem("pooled_zero"), 1)
                nc.vector.tensor_copy(pick[:], ident[0:E, 0:E].rearrange("p (e o) -> p e o", o=1).broadcast_to([E, E, LANES])).then_inc(sem("lanes_ready"), 1)
                dve.wait_ge(sem("pooled_zero"), 1)
                nc.vector.tensor_copy(pooled[:, :, 0:NIMG], poolT[:]).then_inc(sem("lanes_ready"), 1)
                for g in range(NEG + 2):
                    if g < NEG:
                        dve.wait_ge(sem("turned"), g + 1)
                        if g >= 2:
                            dve.wait_ge(sem("second_done"), g - 1)
                        nc.vector.tensor_copy(hidT[:, g % 2], ps[:, 2 + g % 2, :].rearrange("p (c n) -> p c n", n=P)).then_inc(sem("turned_out"), 1)
                    if 1 <= g <= NEG:
                        dve.wait_ge(sem("second_done"), g)
                        if g >= 3:
                            dve.wait_ge(sem("result_turned"), g - 2)
                        nc.vector.tensor_copy(res[:, (g - 1) % 2, :], ps[:, 4 + (g - 1) % 2, 0:P]).then_inc(sem("result_out"), 1)
                    if g >= 2:
                        k = g - 2
                        dve.wait_ge(sem("result_turned"), k + 1)
                        nc.vector.tensor_copy(outT[:, :, k * EG:(k + 1) * EG].rearrange("p b e -> p e b"),
                                              ps[:, 6 + k % 2, 0:P].rearrange("p (e l) -> p e l", l=LANES)[:, :, 0:NIMG]).then_inc(sem("result_kept"), 1)
                dve.wait_ge(sem("outputs_turned"), 1)
                nc.vector.tensor_copy(outE[:], ps[:, 0, 0:NIMG // 2 * P].rearrange("e (b n) -> e b n", n=P)).then_inc(sem("outputs_ready"), 1)
                for b in range(NIMG):
                    for c in range(NC):
                        dve.wait_ge(sem("spread"), b * NC + c + 1)
                        tc = images[b][:, c * BANK:(c + 1) * BANK]
                        nc.vector.tensor_tensor(tc, ps[:, 4 + (b * NC + c) % 4, :], tc, ALU.add).then_inc(sem("added"), 1)


_INS = ['x', 'L0_conv_mask', 'L1_attn_W_qkv', 'L1_attn_b_qkv', 'L1_attn_W_proj', 'L1_attn_b_proj', 'L1_ffn_gate_w',
        'L1_ffn_gate_b', 'L1_ffn_weight1', 'L1_ffn_weight2']
_OUTS = [((4, 128, 64, 64), 'float32')]


def kernel(**inputs):
    import numpy as _np
    import concourse.bacc as _bacc
    from concourse import mybir as _mybir
    from concourse.bass_utils import run_bass_kernel_spmd as _run

    nc = _bacc.Bacc("TRN2", target_bir_lowering=False, num_devices=1)
    arrays, args = {}, []
    for name in _INS:
        a = _np.ascontiguousarray(inputs[name])
        arrays[f"in_{name}_dram"] = a
        args.append(nc.dram_tensor(f"in_{name}_dram", a.shape, _mybir.dt.from_np(a.dtype), kind="ExternalInput").ap())
    for i, (shape, dtype) in enumerate(_OUTS):
        dt = _mybir.dt.from_np(_np.dtype(dtype))
        args.append(nc.dram_tensor(f"out_{i}_dram", shape, dt, kind="ExternalOutput").ap())
    build(nc, *args)
    r = _run(nc, [arrays], core_ids=[0])
    got = tuple(r.results[0][f"out_{i}_dram"] for i in range(len(_OUTS)))
    return got[0]
```

```python
import concourse.bass as bass
from concourse import mybir
from contextlib import ExitStack

f32 = mybir.dt.float32
f32r = mybir.dt.float32r
ALU = mybir.AluOpType
ACT = mybir.ActivationFunctionType
AX = mybir.AxisListType

P = 128
NIMG = 4
IMG = 64
TOK = IMG * IMG
NT = TOK // P
BANK = 512
NC = TOK // BANK
H = 4
D = 32
G = 4
LOW = 32
LOC = LOW * LOW
PAD = LOW + 2
LT = LOC // P
ROWS = P // LOW
E = 64
HID = 512
HC = HID // P
GN_EPS, LN_EPS, PATCH_EPS = 1e-5, 1e-5, 1e-4
SCALE0 = 10.0
SCALE1 = float(P) ** -0.5
MOVES = 3 * H
PBUFS = 4
PAIR = 2 * BANK
POOL_TILES = (2, 3, 6, 9, 12, 15, 18, 21, 24, 27, 30)
DVE_TILES = tuple(t for t in range(NT) if t not in POOL_TILES)
LOGIT_BOUND = 64.0
EG = 4
NEG = E // EG
WBUFS = 4
LANES = P // EG


def slot_of(u):
    return 1 if u == 2 * NT - 1 else u % 3


def split_rows(ap):
    return ap.rearrange("p (q t) c -> p q t c", t=LT)


def tile_order(ap):
    return ap.rearrange("p (t q c) -> p q t c", q=ROWS, c=LOW)


def build(nc, x, mask, w_qkv, b_qkv, w_proj, b_proj, gate_w, gate_b, w1, w2, out):
    ctx = ExitStack()
    sems = {}

    def sem(name):
        if name not in sems:
            sems[name] = ctx.enter_context(nc.semaphore(name))
        return sems[name]

    def clear_all():
        nums = [s.num for s in sems.values()]
        nc.all_engine_barrier(sems_to_clear=range(min(nums), max(nums) + 1))

    with ctx:
        def sb(name, shape, dt=f32):
            return ctx.enter_context(nc.sbuf_tensor(name, shape, dt))

        for n in ("load", "consts", "chain_pool", "chain_dve", "chain_act", "tr", "ready_a", "ready_b", "ready_c",
                  "ready_d", "ready_e", "ready_f", "ready_g", "ready_h", "store", "mm_a", "mm_b", "mm_c", "mm_d",
                  "free_a", "free_b", "exp_done", "scores_done", "pv_done", "sum_dve", "sum_pool", "move", "ln_tr",
                  "ln_raw", "ln_var", "ln_root", "ln_norm", "ln_back", "ln_out", "logits_out", "top_ready",
                  "probs_ready", "selected", "selected_pool", "scaled", "query_ready", "query_high", "query_split",
                  "key_ready", "key_high", "key_split", "value_ready", "value_out", "turned_sel", "kept_sel",
                  "pooled_done", "pooled_kept", "columns_folded", "diag_ready", "exps_turned", "gram_kept",
                  "masked", "moved_on", "parity_ready", "pasted", "rows_folded", "scores_ready", "scores_scaled",
                  "shifted_ready", "source_kept", "source_turned", "turned_out", "unfolded_used", "added",
                  "bank7_written", "bias_in", "canvas_added", "channel_stats", "first_done", "gelu_done",
                  "group_stats", "heads_normed", "lanes_ready", "logits_ready", "norms_ready", "norms_rooted",
                  "out_stored", "outputs_ready", "outputs_turned", "parts_ready", "projection_added",
                  "queries_high", "queries_split", "result_kept", "result_out", "result_turned", "root_ready",
                  "second_done", "spread", "squares_read", "squares_ready", "squares_summed", "sums_inverted",
                  "turned", "variance_ready", "weighted_out", "zeroed"):
            sem(n)

        t_d = nc.dram_tensor("t_scratch", [NIMG, P, TOK], f32, kind="Internal").ap()
        sel_d = nc.dram_tensor("sel_scratch", [NIMG, E, TOK], f32, kind="Internal").ap()

        ps = ctx.enter_context(nc.psum_tensor("ps", [P, 8, BANK], f32))
        ident = sb("ident", [P, P])
        ones = sb("ones", [P, P])
        gmat = sb("gmat", [P, P])
        wq = sb("wq", [P, P])
        wk = sb("wk", [P, P])
        wv = sb("wv", [P, P])
        wp = sb("wp", [P, P])
        wgT = sb("wgT", [P, E])
        bq = sb("bq", [P, 1])
        bk = sb("bk", [P, 1])
        bp = sb("bp", [P, 1])
        bg = sb("bg", [E, 1])
        bv = sb("bv", [P, P])
        mm = sb("mm", [P, LOC])
        left = sb("left", [P, 1])
        right = sb("right", [P, 1])
        poolT = sb("poolT", [P, E, NIMG])
        bounded = sb("bounded", [1, 1], mybir.dt.int32)
        X = sb("X", [P, TOK])

        def newton_rsqrt(dve, chain, y, w, t):
            chain(nc.vector.tensor_tensor(t, y, y, ALU.mult))
            chain(nc.vector.tensor_tensor(t, t, w, ALU.mult))
            chain(nc.vector.tensor_scalar(t, t, -0.5, 1.5, ALU.mult, ALU.add))
            chain(nc.vector.tensor_tensor(y, y, t, ALU.mult))

        def chain_of(eng, s):
            n = [0]

            def chain(ins):
                n[0] += 1
                ins.then_inc(s, 1)
                eng.wait_ge(s, n[0])
            return chain

        with ExitStack() as tmp:
            wqkv = tmp.enter_context(nc.sbuf_tensor("wqkv", [P, 3 * P], f32))
            bqkv = tmp.enter_context(nc.sbuf_tensor("bqkv", [P, 3 * P], f32))
            gw = tmp.enter_context(nc.sbuf_tensor("gw", [E, P], f32))
            mrow = tmp.enter_context(nc.sbuf_tensor("mrow", [1, LOW, 256], f32))
            mpad = tmp.enter_context(nc.sbuf_tensor("mpad", [P, PAD, PAD], f32))
            mbox = tmp.enter_context(nc.sbuf_tensor("mbox", [P, PAD, LOW], f32))
            with nc.Block() as block:
                @block.sync
                def _(sp):
                    sp.dma_start(wqkv[:], w_qkv).then_inc(sem("load"), 16)
                    sp.dma_start(bqkv[:], b_qkv.rearrange("(a n) -> a n", a=1).broadcast_to([P, 3 * P])).then_inc(sem("load"), 16)
                    sp.dma_start(gw[:], gate_w).then_inc(sem("load"), 16)
                    sp.dma_start(wp[:], w_proj).then_inc(sem("load"), 16)
                    b3 = b_qkv.rearrange("(p k) -> p k", k=3)
                    with nc.allow_non_contiguous_dma("128 bias values, once"):
                        sp.dma_start(bq[:], b3[:, 0:1]).then_inc(sem("load"), 16)
                        sp.dma_start(bk[:], b3[:, 1:2]).then_inc(sem("load"), 16)
                        sp.dma_start(bp[:], b_proj.rearrange("(p k) -> p k", k=1)).then_inc(sem("load"), 16)
                        sp.dma_start(bg[:], gate_b.rearrange("(p k) -> p k", k=1)).then_inc(sem("load"), 16)
                    sp.dma_start(mrow[:], mask[0:1, 0, :, :].rearrange("a (r s) c -> a r s c", s=8)[:, :, 0, :]).then_inc(sem("load"), 16)

                @block.gpsimd
                def _(pool):
                    chain = chain_of(pool, sem("chain_pool"))
                    chain(nc.gpsimd.memset(ident[:], 0.0))
                    chain(nc.gpsimd.affine_select(out=ident[:], in_=ident[:], compare_op=ALU.not_equal, fill=1.0,
                                                  base=0, pattern=[[-1, P]], channel_multiplier=1))
                    nc.gpsimd.memset(ones[:], 1.0).then_inc(sem("consts"), 1)
                    chain(nc.gpsimd.memset(gmat[:], 1.0 / G))
                    g3 = gmat[:].rearrange("p (g r) -> p g r", r=G)
                    chain(nc.gpsimd.affine_select(out=g3, in_=g3, compare_op=ALU.is_ge, fill=0.0, base=0,
                                                  pattern=[[-G, P // G], [0, G]], channel_multiplier=1))
                    chain(nc.gpsimd.affine_select(out=g3, in_=g3, compare_op=ALU.is_ge, fill=0.0, base=G - 1,
                                                  pattern=[[G, P // G], [0, G]], channel_multiplier=-1))
                    chain(nc.gpsimd.memset(left[:], 1.0))
                    for q in range(ROWS):
                        chain(nc.gpsimd.memset(left[q * LOW:q * LOW + 1, :], 0.0))
                    nc.gpsimd.memset(mpad[:], 0.0).then_inc(sem("consts"), 1)

                @block.tensor
                def _(pe):
                    pe.wait_ge(sem("load"), 9 * 16)
                    pe.wait_ge(sem("consts"), 2)
                    pe.wait_ge(sem("chain_pool"), 6 + ROWS)
                    nc.tensor.transpose(ps[:, 0, 0:E], gw[:], ident[0:E, 0:E]).then_inc(sem("tr"), 1)
                    picked = mrow[:].rearrange("a r (c s) -> a r c s", s=8)[:, :, :, 0]
                    for n in range(2):
                        nc.tensor.matmul(ps[:, 1 + n, :], ones[0:1, :], picked[:, 16 * n:16 * n + 16, :],
                                         start=True, stop=True).then_inc(sem("tr"), 1)

                @block.vector
                def _(dve):
                    chain = chain_of(dve, sem("chain_dve"))
                    dve.wait_ge(sem("load"), 9 * 16)
                    w3 = wqkv[:].rearrange("p (n k) -> p n k", k=3)
                    for k, w in enumerate((wq, wk, wv)):
                        nc.vector.tensor_copy(w[:], w3[:, :, k]).then_inc(sem("ready_a"), 1)
                    nc.vector.tensor_copy(bv[:], bqkv[:].rearrange("p (n k) -> p n k", k=3)[:, :, 2]).then_inc(sem("ready_a"), 1)
                    dve.wait_ge(sem("chain_pool"), 6 + ROWS)
                    nc.vector.stream_shuffle(right[:], left[:], [(j + 1) % LOW for j in range(LOW)]).then_inc(sem("ready_a"), 1)
                    dve.wait_ge(sem("tr"), 3)
                    dve.wait_ge(sem("consts"), 2)
                    nc.vector.tensor_copy(wgT[:], ps[:, 0, 0:E]).then_inc(sem("ready_a"), 1)
                    chain(nc.vector.tensor_copy(mpad[:, 1:1 + LOW, 1:1 + LOW], ps[:, 1:3, :].rearrange("p n (r c) -> p (n r) c", c=LOW)))
                    chain(nc.vector.tensor_tensor(mbox[:], mpad[:, :, 0:LOW], mpad[:, :, 1:1 + LOW], ALU.add))
                    chain(nc.vector.tensor_tensor(mbox[:], mbox[:], mpad[:, :, 2:2 + LOW], ALU.add))
                    by_tile = tile_order(mm[:])
                    chain(nc.vector.tensor_tensor(by_tile, split_rows(mbox[:, 0:LOW, :]), split_rows(mbox[:, 1:1 + LOW, :]), ALU.add))
                    chain(nc.vector.tensor_tensor(by_tile, by_tile, split_rows(mbox[:, 2:2 + LOW, :]), ALU.add))
                    chain(nc.vector.tensor_scalar(mm[:], mm[:], 0.0, None, ALU.is_equal))
        clear_all()
        bound_logits(nc, sem, chain_of, ps, ones, wq, wk, bq, bk, bounded)
        clear_all()

        def ln_tensor(pe):
            for g in range(NC):
                if g >= 4:
                    pe.wait_ge(sem("ln_raw"), g - 3)
                for r in range(4):
                    j = 4 * g + r
                    last = nc.tensor.transpose(ps[:, g % 4, r * P:(r + 1) * P], X[:, j * P:(j + 1) * P], ident[:])
                last.then_inc(sem("ln_tr"), 1)
            return


        def ln_tensor_back(pe, tok, then=None):
            for g in range(NC):
                pe.wait_ge(sem("ln_norm"), g + 1)
                if g >= 4:
                    pe.wait_ge(sem("ln_out"), g - 3)
                for r in range(4):
                    last = nc.tensor.transpose(ps[:, 4 + g % 4, r * P:(r + 1) * P], tok[:, 4 * g + r, :], ident[:])
                last.then_inc(sem("ln_back"), 1)
                if then:
                    then(g)

        def ln_scalar(act, tok, wv_, yv_, xnT, then=None):
            for g in range(NC):
                act.wait_ge(sem("ln_tr"), g + 1)
                nc.scalar.activation(tok[:, 4 * g:4 * g + 4, :], ps[:, g % 4, :].rearrange("p (r n) -> p r n", n=P),
                                     ACT.Copy).then_inc(sem("ln_raw"), 1)
            act.wait_ge(sem("ln_var"), 1)
            nc.scalar.activation(yv_, wv_, ACT.Sqrt).then_inc(sem("ln_root"), 1)
            for g in range(NC):
                act.wait_ge(sem("ln_back"), g + 1)
                nc.scalar.activation(xnT[:, g * BANK:(g + 1) * BANK], ps[:, 4 + g % 4, :], ACT.Copy).then_inc(sem("ln_out"), 1)
                if then:
                    then(g)

        def ln_vector(dve, chain, tok, st, mv, w, y, t, then=None):
            for g in range(NC):
                dve.wait_ge(sem("ln_raw"), g + 1)
                for r in range(4):
                    last = nc.vector.bn_stats(st[:, 4 * g + r, :], tok[:, 4 * g + r, :])
            chain(last)
            for j in range(NT):
                last = nc.vector.bn_aggr(mv[:, j, :], st[:, j, :])
            chain(last)
            nc.vector.tensor_scalar(w[:], mv[:, :, 1], LN_EPS, None, ALU.add).then_inc(sem("ln_var"), 1)
            dve.wait_ge(sem("ln_root"), 1)
            chain(nc.vector.reciprocal(y[:], y[:]))
            newton_rsqrt(dve, chain, y[:], w[:], t[:])
            for g in range(NC):
                for j in range(4 * g, 4 * g + 4):
                    last = nc.vector.tensor_scalar(tok[:, j, :], tok[:, j, :], mv[:, j, 0:1], y[:, j:j + 1],
                                                   ALU.subtract, ALU.mult)
                last.then_inc(sem("ln_norm"), 1)
                if then:
                    then(g)

        with nc.Fori(0, NIMG) as b:
            contextual_attention(nc, sem, chain_of, newton_rsqrt, b, x, X, ps, ident, ones, gmat, mm, left, right)
            clear_all()
            with ExitStack() as big:
                def sbb(name, shape, dt=f32):
                    return big.enter_context(nc.sbuf_tensor(name, shape, dt))
                xnT = sbb("xnT", [P, TOK + BANK])
                KS = sbb("KS", [3 * D, H, TOK], f32r)
                V = sbb("V", [P, NT, P])
                QS0 = sbb("QS0", [3 * D, H, BANK], f32r)
                with ExitStack() as tmp:
                    def sbt(name, shape, dt=f32):
                        return tmp.enter_context(nc.sbuf_tensor(name, shape, dt))
                    tok = sbt("tok", [P, NT, P])
                    st = sbt("st", [P, NT, 6])
                    mv = sbt("mv", [P, NT, 2])
                    w = sbt("w", [P, NT])
                    y = sbt("y", [P, NT])
                    t = sbt("t", [P, NT])
                    qhi = sbt("qhi0", [P, BANK], f32r)
                    qlo = sbt("qlo0", [P, BANK], f32r)
                    khi = sbt("khi", [P, TOK], f32r)
                    klo = sbt("klo", [P, TOK], f32r)
                    by_act = tuple((0, h) for h in range(H))
                    by_dve = ((2, 0), (2, 1))
                    late = slice(TOK // 2, TOK)
                    with nc.Block() as block:
                        @block.tensor
                        def _(pe):
                            def keys(g):
                                pe.wait_ge(sem("ln_out"), g + 1)
                                if g == 0:
                                    nc.tensor.matmul(ps[:, 2, :], wq[:], xnT[:, 0:BANK], start=True, stop=True).then_inc(sem("query_ready"), 1)
                                if g >= 2:
                                    pe.wait_ge(sem("key_split"), g - 1)
                                nc.tensor.matmul(ps[:, g % 2, :], wk[:], xnT[:, g * BANK:(g + 1) * BANK],
                                                 start=True, stop=True).then_inc(sem("key_ready"), 1)

                            ln_tensor(pe)
                            ln_tensor_back(pe, tok, lambda g: keys(g - 1) if g else None)
                            keys(NC - 1)
                            pe.wait_ge(sem("query_split"), 1)
                            for g in range(NC):
                                if g >= 2:
                                    pe.wait_ge(sem("value_out"), g - 1)
                                for r in range(4):
                                    j = 4 * g + r
                                    last = nc.tensor.matmul(ps[:, 2 + g % 2, r * P:(r + 1) * P], xnT[:, j * P:(j + 1) * P],
                                                            wv[:], start=True, stop=True)
                                last.then_inc(sem("value_ready"), 1)

                        @block.scalar
                        def _(act):
                            def key_high(g):
                                if g == 0:
                                    act.wait_ge(sem("query_ready"), 1)
                                    nc.scalar.activation(qhi[:], ps[:, 2, :], ACT.Identity, bias=bq[:]).then_inc(sem("query_high"), 1)
                                act.wait_ge(sem("key_ready"), g + 1)
                                nc.scalar.activation(khi[:, g * BANK:(g + 1) * BANK], ps[:, g % 2, :], ACT.Identity, bias=bk[:]).then_inc(sem("key_high"), 1)

                            ln_scalar(act, tok, w[:], y[:], xnT, lambda g: key_high(g - 1) if g else None)
                            key_high(NC - 1)
                            act.wait_ge(sem("key_high"), NC)
                            for k, h in by_act:
                                nc.scalar.activation(KS[k * D:(k + 1) * D, h, late], khi[h * D:(h + 1) * D, late].bitcast(f32), ACT.Copy)

                        @block.vector
                        def _(dve):
                            chain = chain_of(dve, sem("chain_dve"))

                            def key_low(g):
                                if g == 0:
                                    dve.wait_ge(sem("query_high"), 1)
                                    nc.vector.scalar_tensor_tensor(qlo[:], ps[:, 2, :], bq[:], qhi[:].bitcast(f32), ALU.add, ALU.subtract).then_inc(sem("query_split"), 1)
                                dve.wait_ge(sem("key_high"), g + 1)
                                nc.vector.scalar_tensor_tensor(klo[:, g * BANK:(g + 1) * BANK], ps[:, g % 2, :], bk[:], khi[:, g * BANK:(g + 1) * BANK].bitcast(f32),
                                                               ALU.add, ALU.subtract).then_inc(sem("key_split"), 1)

                            ln_vector(dve, chain, tok, st, mv, w, y, t, lambda g: key_low(g - 3) if g >= 3 else None)
                            for g in range(NC - 3, NC):
                                key_low(g)
                            for g in range(NC):
                                dve.wait_ge(sem("value_ready"), g + 1)
                                nc.vector.tensor_tensor(V[:, 4 * g:4 * g + 4, :], ps[:, 2 + g % 2, :].rearrange("p (r n) -> p r n", n=P),
                                                        bv[:].rearrange("p (o n) -> p o n", o=1).broadcast_to([P, 4, P]),
                                                        ALU.add).then_inc(sem("value_out"), 1)
                            dve.wait_ge(sem("key_split"), NC)
                            for k, h in by_dve:
                                nc.vector.tensor_copy(KS[k * D:(k + 1) * D, h, late], klo[h * D:(h + 1) * D, late].bitcast(f32))

                        @block.sync
                        def _(sp):
                            sp.wait_ge(sem("query_split"), 1)
                            move_parts(sp, sem("move"), QS0[:], qhi[:], qlo[:], (0, 1, 0))
                            for k in range(2):
                                half = slice(k * (TOK // 2), (k + 1) * (TOK // 2))
                                sp.wait_ge(sem("key_split"), (k + 1) * NC // 2)
                                move_parts(sp, sem("move"), KS[:, :, half], khi[:, half], klo[:, half], (0, 0, 1),
                                           but=by_act + by_dve if k else ())
                            sp.wait_ge(sem("move"), 16 * (MOVES * 3 - len(by_act + by_dve)))
                clear_all()
                flag = nc.values_load(bounded[0:1, 0:1], min_val=0, max_val=P)
                with nc.If(flag >= P):
                    self_attention(nc, sem, X, ps, ones, wq, bq, wp, bp, xnT, KS, V, QS0)
                    clear_all()
                with nc.Else():
                    self_attention_with_maximum(nc, sem, clear_all, X, ps, ident, wq, bq, wk, bk, wp, bp, xnT, V)
                    clear_all()

            with ExitStack() as tmp:
                def sbt(name, shape, dt=f32):
                    return tmp.enter_context(nc.sbuf_tensor(name, shape, dt))
                tok = sbt("tok2", [P, NT, P])
                xnT = sbt("xnT2", [P, TOK])
                st = sbt("st2", [P, NT, 6])
                mv = sbt("mv2", [P, NT, 2])
                w = sbt("w2s", [P, NT])
                y = sbt("y2", [P, NT])
                t = sbt("t2", [P, NT])
                logit = sbt("logit", [E, TOK])
                prob = sbt("prob", [E, TOK])
                rest = sbt("rest", [E, TOK])
                best = sbt("best", [E, NC, 8])
                top = sbt("top", [E, 8])
                topp = sbt("topp", [E, 8])
                nmax = sbt("nmax", [E, 1])
                zsum = sbt("zsum", [E, 1])
                rz = sbt("rzg", [E, 1])
                selT = sbt("selT", [P, NT, E])
                QT = TOK // 4
                with nc.Block() as block:
                    @block.sync
                    def _(sp):
                        sp.dma_start(t_d[bass.ds(b, 1)].rearrange("a p n -> (a p) n"), X[:]).then_inc(sem("store"), 16)
                        sp.wait_ge(sem("scaled"), 4)
                        sp.dma_start(sel_d[bass.ds(b, 1)].rearrange("a p n -> (a p) n"), rest[:]).then_inc(sem("store"), 16)
                        sp.wait_ge(sem("store"), 32)

                    @block.tensor
                    def _(pe):
                        ln_tensor(pe)
                        ln_tensor_back(pe, tok)
                        for g in range(NC):
                            pe.wait_ge(sem("ln_out"), NC if g >= 4 else g + 1)
                            nc.tensor.matmul(ps[0:E, g, :], wgT[:], xnT[:, g * BANK:(g + 1) * BANK],
                                             start=True, stop=True).then_inc(sem("logits_ready"), 1)
                        for j in range(NT):
                            if j % 8 == 0:
                                pe.wait_ge(sem("scaled"), j // 8 + 1)
                            last = nc.tensor.transpose(ps[:, j // 8, (j % 8) * E:(j % 8 + 1) * E], rest[:, j * P:(j + 1) * P], ident[0:E, 0:E])
                            if j % 8 == 7:
                                last.then_inc(sem("turned_sel"), 1)
                        for j in range(NT):
                            if j % 8 == 0:
                                pe.wait_ge(sem("kept_sel"), j // 8 + 1)
                            last = nc.tensor.matmul(ps[:, 4, 0:E], tok[:, j, :], selT[:, j, :], start=(j == 0), stop=(j == NT - 1))
                        last.then_inc(sem("pooled_done"), 1)

                    @block.scalar
                    def _(act):
                        ln_scalar(act, tok, w[:], y[:], xnT)
                        for g in range(NC):
                            act.wait_ge(sem("logits_ready"), g + 1)
                            nc.scalar.activation(logit[:, g * BANK:(g + 1) * BANK], ps[0:E, g, :], ACT.Identity, bias=bg[:]).then_inc(sem("logits_out"), 1)
                        act.wait_ge(sem("top_ready"), 1)
                        nc.scalar.activation(topp[:], top[:], ACT.Exp, bias=nmax[:])
                        nc.scalar.activation(prob[:], logit[:], ACT.Exp, bias=nmax[:], accum_out=zsum[:]).then_inc(sem("probs_ready"), 1)
                        for k in range(4):
                            act.wait_ge(sem("selected"), min(k, 2) + 2)
                            if k == 3:
                                act.wait_ge(sem("selected_pool"), 1)
                            quarter = rest[:, k * QT:(k + 1) * QT]
                            nc.scalar.activation(quarter, quarter, ACT.Copy, scale=rz[:]).then_inc(sem("scaled"), 1)
                        for k in range(4):
                            act.wait_ge(sem("turned_sel"), k + 1)
                            nc.scalar.activation(selT[:, 8 * k:8 * k + 8, :], ps[:, k, :].rearrange("p (r n) -> p r n", n=E), ACT.Copy).then_inc(sem("kept_sel"), 1)

                    @block.gpsimd
                    def _(pool):
                        pool.wait_ge(sem("selected"), 1)
                        nc.gpsimd.tensor_tensor(rest[:, 3 * QT:], prob[:, 3 * QT:], rest[:, 3 * QT:], ALU.subtract).then_inc(sem("selected_pool"), 1)

                    @block.vector
                    def _(dve):
                        chain = chain_of(dve, sem("chain_dve"))
                        ln_vector(dve, chain, tok, st, mv, w, y, t)
                        for g in range(NC):
                            dve.wait_ge(sem("logits_out"), g + 1)
                            last = nc.vector.max(out=best[:, g, :], in_=logit[:, g * BANK:(g + 1) * BANK])
                        chain(last)
                        chain(nc.vector.max(out=top[:], in_=best[:].rearrange("e g k -> e (g k)")))
                        nc.vector.tensor_scalar(nmax[:], top[:, 0:1], -1.0, None, ALU.mult).then_inc(sem("top_ready"), 1)
                        dve.wait_ge(sem("probs_ready"), 1)
                        chain(nc.vector.match_replace(out=rest[:], in_to_replace=topp[:], in_values=prob[:], imm_value=0.0))
                        nc.vector.reciprocal(rz[:], zsum[:]).then_inc(sem("selected"), 1)
                        for k in range(3):
                            quarter = rest[:, k * QT:(k + 1) * QT]
                            nc.vector.tensor_tensor(quarter, prob[:, k * QT:(k + 1) * QT], quarter, ALU.subtract).then_inc(sem("selected"), 1)
                        dve.wait_ge(sem("pooled_done"), 1)
                        nc.vector.tensor_copy(poolT[:, :, bass.ds(b, 1)], ps[:, 4, 0:E].rearrange("p (e o) -> p e o", o=1)).then_inc(sem("pooled_kept"), 1)
            clear_all()

        experts(nc, sem, ps, ident, poolT, X, t_d, sel_d, w1, w2, out)


def move_parts(sp, moved, stack, high, low, parts, but=()):
    for k, part in enumerate(parts):
        for h in range(H):
            if (k, h) in but:
                continue
            src = (high, low)[part][h * D:(h + 1) * D, :].bitcast(f32)
            sp.dma_start(stack[k * D:(k + 1) * D, h, :].bitcast(f32), src).then_inc(moved, 16)


def contextual_attention(nc, sem, chain_of, newton_rsqrt, b, x, X, ps, ident, ones, gmat, mm, left, right):
    with ExitStack() as tmp:
        def sbt(name, shape, dt=f32):
            return tmp.enter_context(nc.sbuf_tensor(name, shape, dt))
        xg = sbt("xg", [P, IMG + 1, IMG])
        low_hi = sbt("low_hi", [P, PAD, PAD], f32r)
        low_lo = sbt("low_lo", [P, PAD, PAD], f32r)
        sq = sbt("sq", [P, PAD, PAD])
        gst = sbt("gst", [P, NC, 6])
        gmv = sbt("gmv", [P, 2])
        ge2 = sbt("ge2", [P, 2])
        gsm = sbt("gsm", [P, 4])
        wgt = sbt("wgt", [P, LOC])
        e = [sbt(f"e{i}", [P, LOC]) for i in range(2)]
        nmx = sbt("nmx", [P, LT])
        zs = sbt("zs", [P, LT])
        rz = sbt("rz0", [P, LT])
        diag = [sbt(f"diag{i}", [P, P]) for i in range(2)]
        stage = [sbt(f"stage{i}", [P, LT, ROWS, PAD]) for i in range(2)]
        shuf = [sbt(f"shuf{i}", [P, PAD * PAD]) for i in range(2)]
        C = [sbt(f"C{i}", [P, LT, PAD, LOW]) for i in range(2)]
        shifted = [[sbt(f"shifted{k}{v}", [P, LT + 2, ROWS, LOW], f32r) for v in range(3)] for k in range(2)]
        nextq = [s[:, 0:(PAD - 1) * LOW].rearrange("p (r c) -> p r c", c=LOW) for s in shuf]
        xs = C[1][:].rearrange("p a r c -> p (a r c)")[:, 0:4 * (LT + 1) * P].rearrange("p (a i n) -> p a i n", a=2, i=2)
        kept = xg[:].rearrange("p r c -> p (r c)")
        kept_at = [0]
        for l in range(LT - 1):
            kept_at.append(kept_at[-1] + (LT - 1 - l) * P)

        def computed_from(pt):
            return pt - 1 if pt % 4 == 3 else pt

        XT = sbt("XT", [P, 2, 2, LT + 1, P])
        xv = X[:].rearrange("p (r c) -> p r c", c=IMG)
        LOADS = 4
        x_in = [sem(f"x_in{k}") for k in range(LOADS)]
        NX = 4 * LT + 2

        def xt_index(n):
            if n < 4 * LT:
                return n // (2 * LT), n // LT % 2, n % LT
            return 1, n - 4 * LT, LT

        with nc.Block() as block:
            @block.sync
            def _(sp):
                for k in range(LOADS):
                    part = slice(k * (TOK // LOADS), (k + 1) * (TOK // LOADS))
                    sp.dma_start(X[:, part], x[bass.ds(b, 1)].rearrange("a c h w -> (a c) (h w)")[:, part]).then_inc(x_in[k], 16)

            @block.gpsimd
            def _(pool):
                nc.gpsimd.memset(xg[:, 0, :], 0.0)
                nc.gpsimd.memset(low_hi[:].bitcast(f32), 0.0)
                nc.gpsimd.memset(low_lo[:].bitcast(f32), 0.0)
                nc.gpsimd.memset(sq[:], 0.0)
                for i in range(2):
                    nc.gpsimd.memset(stage[i][:], 0.0)
                for i in range(2):
                    nc.gpsimd.memset(XT[0:P, 1, i, LT, :], 0.0)
                nc.gpsimd.memset(gsm[:, 3:4], 0.0).then_inc(sem("consts"), 1)
                pool.wait_ge(sem("source_kept"), (NX + 3) // 4)
                for i in range(2):
                    nc.gpsimd.memset(C[i][:, :, 0, :], 0.0)
                    nc.gpsimd.memset(C[i][:, :, PAD - 1, :], 0.0).then_inc(sem("consts"), 1)
                for pt in range(LT):
                    pool.wait_ge(sem("exp_done"), pt + 1)
                    nc.gpsimd.tensor_tensor(e[pt % 2][:], e[pt % 2][:], mm[:], ALU.mult).then_inc(sem("masked"), 1)
                pool.wait_ge(sem("columns_folded"), 2 * LT)
                for i in range(2):
                    nc.gpsimd.memset(nextq[i][0:LOW], 0.0).then_inc(sem("consts"), 1)

            @block.vector
            def _(dve):
                chain = chain_of(dve, sem("chain_dve"))
                for k in range(NC):
                    if k % (NC // LOADS) == 0:
                        dve.wait_ge(x_in[k * LOADS // NC], 16)
                    last = nc.vector.bn_stats(gst[:, k, :], X[:, k * BANK:(k + 1) * BANK])
                chain(last)
                chain(nc.vector.bn_aggr(gmv[:], gst[:]))
                chain(nc.vector.tensor_copy(ge2[:, 0:1], gmv[:, 0:1]))
                nc.vector.scalar_tensor_tensor(ge2[:, 1:2], gmv[:, 0:1], gmv[:, 0:1], gmv[:, 1:2], ALU.mult, ALU.add).then_inc(sem("channel_stats"), 1)
                dve.wait_ge(sem("group_stats"), 1)
                m, v, y, t = gmv[:, 0:1], gmv[:, 1:2], gsm[:, 0:1], gsm[:, 1:2]
                chain(nc.vector.tensor_copy(gmv[:], ps[:, 7, 0:2]))
                chain(nc.vector.tensor_tensor(t, m, m, ALU.mult))
                chain(nc.vector.tensor_tensor(v, v, t, ALU.subtract))
                nc.vector.tensor_scalar(v, v, GN_EPS, None, ALU.add).then_inc(sem("variance_ready"), 1)
                dve.wait_ge(sem("root_ready"), 1)
                chain(nc.vector.reciprocal(y, y))
                newton_rsqrt(dve, chain, y, v, t)
                dve.wait_ge(sem("consts"), 1)
                chain(nc.vector.tensor_scalar(xg[:, 1:IMG + 1, :], xv, m, y, ALU.subtract, ALU.mult))
                down = xg[:, 1:IMG + 1:2, 0:IMG:2]
                nc.vector.tensor_copy(low_hi[:, 1:1 + LOW, 1:1 + LOW], down).then_inc(sem("parts_ready"), 1)
                nc.vector.tensor_tensor(sq[:, 1:1 + LOW, 1:1 + LOW], down, down, ALU.mult).then_inc(sem("squares_ready"), 1)
                dve.wait_ge(sem("parts_ready"), 1)
                nc.vector.tensor_tensor(low_lo[:, 1:1 + LOW, 1:1 + LOW], down, low_hi[:, 1:1 + LOW, 1:1 + LOW].bitcast(f32),
                                        ALU.subtract).then_inc(sem("parts_ready"), 1)
                dve.wait_ge(sem("squares_summed"), 1)
                n2 = shuf[0][:, 0:PAD * PAD]
                nc.vector.tensor_copy(n2, ps[:, 4:7, :].rearrange("p a n -> p (a n)")[:, 0:PAD * PAD]).then_inc(sem("squares_read"), 1)
                dve.wait_ge(sem("squares_read"), 1)
                n2 = n2.rearrange("p (r c) -> p r c", c=PAD)
                rows = shuf[1][:, 0:PAD * LOW].rearrange("p (r c) -> p r c", c=LOW)
                chain(nc.vector.tensor_tensor(rows, n2[:, :, 0:LOW], n2[:, :, 1:1 + LOW], ALU.add))
                chain(nc.vector.tensor_tensor(rows, rows, n2[:, :, 2:2 + LOW], ALU.add))
                box = tile_order(e[0][:])
                chain(nc.vector.tensor_tensor(box, split_rows(rows[:, 0:LOW, :]), split_rows(rows[:, 1:1 + LOW, :]), ALU.add))
                chain(nc.vector.tensor_tensor(box, box, split_rows(rows[:, 2:2 + LOW, :]), ALU.add))
                chain(nc.vector.tensor_scalar(e[0][:], e[0][:], PATCH_EPS * PATCH_EPS, None, ALU.max))
                nc.vector.tensor_copy(gsm[:, 2:3], e[0][:, 0:1]).then_inc(sem("norms_ready"), 1)
                dve.wait_ge(sem("norms_rooted"), 1)
                newton_rsqrt(dve, chain, wgt[:], e[0][:], e[1][:])
                chain(nc.vector.scalar_tensor_tensor(wgt[:], wgt[:], SCALE0, mm[:], ALU.mult, ALU.mult))

                def finish(pt):
                    dve.wait_ge(sem("exp_done"), pt + 1)
                    chain(nc.vector.reciprocal(rz[:, pt:pt + 1], zs[:, pt:pt + 1]))
                    if pt >= 2:
                        dve.wait_ge(sem("exps_turned"), pt - 1)
                    nc.vector.tensor_scalar(diag[pt % 2][:], ident[:], rz[:, pt:pt + 1], None, ALU.mult).then_inc(sem("diag_ready"), 1)

                def fold_columns(pt, i):
                    dve.wait_ge(sem("turned_out"), pt + 1)
                    s = stage[pt % 2]
                    flat = s[:].rearrange("p a r c -> p (a r c)")
                    lanes = [min(max(j + 2 * i - 1, 0), LOW - 1) for j in range(LOW)]
                    chain(nc.vector.stream_shuffle(shuf[i][:, 0:LT * ROWS * PAD], flat, lanes))
                    sh = shuf[i][:, 0:LT * ROWS * PAD].rearrange("p (a r c) -> p a r c", r=ROWS, c=PAD)
                    keep = (left, right)[i]
                    for q in range(ROWS):
                        last = nc.vector.scalar_tensor_tensor(C[i][:, :, 1 + pt + LT * q, :], sh[:, :, q, 2 * i:2 * i + LOW],
                                                              keep[:], s[:, :, q, 1:1 + LOW], ALU.mult, ALU.add)
                    last.then_inc(sem("columns_folded"), 1)

                for pt in range(LT):
                    dve.wait_ge(sem("scores_ready"), pt + 1)
                    dve.wait_ge(sem("gram_kept"), min(pt + 1, LT - 1))
                    if pt >= 2:
                        dve.wait_ge(sem("exps_turned"), pt - 1)
                    chain(nc.vector.tensor_tensor_reduce(out=e[pt % 2][:], in0=ps[:, 2 * (pt % 2):2 * (pt % 2) + 2, :].rearrange("p a n -> p (a n)"),
                                                         in1=wgt[:], scale=1.0, scalar=-3.0e38, op0=ALU.mult, op1=ALU.max,
                                                         accum_out=nmx[:, pt:pt + 1]))
                    nc.vector.tensor_scalar(nmx[:, pt:pt + 1], nmx[:, pt:pt + 1], -1.0, None, ALU.mult).then_inc(sem("scores_scaled"), 1)
                    if pt >= 1:
                        fold_columns(pt - 1, 0)
                    finish(pt)
                    if pt >= 1:
                        fold_columns(pt - 1, 1)
                fold_columns(LT - 1, 0)
                fold_columns(LT - 1, 1)
                dve.wait_ge(sem("columns_folded"), 2 * LT)
                dve.wait_ge(sem("consts"), 3)
                for q in range(ROWS - 1):
                    nc.vector.tensor_copy(nextq[1][(q + 1) * LOW:(q + 2) * LOW], C[1][q * LOW:(q + 1) * LOW, LT - 1, 0:PAD - 1, :]).then_inc(sem("moved_on"), 1)
                dve.wait_ge(sem("moved_on"), 2 * (ROWS - 1))
                dve.wait_ge(sem("consts"), 5)
                dve.wait_ge(sem("unfolded_used"), 1)
                for t in range(LT - 1, -1, -1):
                    for i in range(2):
                        if t < LT - 1:
                            dve.wait_ge(sem("rows_folded"), 2 * (LT - 1 - t) + i - 1)
                        above = C[i][:, t - 1, 0:PAD - 1, :] if t else nextq[i][:]
                        nc.vector.tensor_tensor(C[i][:, t, 1:PAD, :], C[i][:, t, 1:PAD, :], above, ALU.add).then_inc(sem("rows_folded"), 1)
                for i in range(2):
                    for a in range(2):
                        for n in range(2):
                            dve.wait_ge(sem("pasted"), 4 * i + 2 * a + n + 1)
                            half = xv[:, a + LOW * n:LOW * n + LOW:2, i:IMG:2]
                            nc.vector.scalar_tensor_tensor(half, ps[:, 4 * a + 2 * i + n, :].rearrange("p (r c) -> p r c", c=LOW), 0.25, half,
                                                           ALU.mult, ALU.add).then_inc(sem("canvas_added"), 1)

            @block.tensor
            def _(pe):
                pe.wait_ge(sem("channel_stats"), 1)
                nc.tensor.matmul(ps[:, 7, 0:2], gmat[:], ge2[:], start=True, stop=True).then_inc(sem("group_stats"), 1)
                def scores(pt):
                    if pt >= 2:
                        pe.wait_ge(sem("scores_scaled"), pt - 1)
                        pe.wait_ge(sem("gram_kept"), pt - 1)
                    begin = computed_from(pt)
                    k = 0
                    for wt, mv in ((0, low_hi), (0, low_lo), (1, low_hi)):
                        for v in range(3):
                            if pt == 0:
                                pe.wait_ge(sem("shifted_ready"), 3 * wt + v + 1)
                                pe.wait_ge(sem("parts_ready"), 1 if mv is low_hi else 2)
                            for u in range(3):
                                for n in range(begin // 4, 2):
                                    lo = max(begin, 4 * n)
                                    win = mv[:, u:u + LOW, v:v + LOW].rearrange("p (q t) c -> p t q c", t=LT)[:, lo:4 * n + 4]
                                    last = nc.tensor.matmul(ps[:, 2 * (pt % 2) + n, (lo - 4 * n) * P:BANK],
                                                            shifted[wt][v][:, pt + u, :, :].rearrange("p q c -> p (q c)"),
                                                            win, start=(k == 0), stop=(k == 26))
                                k += 1
                    if begin:
                        pe.wait_ge(sem("gram_kept"), begin)
                    for l in range(begin):
                        at = kept_at[l] + (pt - l - 1) * P
                        last = nc.tensor.transpose(ps[:, 2 * (pt % 2) + l // 4, (l % 4) * P:(l % 4 + 1) * P], kept[:, at:at + P], ident[:])
                    last.then_inc(sem("scores_ready"), 1)

                def transpose_exps(pt):
                    pe.wait_ge(sem("masked"), pt + 1)
                    pe.wait_ge(sem("diag_ready"), pt + 1)
                    if pt >= 2:
                        pe.wait_ge(sem("turned_out"), pt - 1)
                    for lt in range(LT):
                        k = 4 + 2 * (pt % 2) + lt // 4
                        last = nc.tensor.matmul(ps[:, k, (lt % 4) * P:(lt % 4 + 1) * P], e[pt % 2][:, lt * P:(lt + 1) * P], diag[pt % 2][:], start=True, stop=True)
                    last.then_inc(sem("exps_turned"), 1)

                pe.wait_ge(sem("squares_ready"), 1)
                flat = sq[:].rearrange("p r c -> p (r c)")
                for k in range(3):
                    n = min(BANK, PAD * PAD - k * BANK)
                    last = nc.tensor.matmul(ps[:, 4 + k, 0:n], ones[:], flat[:, k * BANK:k * BANK + n], start=True, stop=True)
                last.then_inc(sem("squares_summed"), 1)
                scores(0)
                pe.wait_ge(sem("parity_ready"), 4)
                pe.wait_ge(sem("squares_read"), 1)
                for n in range(NX):
                    a, i, t = xt_index(n)
                    if n % 4 == 0 and n >= 16:
                        pe.wait_ge(sem("source_kept"), n // 4 - 3)
                    last = nc.tensor.transpose(ps[:, 4 + n // 4 % 4, (n % 4) * P:(n % 4 + 1) * P], xs[:, a, i, t * P:(t + 1) * P], ident[:])
                    if n % 4 == 3 or n == NX - 1:
                        last.then_inc(sem("source_turned"), 1)
                scores(1)
                pe.wait_ge(sem("source_kept"), (NX + 3) // 4)
                for pt in range(LT):
                    transpose_exps(pt)
                    if pt + 2 < LT:
                        scores(pt + 2)
                pe.wait_ge(sem("turned_out"), LT)
                pe.wait_ge(sem("scores_scaled"), LT)
                pe.wait_ge(sem("columns_folded"), 2 * LT)
                for i in range(2):
                    for n in range(2):
                        last = nc.tensor.matmul(ps[:, 4 + 2 * i + n, :], XT[:, 1, i, LT, :], C[i][:, LT - 1, 16 * n + 1:16 * n + 17, :], start=True, stop=False)
                last.then_inc(sem("unfolded_used"), 1)
                for t in range(LT - 1, -1, -1):
                    for i in range(2):
                        pe.wait_ge(sem("rows_folded"), 2 * (LT - 1 - t) + i + 1)
                        for a in range(2):
                            for n in range(2):
                                last = nc.tensor.matmul(ps[:, 4 * a + 2 * i + n, :], XT[:, a, i, t, :], C[i][:, t, 16 * n + 1 + a:16 * n + 17 + a, :],
                                                        start=(a == 0 and t == LT - 1), stop=(t == 0))
                                if t == 0:
                                    last.then_inc(sem("pasted"), 1)

            @block.scalar
            def _(act):
                act.wait_ge(sem("variance_ready"), 1)
                nc.scalar.activation(gsm[:, 0:1], gmv[:, 1:2], ACT.Sqrt).then_inc(sem("root_ready"), 1)
                for k, part in enumerate((low_hi, low_lo)):
                    act.wait_ge(sem("parts_ready"), k + 1)
                    for v in range(3):
                        cols = part[:, :, v:v + LOW].bitcast(f32)
                        nc.scalar.activation(shifted[k][v][:, 0:LT], cols[:, 0:LOW].rearrange("p (q t) c -> p t q c", t=LT), ACT.Copy)
                        for r in (LT, LT + 1):
                            ins = nc.scalar.activation(shifted[k][v][:, r], cols[:, r:r + LT * (ROWS - 1) + 1:LT], ACT.Copy)
                        ins.then_inc(sem("shifted_ready"), 1)
                for a in range(2):
                    tiles = LT + a
                    for i in range(2):
                        dst = xs[:, a, i, 0:tiles * P].rearrange("p (t q c) -> p t q c", q=ROWS, c=LOW)
                        for q in range(ROWS):
                            r0 = 2 * LT * q + 1 - a
                            ins = nc.scalar.activation(dst[:, :, q, :], xg[:, r0:r0 + 2 * tiles - 1:2, i:IMG:2], ACT.Copy)
                        ins.then_inc(sem("parity_ready"), 1)
                act.wait_ge(sem("norms_ready"), 1)
                nc.scalar.activation(wgt[:], e[0][:], ACT.Ln).then_inc(sem("chain_act"), 1)
                act.wait_ge(sem("chain_act"), 1)
                nc.scalar.activation(wgt[:], wgt[:], ACT.Exp, scale=-0.5).then_inc(sem("norms_rooted"), 1)
                def keep(l):
                    act.wait_ge(sem("scores_ready"), l + 1)
                    at, n = kept_at[l], (LT - 1 - l) * P
                    if l == 0:
                        act.wait_ge(sem("parity_ready"), 4)
                    if n:
                        s = 2 * (l % 2)
                        nc.scalar.activation(kept[:, at:at + n], ps[:, s:s + 2, :].rearrange("p a n -> p (a n)")[:, (l + 1) * P:LT * P],
                                             ACT.Copy).then_inc(sem("gram_kept"), 1)

                keep(0)
                act.wait_ge(sem("consts"), 1)
                for k in range((NX + 3) // 4):
                    act.wait_ge(sem("source_turned"), k + 1)
                    a, i, t = xt_index(4 * k)
                    if k < LT:
                        nc.scalar.activation(XT[:, a, i, t:t + 4, :], ps[:, 4 + k % 4, :].rearrange("p (r n) -> p r n", n=P), ACT.Copy).then_inc(sem("source_kept"), 1)
                    else:
                        q = P - LOW
                        nc.scalar.activation(XT[q:P, 1, :, LT, :], ps[q:P, 4 + k % 4, 0:2 * P].rearrange("p (r n) -> p r n", n=P), ACT.Copy).then_inc(sem("source_kept"), 1)
                for pt in range(LT + 1):
                    if 1 <= pt < LT - 1:
                        keep(pt)
                    if pt >= 1:
                        q = pt - 1
                        act.wait_ge(sem("exps_turned"), q + 1)
                        if q >= 2:
                            act.wait_ge(sem("columns_folded"), 2 * (q - 1))
                        k = 4 + 2 * (q % 2)
                        nc.scalar.activation(stage[q % 2][:, :, :, 1:1 + LOW], ps[:, k:k + 2, :].rearrange("p k (a r c) -> p (k a) r c", r=ROWS, c=LOW),
                                             ACT.Copy).then_inc(sem("turned_out"), 1)
                    if pt < LT:
                        act.wait_ge(sem("scores_scaled"), pt + 1)
                        nc.scalar.activation(e[pt % 2][:], e[pt % 2][:], ACT.Exp, bias=nmx[:, pt:pt + 1], accum_out=zs[:, pt:pt + 1]).then_inc(sem("exp_done"), 1)
                act.wait_ge(sem("columns_folded"), 2 * LT)
                act.wait_ge(sem("consts"), 3)
                for q in range(ROWS - 1):
                    nc.scalar.activation(nextq[0][(q + 1) * LOW:(q + 2) * LOW], C[0][q * LOW:(q + 1) * LOW, LT - 1, 0:PAD - 1, :],
                                         ACT.Copy).then_inc(sem("moved_on"), 1)


def bound_logits(nc, sem, chain_of, ps, ones, wq, wk, bq, bk, bounded):
    with ExitStack() as tmp:
        def sbt(name, shape, dt=f32):
            return tmp.enter_context(nc.sbuf_tensor(name, shape, dt))
        same = sbt("same", [P, P])
        gram = sbt("gram", [P, 2, P])
        square = sbt("square", [P, 2, P])
        scratch = sbt("scratch", [P, 2, P])
        rows = sbt("rows", [P, 4])
        norms = sbt("norms", [P, 4])
        roots = sbt("roots", [P, 4])
        length = sbt("length", [P, 2])
        fine = sbt("fine", [P, 5])
        good = sbt("good", [P, 1])
        with nc.Block() as block:
            @block.gpsimd
            def _(pool):
                chain = chain_of(pool, sem("chain_pool"))
                chain(nc.gpsimd.memset(same[:], 1.0))
                s3 = same[:].rearrange("p (h d) -> p h d", d=D)
                chain(nc.gpsimd.affine_select(out=s3, in_=s3, compare_op=ALU.is_ge, fill=0.0, base=0,
                                              pattern=[[-D, H], [0, D]], channel_multiplier=1))
                chain(nc.gpsimd.affine_select(out=s3, in_=s3, compare_op=ALU.is_ge, fill=0.0, base=D - 1,
                                              pattern=[[D, H], [0, D]], channel_multiplier=-1))

            @block.tensor
            def _(pe):
                for k, w in enumerate((wq, wk)):
                    nc.tensor.matmul(ps[:, k, 0:P], w[:], w[:], start=True, stop=True).then_inc(sem("mm_a"), 1)
                for k in range(2):
                    pe.wait_ge(sem("ready_a"), k + 1)
                    nc.tensor.matmul(ps[:, 2 + k, 0:P], gram[:, k, :], gram[:, k, :], start=True, stop=True).then_inc(sem("mm_b"), 1)
                pe.wait_ge(sem("ready_b"), 4)
                nc.tensor.matmul(ps[:, 4, 0:4], same[:], rows[:], start=True, stop=True).then_inc(sem("mm_c"), 1)
                pe.wait_ge(sem("ready_e"), 1)
                nc.tensor.matmul(ps[0:1, 5, 0:1], good[:], ones[:, 0:1], start=True, stop=True).then_inc(sem("mm_d"), 1)

            @block.scalar
            def _(act):
                act.wait_ge(sem("ready_c"), 1)
                nc.scalar.activation(roots[:], norms[:], ACT.Ln).then_inc(sem("chain_act"), 1)
                act.wait_ge(sem("chain_act"), 1)
                nc.scalar.activation(roots[:, 0:2], roots[:, 0:2], ACT.Exp, scale=0.125).then_inc(sem("ready_d"), 1)
                nc.scalar.activation(roots[:, 2:4], roots[:, 2:4], ACT.Exp, scale=0.5).then_inc(sem("ready_d"), 1)

            @block.vector
            def _(dve):
                chain = chain_of(dve, sem("chain_dve"))
                dve.wait_ge(sem("chain_pool"), 3)
                for k in range(2):
                    dve.wait_ge(sem("mm_a"), k + 1)
                    nc.vector.tensor_tensor(gram[:, k, :], ps[:, k, 0:P], same[:], ALU.mult).then_inc(sem("ready_a"), 1)
                for k, bias in enumerate((bq, bk)):
                    nc.vector.tensor_tensor(rows[:, 2 + k:3 + k], bias[:], bias[:], ALU.mult).then_inc(sem("ready_b"), 1)
                for k in range(2):
                    dve.wait_ge(sem("mm_b"), k + 1)
                    chain(nc.vector.tensor_copy(square[:, k, :], ps[:, 2 + k, 0:P]))
                    nc.vector.tensor_tensor_reduce(out=scratch[:, k, :], in0=square[:, k, :], in1=square[:, k, :], scale=1.0, scalar=0.0,
                                                   op0=ALU.mult, op1=ALU.add, accum_out=rows[:, k:k + 1]).then_inc(sem("ready_b"), 1)
                dve.wait_ge(sem("mm_c"), 1)
                chain(nc.vector.tensor_scalar(fine[:, 0:4], ps[:, 4, 0:4], 1.0e18, None, ALU.is_le))
                nc.vector.tensor_scalar(norms[:], ps[:, 4, 0:4], 1.0e-15, 1.0e18, ALU.max, ALU.min).then_inc(sem("ready_c"), 1)
                dve.wait_ge(sem("ready_d"), 2)
                chain(nc.vector.scalar_tensor_tensor(length[:], roots[:, 0:2], float(P) ** 0.5, roots[:, 2:4], ALU.mult, ALU.add))
                chain(nc.vector.tensor_tensor(fine[:, 4:5], length[:, 0:1], length[:, 1:2], ALU.mult))
                chain(nc.vector.tensor_scalar(fine[:, 4:5], fine[:, 4:5], LOGIT_BOUND / SCALE1, None, ALU.is_le))
                nc.vector.tensor_reduce(good[:], fine[:], AX.X, ALU.min).then_inc(sem("ready_e"), 1)
                dve.wait_ge(sem("mm_d"), 1)
                nc.vector.tensor_copy(bounded[:], ps[0:1, 5, 0:1]).then_inc(sem("ready_f"), 1)
                dve.wait_ge(sem("ready_f"), 1)


def self_attention_with_maximum(nc, sem, clear_all, X, ps, ident, wq, bq, wk, bk, wp, bp, xnT, V):
    with ExitStack() as tmp:
        def sbt(name, shape, dt=f32):
            return tmp.enter_context(nc.sbuf_tensor(name, shape, dt))
        kf = sbt("kf", [P, TOK])
        qf = sbt("qf", [P, TOK])
        qt = sbt("qt", [P, P])
        row = sbt("row", [P, TOK])
        pt = sbt("pt", [P, NT, P])
        nmax = sbt("nmaxg", [P, H])
        total = sbt("total", [P, H])
        rtotal = sbt("rtotal", [P, H])
        heads = sbt("heads", [P, P])
        headsT = sbt("headsT", [P, P])
        with nc.Block() as block:
            @block.tensor
            def _(pe):
                for g in range(2 * NC):
                    if g >= 8:
                        pe.wait_ge(sem("free_a"), g // 2 - 3)
                        pe.wait_ge(sem("free_b"), g // 2 - 3)
                    nc.tensor.matmul(ps[:, g % 8, :], (wk, wq)[g % 2][:], xnT[:, g // 2 * BANK:(g // 2 + 1) * BANK],
                                     start=True, stop=True).then_inc(sem("mm_a"), 1)

            @block.scalar
            def _(act):
                for g in range(NC):
                    act.wait_ge(sem("mm_a"), 2 * g + 1)
                    nc.scalar.activation(kf[:, g * BANK:(g + 1) * BANK], ps[:, 2 * g % 8, :], ACT.Identity, bias=bk[:]).then_inc(sem("free_a"), 1)

            @block.vector
            def _(dve):
                for g in range(NC):
                    dve.wait_ge(sem("mm_a"), 2 * g + 2)
                    nc.vector.tensor_scalar(qf[:, g * BANK:(g + 1) * BANK], ps[:, (2 * g + 1) % 8, :], bq[:], None, ALU.add).then_inc(sem("free_b"), 1)
        clear_all()
        with nc.Fori(0, NT) as t:
            with nc.Block() as block:
                @block.tensor
                def _(pe):
                    pe.wait_ge(sem("ready_a"), 1)
                    for h in range(H):
                        rows = slice(h * D, (h + 1) * D)
                        if h:
                            pe.wait_ge(sem("ready_f"), h)
                        for g in range(NC):
                            nc.tensor.matmul(ps[:, g, :], qt[rows, :], kf[rows, g * BANK:(g + 1) * BANK],
                                             start=True, stop=True).then_inc(sem("mm_a"), 1)
                        pe.wait_ge(sem("ready_d"), h + 1)
                        for g in range(NC):
                            for r in range(4):
                                k = 4 * g + r
                                last = nc.tensor.transpose(ps[:, g, r * P:(r + 1) * P], row[:, k * P:(k + 1) * P], ident[:])
                            last.then_inc(sem("mm_b"), 1)
                        pe.wait_ge(sem("ready_e"), NC * (h + 1))
                        for k in range(NT):
                            last = nc.tensor.matmul(ps[:, 0, 0:D], pt[:, k, :], V[:, k, rows], start=(k == 0), stop=(k == NT - 1))
                        last.then_inc(sem("mm_c"), 1)
                    pe.wait_ge(sem("ready_f"), H)
                    nc.tensor.transpose(ps[:, 1, 0:P], heads[:], ident[:]).then_inc(sem("mm_d"), 1)
                    pe.wait_ge(sem("ready_g"), 1)
                    nc.tensor.matmul(ps[:, 2, 0:P], wp[:], headsT[:], start=True, stop=True).then_inc(sem("mm_d"), 1)

                @block.scalar
                def _(act):
                    for h in range(H):
                        if h:
                            act.wait_ge(sem("mm_b"), NC * h)
                        for g in range(NC):
                            act.wait_ge(sem("mm_a"), NC * h + g + 1)
                            nc.scalar.activation(row[:, g * BANK:(g + 1) * BANK], ps[:, g, :], ACT.Copy).then_inc(sem("ready_b"), 1)
                        act.wait_ge(sem("ready_c"), h + 1)
                        nc.scalar.activation(row[:], row[:], ACT.Exp, bias=nmax[:, h:h + 1], scale=SCALE1, accum_out=total[:, h:h + 1]).then_inc(sem("ready_d"), 1)
                    act.wait_ge(sem("mm_d"), 1)
                    nc.scalar.activation(headsT[:], ps[:, 1, 0:P], ACT.Copy).then_inc(sem("ready_g"), 1)

                @block.vector
                def _(dve):
                    nc.vector.tensor_copy(qt[:], qf[:, bass.ds(t * P, P)]).then_inc(sem("ready_a"), 1)
                    for h in range(H):
                        dve.wait_ge(sem("ready_b"), NC * (h + 1))
                        nc.vector.reduce_max(nmax[:, h:h + 1], row[:], AX.X).then_inc(sem("chain_dve"), 1)
                        dve.wait_ge(sem("chain_dve"), 2 * h + 1)
                        nc.vector.tensor_scalar(nmax[:, h:h + 1], nmax[:, h:h + 1], -SCALE1, None, ALU.mult).then_inc(sem("ready_c"), 1)
                        dve.wait_ge(sem("ready_d"), h + 1)
                        nc.vector.reciprocal(rtotal[:, h:h + 1], total[:, h:h + 1]).then_inc(sem("chain_dve"), 1)
                        for g in range(NC):
                            dve.wait_ge(sem("mm_b"), NC * h + g + 1)
                            nc.vector.tensor_copy(pt[:, 4 * g:4 * g + 4, :], ps[:, g, :].rearrange("p (r n) -> p r n", n=P)).then_inc(sem("ready_e"), 1)
                        dve.wait_ge(sem("mm_c"), h + 1)
                        dve.wait_ge(sem("chain_dve"), 2 * h + 2)
                        nc.vector.tensor_scalar(heads[:, h * D:(h + 1) * D], ps[:, 0, 0:D], rtotal[:, h:h + 1], None, ALU.mult).then_inc(sem("ready_f"), 1)
                    dve.wait_ge(sem("mm_d"), 2)
                    xc = X[:, bass.ds(t * P, P)]
                    nc.vector.scalar_tensor_tensor(xc, ps[:, 2, 0:P], bp[:], xc, ALU.add, ALU.add).then_inc(sem("ready_h"), 1)
            clear_all()


def self_attention(nc, sem, X, ps, ones, wq, bq, wp, bp, xnT, KS, V, QS0):
    with ExitStack() as tmp:
        def sbt(name, shape, dt=f32):
            return tmp.enter_context(nc.sbuf_tensor(name, shape, dt))
        QS = (QS0, sbt("QS1", [3 * D, H, BANK], f32r))
        qhi = sbt("qhi", [P, BANK], f32r)
        qlo = sbt("qlo", [P, BANK], f32r)
        PR = sbt("PR", [P, PBUFS, H * BANK])
        acc = sbt("acc", [P, 3, H * BANK])
        raw = sbt("raw", [P, BANK])
        rz = sbt("rz", [P, BANK])
        HALF = BANK // 2
        U = 2 * NT
        ND, NP_ = len(DVE_TILES) - 1, len(POOL_TILES) - 1

        def sums_with(tiles, kt):
            return max(tiles.index(kt), 1)


        with nc.Block() as block:
            @block.sync
            def _(sp):
                def stack(c, par):
                    sp.wait_ge(sem("queries_split"), c)
                    move_parts(sp, sem("move"), QS[par][:], qhi[:], qlo[:], (0, 1, 0))
                stack(1, 1)
                with sp.Fori(1, NC - 1, 2) as i:
                    stack(i + 1, 0)
                    stack(i + 2, 1)
                sp.wait_ge(sem("move"), 16 * MOVES * (NC - 1))

            @block.tensor
            def _(pe):
                def queries(c):
                    nc.tensor.matmul(ps[:, 7, :], wq[:], xnT[:, bass.ds(c * BANK, BANK)], start=True, stop=True).then_inc(sem("bank7_written"), 1)

                def scores(u, par):
                    kt, hp = u // 2, u % 2
                    for h in (2 * hp, 2 * hp + 1):
                        last = nc.tensor.matmul(ps[:, 2 * slot_of(u) + h % 2, :], KS[:, h, kt * P:(kt + 1) * P],
                                                QS[par][:, h, :], start=True, stop=True)
                    last.then_inc(sem("scores_done"), 1)

                def finish(c, par):
                    pe.wait_ge(sem("queries_split"), c + 1)
                    pe.wait_ge(sem("sum_dve"), (c + 1) * ND)
                    pe.wait_ge(sem("sum_pool"), (c + 1) * NP_)
                    for k in (par, 2):
                        for h in range(H):
                            last = nc.tensor.matmul(ps[h * D:(h + 1) * D, 7, :], ones[:, 0:D],
                                                    acc[:, k, h * BANK:(h + 1) * BANK], start=(k < 2), stop=(k == 2))
                    last.then_inc(sem("bank7_written"), 1)

                def finish_last():
                    pe.wait_ge(sem("projection_added"), NC - 1)
                    for k, addend in enumerate((PR[:, (NT - 1) % PBUFS, :], acc[:, 1, :], acc[:, 2, :])):
                        if k == 1:
                            pe.wait_ge(sem("sum_dve"), NC * ND - 1)
                        if k == 2:
                            pe.wait_ge(sem("sum_pool"), NC * NP_)
                        for h in range(H):
                            last = nc.tensor.matmul(ps[h * D:(h + 1) * D, 7, :], ones[:, 0:D], addend[:, h * BANK:(h + 1) * BANK],
                                                    start=(k == 0), stop=(k == 2))
                    last.then_inc(sem("bank7_written"), 1)

                def project(c):
                    pe.wait_ge(sem("heads_normed"), c + 1)
                    nc.tensor.matmul(ps[:, 7, :], wp[:], rz[:], start=True, stop=True).then_inc(sem("bank7_written"), 1)

                def project_last():
                    for part in range(2):
                        pe.wait_ge(sem("heads_normed"), NC + part)
                        nc.tensor.matmul(ps[:, part, 0:HALF], wp[:], rz[:, part * HALF:(part + 1) * HALF],
                                         start=True, stop=True).then_inc(sem("bank7_written"), 1)

                def block_of(i, par, first, final=False):
                    nxt = 1 - par
                    for kt in range(NT):
                        for u in (2 * kt + 2, 2 * kt + 3):
                            if u < U:
                                if u >= 3:
                                    pe.wait_ge(sem("exp_done"), i * U + (U - 2 if u == U - 1 else u - 2))
                                scores(u, par)
                            elif final:
                                continue
                            elif u == U:
                                pe.wait_ge(sem("move"), (i + 1) * (16 * MOVES))
                                scores(0, nxt)
                            else:
                                pe.wait_ge(sem("exp_done"), (i + 1) * U)
                                scores(1, nxt)
                        if kt == 0 and not first:
                            pe.wait_ge(sem("weighted_out"), i)
                        pe.wait_ge(sem("exp_done"), i * U + (2 * kt + 2))
                        for h in range(H):
                            last = nc.tensor.matmul(ps[h * D:(h + 1) * D, 6, :], V[:, kt, h * D:(h + 1) * D],
                                                    PR[:, kt % PBUFS, h * BANK:(h + 1) * BANK], start=(kt == 0), stop=(kt == NT - 1))
                        last.then_inc(sem("pv_done"), 1)
                        if kt == 2 and not first:
                            finish(i - 1, nxt)
                        if kt == 15 and not first:
                            project(i - 1)
                        if kt == 19 and not final:
                            if not first:
                                pe.wait_ge(sem("projection_added"), i)
                            queries(i + 1)

                scores(0, 0)
                scores(1, 0)
                block_of(0, 0, True)
                with pe.Fori(1, NC - 1, 2) as i:
                    block_of(i, 1, False)
                    block_of(i + 1, 0, False)
                block_of(NC - 1, 1, False, final=True)
                finish_last()
                project_last()

            @block.scalar
            def _(act):
                def block_of(i, first):
                    for kt in range(NT):
                        if kt >= PBUFS:
                            k = kt - PBUFS
                            act.wait_ge(sem("pv_done"), i * NT + (k + 1))
                            if k in DVE_TILES:
                                act.wait_ge(sem("sum_dve"), i * ND + sums_with(DVE_TILES, k))
                            else:
                                act.wait_ge(sem("sum_pool"), i * NP_ + sums_with(POOL_TILES, k))
                        elif not first:
                            k = NT - PBUFS + kt
                            act.wait_ge(sem("pv_done"), i * NT - (NT - 1 - k))
                            if k in DVE_TILES:
                                act.wait_ge(sem("sum_dve"), i * ND - (ND - sums_with(DVE_TILES, k)))
                            else:
                                act.wait_ge(sem("sum_pool"), i * NP_ - (NP_ - sums_with(POOL_TILES, k)))
                        for hp in range(2):
                            u = 2 * kt + hp
                            act.wait_ge(sem("scores_done"), i * U + (u + 1))
                            s = 2 * slot_of(u)
                            nc.scalar.activation(PR[:, kt % PBUFS, hp * PAIR:(hp + 1) * PAIR], ps[:, s:s + 2, :].rearrange("p a n -> p (a n)"),
                                                 ACT.Exp, scale=SCALE1).then_inc(sem("exp_done"), 1)
                block_of(0, True)
                with act.Fori(1, NC) as i:
                    block_of(i, False)

            @block.gpsimd
            def _(pool):
                def divide(i):
                    pool.wait_ge(sem("weighted_out"), i)
                    pool.wait_ge(sem("sums_inverted"), 2 * i)
                    nc.gpsimd.tensor_tensor(rz[:], rz[:], raw[:], ALU.mult).then_inc(sem("heads_normed"), 1)

                def block_of(i, first):
                    dst = acc[:, 2, :]
                    for k, kt in enumerate(POOL_TILES):
                        if k >= 1:
                            pool.wait_ge(sem("exp_done"), i * U + (2 * kt + 2))
                        if k == 1:
                            if not first:
                                pool.wait_ge(sem("bank7_written"), 3 * i - 1)
                            nc.gpsimd.tensor_tensor(dst, PR[:, POOL_TILES[0] % PBUFS, :], PR[:, kt % PBUFS, :], ALU.add).then_inc(sem("sum_pool"), 1)
                        elif k > 1:
                            pool.wait_ge(sem("sum_pool"), i * NP_ + (k - 1))
                            nc.gpsimd.tensor_tensor(dst, dst, PR[:, kt % PBUFS, :], ALU.add).then_inc(sem("sum_pool"), 1)
                        if kt == 9 and not first:
                            divide(i)

                block_of(0, True)
                with pool.Fori(1, NC) as i:
                    block_of(i, False)

            @block.vector
            def _(dve):
                def queries_low(c):
                    dve.wait_ge(sem("queries_high"), c)
                    nc.vector.scalar_tensor_tensor(qlo[:], ps[:, 7, :], bq[:], qhi[:].bitcast(f32), ALU.add, ALU.subtract).then_inc(sem("queries_split"), 1)

                def invert(i, part):
                    dve.wait_ge(sem("bank7_written"), 3 * i - 1)
                    half = slice(part * (BANK // 2), (part + 1) * (BANK // 2))
                    nc.vector.reciprocal(rz[:, half], ps[:, 7, half]).then_inc(sem("sums_inverted"), 1)

                def add_out(i):
                    dve.wait_ge(sem("bank7_written"), 3 * i)
                    xc = X[:, bass.ds(i * BANK - BANK, BANK)]
                    nc.vector.scalar_tensor_tensor(xc, ps[:, 7, :], bp[:], xc, ALU.add, ALU.add).then_inc(sem("projection_added"), 1)

                def block_of(i, par, first, final=False):
                    dst = acc[:, par, :]
                    for kt in range(NT):
                        k = DVE_TILES.index(kt) if kt in DVE_TILES else 0
                        if kt == NT - 1:
                            dve.wait_ge(sem("pv_done"), (i + 1) * NT)
                            nc.vector.tensor_copy(raw[:], ps[:, 6, :]).then_inc(sem("weighted_out"), 1)
                        if kt == NT - 1 and final:
                            continue
                        if k >= 1:
                            dve.wait_ge(sem("exp_done"), i * U + (2 * kt + 2))
                        if k == 1:
                            nc.vector.tensor_tensor(dst, PR[:, DVE_TILES[0] % PBUFS, :], PR[:, kt % PBUFS, :], ALU.add).then_inc(sem("sum_dve"), 1)
                        elif k > 1:
                            dve.wait_ge(sem("sum_dve"), i * ND + (k - 1))
                            nc.vector.tensor_tensor(dst, dst, PR[:, kt % PBUFS, :], ALU.add).then_inc(sem("sum_dve"), 1)
                        if kt == 5 and not first:
                            invert(i, 0)
                        if kt == 8 and not first:
                            invert(i, 1)
                        if kt == 17 and not first:
                            add_out(i)
                        if kt == 21 and not final:
                            dve.wait_ge(sem("bank7_written"), 3 * i + 1)
                            if not first:
                                dve.wait_ge(sem("move"), i * (16 * MOVES))
                            nc.vector.tensor_scalar(qhi[:], ps[:, 7, :], bq[:], None, ALU.add).then_inc(sem("queries_high"), 1)
                        if kt == 23 and not final:
                            queries_low(i + 1)

                block_of(0, 0, True)
                with dve.Fori(1, NC - 1, 2) as i:
                    block_of(i, 1, False)
                    block_of(i + 1, 0, False)
                block_of(NC - 1, 1, False, final=True)
                dve.wait_ge(sem("bank7_written"), 3 * NC - 2)
                dve.wait_ge(sem("weighted_out"), NC)
                for part in range(2):
                    half = slice(part * HALF, (part + 1) * HALF)
                    nc.vector.reciprocal(rz[:, half], ps[:, 7, half]).then_inc(sem("sums_inverted"), 1)
                    dve.wait_ge(sem("sums_inverted"), 2 * (NC - 1) + part + 1)
                    nc.vector.tensor_tensor(rz[:, half], rz[:, half], raw[:, half], ALU.mult).then_inc(sem("heads_normed"), 1)
                for part in range(2):
                    dve.wait_ge(sem("bank7_written"), 3 * NC - 1 + part)
                    xc = X[:, TOK - BANK + part * HALF:TOK - BANK + (part + 1) * HALF]
                    nc.vector.scalar_tensor_tensor(xc, ps[:, part, 0:HALF], bp[:], xc, ALU.add, ALU.add)


def experts(nc, sem, ps, ident, poolT, X, t_d, sel_d, w1, w2, out):
    with ExitStack() as tmp:
        def sbt(name, shape, dt=f32):
            return tmp.enter_context(nc.sbuf_tensor(name, shape, dt))
        W1 = sbt("W1", [P, WBUFS, EG, HID])
        W2 = sbt("W2", [P, WBUFS, EG, HC, P])
        B1 = sbt("B1", [P, HID])
        B2 = sbt("B2", [P, P])
        pick = sbt("pick", [P, E, LANES])
        pooled = sbt("pooled", [P, E, LANES])
        hid = sbt("hid", [P, 2, HID])
        hidT = sbt("hidT", [P, 2, HC, P])
        res = sbt("res", [P, 2, P])
        outT = sbt("outT", [P, NIMG, E])
        outE = sbt("outE", [P, NIMG, P])
        tin = sbt("tin", [P, NIMG - 1, TOK])
        sin = sbt("sin", [P, NIMG // 2, TOK])
        w1_in = [sem(f"w1_in{k}") for k in range(WBUFS)]
        w2_in = [sem(f"w2_in{k}") for k in range(WBUFS)]
        tok_in = [sem(f"tok_in{b}") for b in range(NIMG - 1)]
        sel_in = [sem(f"sel_in{a}") for a in range(NIMG // 2)]
        images = [tin[:, b] for b in range(NIMG - 1)] + [X[:]]
        with nc.Block() as block:
            @block.sync
            def _(sp):
                sp.wait_ge(sem("zeroed"), 1)
                sp.dma_start(B1[0:E], w1[:, P, :]).then_inc(sem("bias_in"), 16)
                sp.dma_start(B2[0:E], w2[:, HID, :]).then_inc(sem("bias_in"), 16)
                for g in range(NEG):
                    if g >= WBUFS:
                        sp.wait_ge(sem("first_done"), g - WBUFS + 1)
                    es = slice(g * EG, (g + 1) * EG)
                    sp.dma_start(W1[:, g % WBUFS], w1[es, 0:P, :].rearrange("e d h -> d e h")).then_inc(w1_in[g % WBUFS], 16)
                    if g == NEG // 2:
                        for a in range(NIMG // 2):
                            sp.dma_start(sin[:, a], sel_d[2 * a:2 * a + 2].rearrange("b e n -> (b e) n")).then_inc(sel_in[a], 16)
                sp.wait_ge(w2_in[(NEG - 1) % WBUFS], 16 * (NEG // WBUFS))
                for b in range(NIMG - 1):
                    sp.dma_start(tin[:, b], t_d[b]).then_inc(tok_in[b], 16)

            @block.gpsimd
            def _(pool):
                for g in range(NEG):
                    if g >= WBUFS:
                        pool.wait_ge(sem("second_done"), g - WBUFS + 1)
                    es = slice(g * EG, (g + 1) * EG)
                    pool.dma_start(W2[:, g % WBUFS], w2[es, 0:HID, :].rearrange("e (p c) o -> p e c o", c=HC)).then_inc(w2_in[g % WBUFS], 16)

            @block.tensor
            def _(pe):
                def first(g):
                    pe.wait_ge(w1_in[g % WBUFS], 16 * (g // WBUFS + 1))
                    if g >= 2:
                        pe.wait_ge(sem("gelu_done"), g - 1)
                    nc.tensor.matmul(ps[:, g % 2, :], pick[:, g * EG:(g + 1) * EG, :].rearrange("p e l -> p (e l)"), B1[:],
                                     start=True, stop=False)
                    for j in range(EG):
                        last = nc.tensor.matmul(ps[j * LANES:(j + 1) * LANES, g % 2, :], pooled[:, g * EG + j, :],
                                                W1[:, g % WBUFS, j, :], start=False, stop=True)
                    last.then_inc(sem("first_done"), 1)

                def turn(g):
                    pe.wait_ge(sem("gelu_done"), g + 1)
                    if g >= 2:
                        pe.wait_ge(sem("turned_out"), g - 1)
                    for c in range(HC):
                        last = nc.tensor.transpose(ps[:, 2 + g % 2, c * P:(c + 1) * P],
                                                   hid[:, g % 2, :].rearrange("p (m c) -> p m c", c=HC)[:, :, c], ident[:])
                    last.then_inc(sem("turned"), 1)

                def second(g):
                    pe.wait_ge(w2_in[g % WBUFS], 16 * (g // WBUFS + 1))
                    pe.wait_ge(sem("turned_out"), g + 1)
                    if g >= 2:
                        pe.wait_ge(sem("result_out"), g - 1)
                    nc.tensor.matmul(ps[:, 4 + g % 2, 0:P], pick[:, g * EG:(g + 1) * EG, :].rearrange("p e l -> p (e l)"), B2[:],
                                     start=True, stop=False)
                    for j in range(EG):
                        for c in range(HC):
                            last = nc.tensor.matmul(ps[j * LANES:(j + 1) * LANES, 4 + g % 2, 0:P],
                                                    hidT[:, g % 2, c, j * LANES:(j + 1) * LANES],
                                                    W2[:, g % WBUFS, j, c, :], start=False, stop=(c == HC - 1))
                    last.then_inc(sem("second_done"), 1)

                def turn_result(g):
                    pe.wait_ge(sem("result_out"), g + 1)
                    if g >= 2:
                        pe.wait_ge(sem("result_kept"), g - 1)
                    nc.tensor.transpose(ps[:, 6 + g % 2, 0:P], res[:, g % 2, :], ident[:]).then_inc(sem("result_turned"), 1)

                pe.wait_ge(sem("bias_in"), 32)
                pe.wait_ge(sem("lanes_ready"), 2)
                for g in range(NEG + 3):
                    if g < NEG:
                        first(g)
                    if 1 <= g <= NEG:
                        turn(g - 1)
                    if 2 <= g <= NEG + 1:
                        second(g - 2)
                    if g >= 3:
                        turn_result(g - 3)
                pe.wait_ge(sem("result_kept"), NEG)
                for a in range(NIMG // 2):
                    last = nc.tensor.transpose(ps[:, 0, a * P:(a + 1) * P], outT[:, 2 * a:2 * a + 2, :].rearrange("p b e -> p (b e)"), ident[:])
                last.then_inc(sem("outputs_turned"), 1)
                pe.wait_ge(sem("outputs_ready"), 1)
                for b in range(NIMG):
                    pe.wait_ge(sel_in[b // 2], 16)
                    for c in range(NC):
                        n = b * NC + c
                        if n >= 4:
                            pe.wait_ge(sem("added"), n - 3)
                        nc.tensor.matmul(ps[:, 4 + n % 4, :], outE[:, b, :], sin[:, b // 2, c * BANK:(c + 1) * BANK],
                                         start=True, stop=True).then_inc(sem("spread"), 1)

            @block.scalar
            def _(act):
                for g in range(NEG):
                    act.wait_ge(sem("first_done"), g + 1)
                    if g >= 2:
                        act.wait_ge(sem("turned"), g - 1)
                    nc.scalar.activation(hid[:, g % 2, :], ps[:, g % 2, :], ACT.Gelu).then_inc(sem("gelu_done"), 1)
                for k in range(2 * NIMG):
                    b, half = k // 2, slice(k % 2 * (TOK // 2), (k % 2 + 1) * (TOK // 2))
                    act.wait_ge(sem("added"), (k + 1) * NC // 2)
                    act.dma_start(out[b].rearrange("c h w -> c (h w)")[:, half], images[b][:, half]).then_inc(sem("out_stored"), 16)
                act.wait_ge(sem("out_stored"), 16 * 2 * NIMG)

            @block.vector
            def _(dve):
                nc.vector.memset(B1[:], 0.0)
                nc.vector.memset(B2[:], 0.0)
                nc.vector.memset(outE[:], 0.0)
                nc.vector.memset(pooled[:], 0.0).then_inc(sem("zeroed"), 1)
                nc.vector.tensor_copy(pick[:], ident[:, 0:E].rearrange("p (e o) -> p e o", o=1).broadcast_to([P, E, LANES])).then_inc(sem("lanes_ready"), 1)
                dve.wait_ge(sem("zeroed"), 1)
                nc.vector.tensor_copy(pooled[:, :, 0:NIMG], poolT[:]).then_inc(sem("lanes_ready"), 1)
                for g in range(NEG + 2):
                    if g < NEG:
                        dve.wait_ge(sem("turned"), g + 1)
                        if g >= 2:
                            dve.wait_ge(sem("second_done"), g - 1)
                        nc.vector.tensor_copy(hidT[:, g % 2], ps[:, 2 + g % 2, :].rearrange("p (c n) -> p c n", n=P)).then_inc(sem("turned_out"), 1)
                    if 1 <= g <= NEG:
                        dve.wait_ge(sem("second_done"), g)
                        if g >= 3:
                            dve.wait_ge(sem("result_turned"), g - 2)
                        nc.vector.tensor_copy(res[:, (g - 1) % 2, :], ps[:, 4 + (g - 1) % 2, 0:P]).then_inc(sem("result_out"), 1)
                    if g >= 2:
                        k = g - 2
                        dve.wait_ge(sem("result_turned"), k + 1)
                        nc.vector.tensor_copy(outT[:, :, k * EG:(k + 1) * EG].rearrange("p b e -> p e b"),
                                              ps[:, 6 + k % 2, 0:P].rearrange("p (e l) -> p e l", l=LANES)[:, :, 0:NIMG]).then_inc(sem("result_kept"), 1)
                dve.wait_ge(sem("outputs_turned"), 1)
                for b in range(NIMG):
                    half = slice(E * (b % 2), E * (b % 2) + E)
                    last = nc.vector.tensor_copy(outE[half, b, :], ps[half, 0, b // 2 * P:(b // 2 + 1) * P])
                last.then_inc(sem("outputs_ready"), 1)
                for b in range(NIMG):
                    if b < NIMG - 1:
                        dve.wait_ge(tok_in[b], 16)
                    for c in range(NC):
                        dve.wait_ge(sem("spread"), b * NC + c + 1)
                        tc = images[b][:, c * BANK:(c + 1) * BANK]
                        nc.vector.tensor_tensor(tc, ps[:, 4 + (b * NC + c) % 4, :], tc, ALU.add).then_inc(sem("added"), 1)


_INS = ['x', 'L0_conv_mask', 'L1_attn_W_qkv', 'L1_attn_b_qkv', 'L1_attn_W_proj', 'L1_attn_b_proj', 'L1_ffn_gate_w',
        'L1_ffn_gate_b', 'L1_ffn_weight1', 'L1_ffn_weight2']
_OUTS = [((4, 128, 64, 64), 'float32')]


def kernel(**inputs):
    import numpy as _np
    import concourse.bacc as _bacc
    from concourse import mybir as _mybir
    from concourse.bass_utils import run_bass_kernel_spmd as _run

    nc = _bacc.Bacc("TRN2", target_bir_lowering=False, num_devices=1)
    arrays, args = {}, []
    for name in _INS:
        a = _np.ascontiguousarray(inputs[name])
        arrays[f"in_{name}_dram"] = a
        args.append(nc.dram_tensor(f"in_{name}_dram", a.shape, _mybir.dt.from_np(a.dtype), kind="ExternalInput").ap())
    for i, (shape, dtype) in enumerate(_OUTS):
        dt = _mybir.dt.from_np(_np.dtype(dtype))
        args.append(nc.dram_tensor(f"out_{i}_dram", shape, dt, kind="ExternalOutput").ap())
    build(nc, *args)
    r = _run(nc, [arrays], core_ids=[0])
    got = tuple(r.results[0][f"out_{i}_dram"] for i in range(len(_OUTS)))
    return got[0]
```
